# Optimizing a Trainium2 kernel written in Bass

```python
import numpy as np
import jax
import jax.numpy as jnp

def _softmax(x, axis=-1):
    return jax.nn.softmax(x, axis=axis)

def _gelu(x):
    return jax.nn.gelu(x, approximate=True)

def _silu(x):
    return jax.nn.silu(x)

def _sigmoid(x):
    return jax.nn.sigmoid(x)

def _layernorm(x, axis=-1, eps=1e-05):
    m = jnp.mean(x, axis=axis, keepdims=True)
    v = jnp.var(x, axis=axis, keepdims=True)
    return (x - m) / jnp.sqrt(v + eps)

def _scatter_add(tgt, idx, src, axis=0):
    return tgt.at[idx].add(src)

def _segment_sum(src, seg, n):
    return jax.ops.segment_sum(src, seg, n)
kernel_name = 'mk_gnn_resnorm_d4_gnn_r32_0ce99b'

def setup_inputs(seed: int=0):
    np.random.seed(seed)
    _w = jnp.asarray

    def _rec_inputs():
        import jax
        import jax.numpy as jnp
        _gk = jax.random.key(seed)
        x = -0.0006008 + 1.001 * jax.random.normal(jax.random.fold_in(_gk, 1), (3125, 128), jnp.float32)
        src = jax.random.randint(jax.random.fold_in(_gk, 2), (50000,), 0, 3125, jnp.int32)
        dst = jax.random.randint(jax.random.fold_in(_gk, 3), (50000,), 0, 3125, jnp.int32)
        _o = jnp.argsort(dst, stable=True)
        src = src[_o]
        dst = dst[_o]
        edge_attr_128 = 2.93046e-05 + 1.00006 * jax.random.normal(jax.random.fold_in(_gk, 12), (50000, 128), jnp.float32)
        edge_attr_4 = -0.000107899 + 1.00008 * jax.random.normal(jax.random.fold_in(_gk, 13), (50000, 4), jnp.float32)
        edge_attr_8 = jax.random.uniform(jax.random.fold_in(_gk, 14), (50000, 8), jnp.float32, 0.0, 1)
        edge_type_32 = jax.random.randint(jax.random.fold_in(_gk, 16), (50000,), 0, 32, jnp.int32)
        node_type_16 = jax.random.randint(jax.random.fold_in(_gk, 17), (3125,), 0, 16, jnp.int32)
        return (x, src, dst, edge_attr_128, edge_attr_4, edge_attr_8, edge_type_32, node_type_16)
    x, src, dst, edge_attr_128, edge_attr_4, edge_attr_8, edge_type_32, node_type_16 = _rec_inputs()

    def _L0_gnn_setup():
        import jax, jax.numpy as jnp
        import numpy as np
        N = 625
        E = 10000
        DIN = 128
        HID = 128
        H = 8
        HS = HID // H
        NT = 16
        RT = 32
        L = 2
        OUT = 128
        SQRT_D = float(np.sqrt(HS))

        def typed_linear(x, t, W):
            y_all = jnp.einsum('nd,tdo->nto', x, W)
            return jnp.take_along_axis(y_all, t[:, None, None], axis=1)[:, 0]

        def edge_softmax(a, dst, n):
            amax = jax.ops.segment_max(a, dst, num_segments=n)
            ex = jnp.exp(a - amax[dst])
            s = jax.ops.segment_sum(ex, dst, num_segments=n)
            return ex / s[dst]

        def gt_layer(x, ntype, etype, src, dst, Wk, Wq, Wv, Wa, Watt, Wmsg, pri, skip, g, b):
            n = x.shape[0]
            k = typed_linear(x, ntype, Wk).reshape(n, H, HS)
            q = typed_linear(x, ntype, Wq).reshape(n, H, HS)
            v = typed_linear(x, ntype, Wv).reshape(n, H, HS)
            kT = jnp.einsum('nhd,htdo->nhto', k, Watt)
            vT = jnp.einsum('nhd,htdo->nhto', v, Wmsg)
            kw = kT[src, :, etype]
            m = vT[src, :, etype]
            a = jnp.einsum('ehd,ehd->eh', kw, q[dst]) * pri[:, etype].T / SQRT_D
            att = edge_softmax(a, dst, n)
            msg = (m * att[:, :, None]).reshape(-1, H * HS)
            hag = jax.ops.segment_sum(msg, dst, num_segments=n)
            h = jax.nn.silu(typed_linear(hag, ntype, Wa))
            alpha = jax.nn.sigmoid(skip[ntype])[:, None]
            h = h * alpha + x * (1.0 - alpha)
            mu = jnp.mean(h, axis=-1, keepdims=True)
            var = jnp.mean((h - mu) ** 2, axis=-1, keepdims=True)
            return (h - mu) * jax.lax.rsqrt(var + 1e-05) * g + b
        key = jax.random.key(seed)
        ks = jax.random.split(key, 16)
        f32 = jnp.float32
        return {'x': jax.random.normal(ks[0], (N, DIN), f32), 'ntype': jax.random.randint(ks[1], (N,), 0, NT), 'etype': jax.random.randint(ks[2], (E,), 0, RT), 'src': jax.random.randint(ks[3], (E,), 0, N), 'dst': jax.random.randint(ks[4], (E,), 0, N), 'Wk': jax.random.normal(ks[5], (L, NT, DIN, HID), f32) / np.sqrt(DIN), 'Wq': jax.random.normal(ks[6], (L, NT, DIN, HID), f32) / np.sqrt(DIN), 'Wv': jax.random.normal(ks[7], (L, NT, DIN, HID), f32) / np.sqrt(DIN), 'Wa': jax.random.normal(ks[8], (L, NT, HID, HID), f32) / np.sqrt(HID), 'Watt': jax.random.normal(ks[9], (L, H, RT, HS, HS), f32) / np.sqrt(HS), 'Wmsg': jax.random.normal(ks[10], (L, H, RT, HS, HS), f32) / np.sqrt(HS), 'pri': jnp.ones((L, H, RT), f32), 'skip': jnp.ones((L, NT), f32), 'ln_g': jnp.ones((L, HID), f32), 'ln_b': jnp.zeros((L, HID), f32), 'ff_w': jax.random.normal(ks[11], (HID, OUT), f32) / np.sqrt(HID), 'ff_b': jnp.zeros((OUT,), f32)}
    _L0_gnn_all = _L0_gnn_setup()
    _L0_gnn_in = {k: v for k, v in _L0_gnn_all.items() if k in ('Wk', 'Wq', 'Wv', 'Wa', 'Watt', 'Wmsg', 'pri', 'skip', 'ln_g', 'ln_b', 'ff_w', 'ff_b')}
    del _L0_gnn_all

    def _L1_gnn_setup():
        import jax, jax.numpy as jnp
        import numpy as np
        N, E = (10000, 20000)
        IN_DIM, EDGE_DIM, OUT_DIM = (128, 128, 128)
        key = jax.random.key(seed)
        ks = jax.random.split(key, 9)
        s = 0.02
        return {'x': jax.random.normal(ks[0], (N, IN_DIM), dtype=jnp.float32), 'edge_index': jax.random.randint(ks[1], (2, E), 0, N, dtype=jnp.int64), 'edge_attr': jax.random.normal(ks[2], (E, EDGE_DIM), dtype=jnp.float32), 'We': jax.random.normal(ks[3], (EDGE_DIM, IN_DIM), dtype=jnp.float32) * s, 'be': jnp.zeros((IN_DIM,), dtype=jnp.float32), 'W1': jax.random.normal(ks[4], (2 * IN_DIM, OUT_DIM), dtype=jnp.float32) * s, 'b1': jnp.zeros((OUT_DIM,), dtype=jnp.float32), 'W2': jax.random.normal(ks[5], (OUT_DIM, OUT_DIM), dtype=jnp.float32) * s, 'b2': jnp.zeros((OUT_DIM,), dtype=jnp.float32)}
    _L1_gnn_all = _L1_gnn_setup()
    _L1_gnn_in = {k: v for k, v in _L1_gnn_all.items() if k in ('We', 'be', 'W1', 'b1', 'W2', 'b2')}
    del _L1_gnn_all

    def _L2_gnn_setup():
        import jax, jax.numpy as jnp
        import numpy as np
        MUL = 32
        N_NODES = 50000
        N_EDGES = 25000
        R3 = np.sqrt(3.0).astype(np.float32)
        key = jax.random.key(seed)
        ks = jax.random.split(key, 12)
        inp = {}
        inp['node_feats'] = jax.random.normal(ks[0], (N_NODES, 4 * MUL), dtype=jnp.float32)
        inp['edge_attrs'] = jax.random.normal(ks[1], (N_EDGES, 4), dtype=jnp.float32)
        inp['edge_feats'] = jax.random.uniform(ks[2], (N_EDGES, 8), dtype=jnp.float32)
        inp['edge_index'] = jax.random.randint(ks[3], (2, N_EDGES), 0, N_NODES)
        inp['W_up_s'] = jax.random.normal(ks[4], (MUL, MUL), dtype=jnp.float32)
        inp['W_up_v'] = jax.random.normal(ks[5], (MUL, MUL), dtype=jnp.float32)
        inp['A1'] = jax.random.normal(ks[6], (8, 64), dtype=jnp.float32) / np.sqrt(8.0)
        inp['b1'] = jnp.zeros((64,), dtype=jnp.float32)
        inp['A2'] = jax.random.normal(ks[7], (64, 64), dtype=jnp.float32) / np.sqrt(64.0)
        inp['b2'] = jnp.zeros((64,), dtype=jnp.float32)
        inp['A3'] = jax.random.normal(ks[8], (64, 4 * MUL), dtype=jnp.float32) * (10.0 * np.sqrt(6.0 / (64 + 4 * MUL)))
        inp['W_out_s'] = jax.random.normal(ks[9], (2 * MUL, MUL), dtype=jnp.float32)
        inp['W_out_v'] = jax.random.normal(ks[10], (2 * MUL, MUL), dtype=jnp.float32)
        return inp
    _L2_gnn_all = _L2_gnn_setup()
    _L2_gnn_in = {k: v for k, v in _L2_gnn_all.items() if k in ('W_up_s', 'W_up_v', 'A1', 'b1', 'A2', 'b2', 'A3', 'W_out_s', 'W_out_v')}
    del _L2_gnn_all

    def _L3_gnn_setup():
        import jax, jax.numpy as jnp
        import numpy as np
        N = 3125
        E = 50000
        D_IN = 128
        D_HID = 128
        D_OUT = 128
        EPS = 1e-05

        def _gcn_conv(x, W, b, src, dst, edge_norm, num_nodes):
            h = x @ W
            msg = h[src] * edge_norm[:, None]
            agg = jax.ops.segment_sum(msg, dst, num_segments=num_nodes)
            return agg + b

        def _batch_norm(x, gamma, beta):
            m = jnp.mean(x, axis=0)
            v = jnp.mean(jnp.square(x - m), axis=0)
            return (x - m) * jax.lax.rsqrt(v + EPS) * gamma + beta
        key = jax.random.key(seed)
        ks = jax.random.split(key, 8)
        x = jax.random.normal(ks[0], (N, D_IN), dtype=jnp.float32)
        edge_index = jax.random.randint(ks[1], (2, E), 0, N, dtype=jnp.int64)
        W1 = jax.random.normal(ks[2], (D_IN, D_HID), dtype=jnp.float32) / np.sqrt(D_IN)
        b1 = jnp.zeros((D_HID,), dtype=jnp.float32)
        g1 = jnp.ones((D_HID,), dtype=jnp.float32)
        bt1 = jnp.zeros((D_HID,), dtype=jnp.float32)
        W2 = jax.random.normal(ks[3], (D_HID, D_OUT), dtype=jnp.float32) / np.sqrt(D_HID)
        b2 = jnp.zeros((D_OUT,), dtype=jnp.float32)
        g2 = jnp.ones((D_OUT,), dtype=jnp.float32)
        bt2 = jnp.zeros((D_OUT,), dtype=jnp.float32)
        return {'x': x, 'edge_index': edge_index, 'W1': W1, 'b1': b1, 'g1': g1, 'bt1': bt1, 'W2': W2, 'b2': b2, 'g2': g2, 'bt2': bt2}
    _L3_gnn_all = _L3_gnn_setup()
    _L3_gnn_in = {k: v for k, v in _L3_gnn_all.items() if k in ('W1', 'b1', 'g1', 'bt1', 'W2', 'b2', 'g2', 'bt2')}
    del _L3_gnn_all
    return {'x': x, 'src': src, 'dst': dst, 'edge_attr_128': edge_attr_128, 'edge_attr_4': edge_attr_4, 'edge_attr_8': edge_attr_8, 'edge_type_32': edge_type_32, 'node_type_16': node_type_16, 'L0_gnn_Wk': _L0_gnn_in['Wk'], 'L0_gnn_Wq': _L0_gnn_in['Wq'], 'L0_gnn_Wv': _L0_gnn_in['Wv'], 'L0_gnn_Wa': _L0_gnn_in['Wa'], 'L0_gnn_Watt': _L0_gnn_in['Watt'], 'L0_gnn_Wmsg': _L0_gnn_in['Wmsg'], 'L0_gnn_pri': _L0_gnn_in['pri'], 'L0_gnn_skip': _L0_gnn_in['skip'], 'L0_gnn_ln_g': _L0_gnn_in['ln_g'], 'L0_gnn_ln_b': _L0_gnn_in['ln_b'], 'L0_gnn_ff_w': _L0_gnn_in['ff_w'], 'L0_gnn_ff_b': _L0_gnn_in['ff_b'], 'L1_gnn_We': _L1_gnn_in['We'], 'L1_gnn_be': _L1_gnn_in['be'], 'L1_gnn_W1': _L1_gnn_in['W1'], 'L1_gnn_b1': _L1_gnn_in['b1'], 'L1_gnn_W2': _L1_gnn_in['W2'], 'L1_gnn_b2': _L1_gnn_in['b2'], 'L2_gnn_W_up_s': _L2_gnn_in['W_up_s'], 'L2_gnn_W_up_v': _L2_gnn_in['W_up_v'], 'L2_gnn_A1': _L2_gnn_in['A1'], 'L2_gnn_b1': _L2_gnn_in['b1'], 'L2_gnn_A2': _L2_gnn_in['A2'], 'L2_gnn_b2': _L2_gnn_in['b2'], 'L2_gnn_A3': _L2_gnn_in['A3'], 'L2_gnn_W_out_s': _L2_gnn_in['W_out_s'], 'L2_gnn_W_out_v': _L2_gnn_in['W_out_v'], 'L3_gnn_W1': _L3_gnn_in['W1'], 'L3_gnn_b1': _L3_gnn_in['b1'], 'L3_gnn_g1': _L3_gnn_in['g1'], 'L3_gnn_bt1': _L3_gnn_in['bt1'], 'L3_gnn_W2': _L3_gnn_in['W2'], 'L3_gnn_b2': _L3_gnn_in['b2'], 'L3_gnn_g2': _L3_gnn_in['g2'], 'L3_gnn_bt2': _L3_gnn_in['bt2']}

def reference(x, src, dst, edge_attr_128, edge_attr_4, edge_attr_8, edge_type_32, node_type_16, L0_gnn_Wk, L0_gnn_Wq, L0_gnn_Wv, L0_gnn_Wa, L0_gnn_Watt, L0_gnn_Wmsg, L0_gnn_pri, L0_gnn_skip, L0_gnn_ln_g, L0_gnn_ln_b, L0_gnn_ff_w, L0_gnn_ff_b, L1_gnn_We, L1_gnn_be, L1_gnn_W1, L1_gnn_b1, L1_gnn_W2, L1_gnn_b2, L2_gnn_W_up_s, L2_gnn_W_up_v, L2_gnn_A1, L2_gnn_b1, L2_gnn_A2, L2_gnn_b2, L2_gnn_A3, L2_gnn_W_out_s, L2_gnn_W_out_v, L3_gnn_W1, L3_gnn_b1, L3_gnn_g1, L3_gnn_bt1, L3_gnn_W2, L3_gnn_b2, L3_gnn_g2, L3_gnn_bt2):
    import jax
    import jax.numpy as jnp

    def _L0_gnn_ref(x, ntype, etype, src, dst, Wk, Wq, Wv, Wa, Watt, Wmsg, pri, skip, ln_g, ln_b, ff_w, ff_b):
        import jax, jax.numpy as jnp
        import numpy as np
        N = 625
        E = 10000
        DIN = 128
        HID = 128
        H = 8
        HS = HID // H
        NT = 16
        RT = 32
        L = 2
        OUT = 128
        SQRT_D = float(np.sqrt(HS))

        def typed_linear(x, t, W):
            y_all = jnp.einsum('nd,tdo->nto', x, W)
            return jnp.take_along_axis(y_all, t[:, None, None], axis=1)[:, 0]

        def edge_softmax(a, dst, n):
            amax = jax.ops.segment_max(a, dst, num_segments=n)
            ex = jnp.exp(a - amax[dst])
            s = jax.ops.segment_sum(ex, dst, num_segments=n)
            return ex / s[dst]

        def gt_layer(x, ntype, etype, src, dst, Wk, Wq, Wv, Wa, Watt, Wmsg, pri, skip, g, b):
            n = x.shape[0]
            k = typed_linear(x, ntype, Wk).reshape(n, H, HS)
            q = typed_linear(x, ntype, Wq).reshape(n, H, HS)
            v = typed_linear(x, ntype, Wv).reshape(n, H, HS)
            kT = jnp.einsum('nhd,htdo->nhto', k, Watt)
            vT = jnp.einsum('nhd,htdo->nhto', v, Wmsg)
            kw = kT[src, :, etype]
            m = vT[src, :, etype]
            a = jnp.einsum('ehd,ehd->eh', kw, q[dst]) * pri[:, etype].T / SQRT_D
            att = edge_softmax(a, dst, n)
            msg = (m * att[:, :, None]).reshape(-1, H * HS)
            hag = jax.ops.segment_sum(msg, dst, num_segments=n)
            h = jax.nn.silu(typed_linear(hag, ntype, Wa))
            alpha = jax.nn.sigmoid(skip[ntype])[:, None]
            h = h * alpha + x * (1.0 - alpha)
            mu = jnp.mean(h, axis=-1, keepdims=True)
            var = jnp.mean((h - mu) ** 2, axis=-1, keepdims=True)
            return (h - mu) * jax.lax.rsqrt(var + 1e-05) * g + b
        h = x
        for l in range(L):
            h = gt_layer(h, ntype, etype, src, dst, Wk[l], Wq[l], Wv[l], Wa[l], Watt[l], Wmsg[l], pri[l], skip[l], ln_g[l], ln_b[l])
        return h @ ff_w + ff_b

    def _L1_gnn_ref(x, edge_index, edge_attr, We, be, W1, b1, W2, b2):
        import jax, jax.numpy as jnp
        import numpy as np
        N, E = (10000, 20000)
        IN_DIM, EDGE_DIM, OUT_DIM = (128, 128, 128)
        src, dst = (edge_index[0], edge_index[1])
        num_nodes = x.shape[0]
        edge_emb = edge_attr @ We + be
        edge_agg = jax.ops.segment_sum(edge_emb, dst, num_segments=num_nodes)
        x_comb = jnp.concatenate([x, edge_agg], axis=-1)
        neigh = jax.ops.segment_sum(x_comb[src], dst, num_segments=num_nodes)
        h = x_comb + neigh
        return jax.nn.relu(h @ W1 + b1) @ W2 + b2

    def _L2_gnn_ref(node_feats, edge_attrs, edge_feats, W_up_s, W_up_v, A1, b1, A2, b2, A3, W_out_s, W_out_v, edge_index):
        import jax, jax.numpy as jnp
        import numpy as np
        MUL = 32
        N_NODES = 50000
        N_EDGES = 25000
        R3 = np.sqrt(3.0).astype(np.float32)
        num_nodes = node_feats.shape[0]
        sender, receiver = (edge_index[0], edge_index[1])
        s = node_feats[:, :MUL]
        v = node_feats[:, MUL:].reshape(num_nodes, MUL, 3)
        inv = 1.0 / np.sqrt(MUL).astype(np.float32)
        s = s @ W_up_s * inv
        v = jnp.einsum('nui,uw->nwi', v, W_up_v) * inv
        h = jax.nn.silu(edge_feats @ A1 + b1)
        h = jax.nn.silu(h @ A2 + b2)
        tpw = h @ A3
        w0, w1, w2, w3 = jnp.split(tpw, 4, axis=1)
        ss = s[sender]
        vs = v[sender]
        y_s = edge_attrs[:, :1]
        y_v = edge_attrs[:, 1:4]
        out_s0 = ss * y_s * w0
        out_s3 = jnp.einsum('eui,ei->eu', vs, y_v) / R3 * w3
        out_v1 = ss[:, :, None] * y_v[:, None, :] * w1[:, :, None]
        out_v2 = vs * y_s[:, :, None] * w2[:, :, None]
        E = ss.shape[0]
        mji = jnp.concatenate([out_s0, out_s3, out_v1.reshape(E, 3 * MUL), out_v2.reshape(E, 3 * MUL)], axis=1)
        message = jax.ops.segment_sum(mji, receiver, num_segments=num_nodes) / 10.0
        ms = message[:, :2 * MUL]
        mv = message[:, 2 * MUL:].reshape(num_nodes, 2 * MUL, 3)
        inv2 = 1.0 / np.sqrt(2 * MUL).astype(np.float32)
        out_s = ms @ W_out_s * inv2
        out_v = jnp.einsum('nui,uw->nwi', mv, W_out_v) * inv2
        return jnp.concatenate([out_s, out_v.reshape(num_nodes, 3 * MUL)], axis=1)

    def _L3_gnn_ref(x, edge_index, W1, b1, g1, bt1, W2, b2, g2, bt2):
        import jax, jax.numpy as jnp
        import numpy as np
        N = 3125
        E = 50000
        D_IN = 128
        D_HID = 128
        D_OUT = 128
        EPS = 1e-05

        def _gcn_conv(x, W, b, src, dst, edge_norm, num_nodes):
            h = x @ W
            msg = h[src] * edge_norm[:, None]
            agg = jax.ops.segment_sum(msg, dst, num_segments=num_nodes)
            return agg + b

        def _batch_norm(x, gamma, beta):
            m = jnp.mean(x, axis=0)
            v = jnp.mean(jnp.square(x - m), axis=0)
            return (x - m) * jax.lax.rsqrt(v + EPS) * gamma + beta
        num_nodes = x.shape[0]
        loops = jnp.arange(num_nodes, dtype=edge_index.dtype)
        src = jnp.concatenate([edge_index[0], loops])
        dst = jnp.concatenate([edge_index[1], loops])
        deg = jax.ops.segment_sum(jnp.ones_like(dst, dtype=x.dtype), dst, num_segments=num_nodes)
        inv_sqrt_deg = jax.lax.rsqrt(deg)
        edge_norm = inv_sqrt_deg[src] * inv_sqrt_deg[dst]
        h = _gcn_conv(x, W1, b1, src, dst, edge_norm, num_nodes)
        h = _batch_norm(h, g1, bt1)
        h = jax.nn.relu(h)
        h = _gcn_conv(h, W2, b2, src, dst, edge_norm, num_nodes)
        h = _batch_norm(h, g2, bt2)
        return h
    edge_index = jnp.stack([src, dst])
    x = _layernorm(x + _L0_gnn_ref(x, node_type_16, edge_type_32, src, dst, L0_gnn_Wk, L0_gnn_Wq, L0_gnn_Wv, L0_gnn_Wa, L0_gnn_Watt, L0_gnn_Wmsg, L0_gnn_pri, L0_gnn_skip, L0_gnn_ln_g, L0_gnn_ln_b, L0_gnn_ff_w, L0_gnn_ff_b), axis=-1)
    x = _layernorm(x + _L1_gnn_ref(x, edge_index, edge_attr_128, L1_gnn_We, L1_gnn_be, L1_gnn_W1, L1_gnn_b1, L1_gnn_W2, L1_gnn_b2), axis=-1)
    x = _layernorm(x + _L2_gnn_ref(x, edge_attr_4, edge_attr_8, L2_gnn_W_up_s, L2_gnn_W_up_v, L2_gnn_A1, L2_gnn_b1, L2_gnn_A2, L2_gnn_b2, L2_gnn_A3, L2_gnn_W_out_s, L2_gnn_W_out_v, edge_index), axis=-1)
    x = _layernorm(x + _L3_gnn_ref(x, edge_index, L3_gnn_W1, L3_gnn_b1, L3_gnn_g1, L3_gnn_bt1, L3_gnn_W2, L3_gnn_b2, L3_gnn_g2, L3_gnn_bt2), axis=-1)
    return x

_drawn_inputs = setup_inputs


def setup_inputs(seed=0):
    import zlib

    import numpy as np

    out = dict(_drawn_inputs(seed))
    spreads = {'L0_gnn_pri': (1.0, 0.2),
     'L0_gnn_skip': (1.0, 0.2),
     'L0_gnn_ln_g': (1.0, 0.2),
     'L0_gnn_ln_b': (0.0, 0.1),
     'L0_gnn_ff_b': (0.0, 0.1),
     'L1_gnn_be': (0.0, 0.1),
     'L1_gnn_b1': (0.0, 0.652),
     'L1_gnn_b2': (0.0, 0.1),
     'L2_gnn_b1': (0.0, 0.1),
     'L2_gnn_b2': (0.0, 0.1),
     'L3_gnn_b1': (0.0, 0.8),
     'L3_gnn_g1': (1.0, 0.2),
     'L3_gnn_bt1': (0.0, 0.1),
     'L3_gnn_b2': (0.0, 0.8),
     'L3_gnn_g2': (1.0, 0.2),
     'L3_gnn_bt2': (0.0, 0.1)}
    factors = {}
    for name, (base, spread) in spreads.items():
        noise = np.random.default_rng([zlib.crc32(name.encode()), seed]).standard_normal(out[name].shape)
        drawn = base * np.exp(spread * noise) if base else spread * noise
        out[name] = jnp.asarray(drawn.astype(out[name].dtype))
    for name, factor in factors.items():
        out[name] = (out[name] * factor).astype(out[name].dtype)
    return out
```

```python
from contextlib import ExitStack

import concourse.bass as bass
import concourse.mybir as mybir

F32, I32, BF16, U8 = mybir.dt.float32, mybir.dt.int32, mybir.dt.bfloat16, mybir.dt.uint8
ALU = mybir.AluOpType
ACT = mybir.ActivationFunctionType
AX = mybir.AxisListType

P = 128
N, E = 3125, 50000
NT = -(-N // P)
NP = NT * P
W = 512
J = W // P
G = 98
EP = G * W
CH = 400
NC = NP // CH
TILES = EP // P
NTYPES, RELS, HEADS, HS, LAYERS = 16, 32, 8, 16, 2
BIG = 1.0e30
FAR = 1.0e6


class Stage:

    def __init__(self, nc, tag):
        self.nc, self.tag = nc, tag
        self.stack = ExitStack()
        self.sems = []

    def sb(self, name, shape, dt=F32):
        return self.stack.enter_context(self.nc.sbuf_tensor(f"{self.tag}_{name}", shape, dt))

    def ps(self, name, shape=(P, W)):
        return self.stack.enter_context(self.nc.psum_tensor(f"{self.tag}_{name}", list(shape), F32))

    def sem(self, name):
        s = self.nc.alloc_semaphore(f"{self.tag}_{name}")
        self.sems.append(s)
        return s

    def block(self):
        return self.stack.enter_context(self.nc.Block())

    def __enter__(self):
        return self

    def __exit__(self, *exc):
        self.stack.close()
        if exc[0] is None:
            self.nc.clear_and_free_semaphores(self.sems)
            self.nc.all_engine_barrier()
        return False


def pairs(eng, step):
    for g in range(4):
        step(g // 2, g % 2)
    with eng.Fori(2, G // 2) as it:
        step(it, 0)
        step(it, 1)


def first(it, u=0, back=1):
    return isinstance(it, int) and 2 * it + u < back


def linked(eng, sem):
    done = [0]

    def link(ins):
        done[0] += 1
        ins.then_inc(sem, 1)
        eng.wait_ge(sem, done[0])
    return link


def constants(nc, K):
    with Stage(nc, "cst") as s:
        made = s.sem("made")
        hid = s.sb("hid", [P, P], I32)
        pid = s.sb("pid", [P, 1], I32)
        hidf = s.sb("hidf", [P, P])
        pidf = s.sb("pidf", [P, 1])
        block = s.block()

        @block.gpsimd
        def _(pool):
            link = linked(pool, made)
            link(nc.gpsimd.memset(K.ident[:, :], 0.0))
            link(nc.gpsimd.affine_select(out=K.ident[:, :], in_=K.ident[:, :], compare_op=ALU.not_equal,
                                         fill=1.0, base=0, pattern=[[-1, P]], channel_multiplier=1))
            link(nc.gpsimd.memset(K.mean[:, :], 1.0 / P))
            link(nc.gpsimd.memset(K.eps[:, :], 1e-5))
            link(nc.gpsimd.memset(K.ones[:, :], 1.0))
            link(nc.gpsimd.iota(hid[:, :], pattern=[[1, P]], base=0, channel_multiplier=0))
            link(nc.gpsimd.iota(pid[:, :], pattern=[[0, 1]], base=0, channel_multiplier=1))

        @block.vector
        def _(dve):
            dve.wait_ge(made, 7)
            done = [7]

            def link(ins):
                done[0] += 1
                ins.then_inc(made, 1)
                dve.wait_ge(made, done[0])
            link(nc.vector.tensor_scalar(K.negid[:, :], K.ident[:, :], -1.0, None, ALU.mult))
            link(nc.vector.tensor_scalar(hid[:, :], hid[:, :], 4, None, ALU.arith_shift_right))
            link(nc.vector.tensor_copy(hidf[:, :], hid[:, :]))
            link(nc.vector.tensor_copy(K.pid[:, :], pid[:, :]))
            link(nc.vector.tensor_scalar(pid[:, :], pid[:, :], 4, None, ALU.arith_shift_right))
            link(nc.vector.tensor_copy(pidf[:, :], pid[:, :]))
            link(nc.vector.tensor_scalar(K.headsum[:, :], hidf[:, :], pidf[:, 0:1], None, ALU.is_equal))


def graph_index(nc, K, D):
    C = EP // P
    with Stage(nc, "idx") as s:
        loaded, made, coarse_in, fetched, back = (s.sem(x) for x in ("loaded", "made", "coarse", "fetched", "back"))
        fine_in = s.sem("fine_in")
        dst = s.sb("dst", [P, C], I32)
        prev = s.sb("prev", [P, C], I32)
        src = s.sb("src", [P, C], I32)
        ety = s.sb("ety", [P, C], I32)
        same = s.sb("same", [P, C])
        same8 = s.sb("same8", [P, C], U8)
        bias = s.sb("bias", [P, C], BF16)
        row = s.sb("row", [P, C], I32)
        coarse_i = s.sb("coarse_i", [P, TILES], I32)
        node_i = s.sb("node_i", [P, NT], I32)
        node = s.sb("node", [P, NT])
        cmp = s.sb("cmp", [P, NT, TILES], BF16)
        tile_f = s.sb("tile_f", [P, 2, NT])
        tile_i = s.sb("tile_i", [P, 2, NT], I32)
        fine = s.sb("fine", [P, 2, NT, P], I32)
        within = s.sb("within", [P, 2, NT])
        count = s.sb("count", [P, 2, NT])
        start = s.sb("start", [P, NT])
        tmp = s.sb("tmp", [P, NT])
        block = s.block()

        @block.sync
        def _(sp):
            sp.dma_start(dst[:, :], D.dst.rearrange("(p c) -> p c", p=P)).then_inc(loaded, 16)
            sp.dma_start(prev[:, :], D.dst_before.rearrange("(p c) -> p c", p=P)).then_inc(loaded, 16)
            sp.dma_start(src[:, :], D.src_flat.rearrange("(p c) -> p c", p=P)).then_inc(loaded, 16)
            sp.dma_start(ety[:, :], D.etype_flat.rearrange("(p c) -> p c", p=P)).then_inc(loaded, 16)
            with nc.allow_non_contiguous_dma(reason="one number of each tile"):
                sp.dma_start(D.coarse.rearrange("(t o) -> t o", o=1),
                             D.dst.rearrange("(t c) -> t c", c=P)[:, P - 1:P]).then_inc(coarse_in, 16)
            sp.wait_ge(coarse_in, 16)
            sp.dma_start(coarse_i[:, :], D.coarse.partition_broadcast(P)).then_inc(coarse_in, 16)
            sp.wait_ge(made, 6)
            sp.dma_start(D.same.rearrange("(p c) -> p c", p=P), same8[:, :]).then_inc(back, 16)
            sp.dma_start(D.start_bias.rearrange("(p c) -> p c", p=P), bias[:, :]).then_inc(back, 16)
            sp.dma_start(D.kvrow.rearrange("(p c) -> p c", p=P), row[:, :]).then_inc(back, 16)
            sp.wait_ge(back, 48)
            sp.dma_start(K.same[:, :], D.same.partition_broadcast(P)).then_inc(back, 16)
            sp.wait_ge(made, 24)
            with nc.allow_non_contiguous_dma(reason="one number of each node"):
                sp.dma_start(D.degree.rearrange("(t p) -> p t", p=P), K.degree[:, :]).then_inc(back, 16)
            sp.wait_ge(back, 80)

        @block.gpsimd
        def _(pool):
            nc.gpsimd.iota(node_i[:, :], pattern=[[P, NT]], base=0, channel_multiplier=1).then_inc(fetched, 1)
            pool.wait_ge(made, 12)
            for k in range(2):
                for t in range(NT):
                    nc.gpsimd.indirect_dma_start(
                        fine[:, k, t, :], None, D.dst.rearrange("(t c) -> t c", c=P),
                        bass.IndirectOffsetOnAxis(ap=tile_i[:, k, t:t + 1], axis=0)).then_inc(fine_in, 16)

        @block.vector
        def _(dve):
            link = linked(dve, made)
            dve.wait_ge(loaded, 64)
            link(nc.vector.tensor_tensor(same[:, :], dst[:, :], prev[:, :], ALU.is_equal))
            link(nc.vector.tensor_copy(same8[:, :], same[:, :]))
            link(nc.vector.tensor_scalar(bias[:, :], same[:, :], -1.0, BIG, ALU.add, ALU.mult))
            link(nc.vector.tensor_scalar(row[:, :], src[:, :], RELS, None, ALU.mult))
            link(nc.vector.tensor_tensor(row[:, :], row[:, :], ety[:, :], ALU.add))
            dve.wait_ge(fetched, 1)
            link(nc.vector.tensor_copy(node[:, :], node_i[:, :]))
            dve.wait_ge(coarse_in, 32)
            for k, op in enumerate((ALU.is_le, ALU.is_lt)):
                link(nc.vector.tensor_tensor(cmp[:, :, :],
                                             coarse_i[:, :].unsqueeze(1).broadcast_to([P, NT, TILES]),
                                             node[:, :].unsqueeze(2).broadcast_to([P, NT, TILES]), op))
                link(nc.vector.tensor_reduce(tile_f[:, k, :], cmp[:, :, :], AX.X, ALU.add))
            link(nc.vector.tensor_scalar(tile_f[:, :, :], tile_f[:, :, :], TILES - 1.0, None, ALU.min))
            link(nc.vector.tensor_copy(tile_i[:, :, :], tile_f[:, :, :]))
            dve.wait_ge(fine_in, 2 * NT * 16)
            for k, op in enumerate((ALU.is_le, ALU.is_lt)):
                link(nc.vector.tensor_tensor(cmp[:, :, 0:P], fine[:, k, :, :],
                                             node[:, :].unsqueeze(2).broadcast_to([P, NT, P]), op))
                link(nc.vector.tensor_reduce(within[:, k, :], cmp[:, :, 0:P], AX.X, ALU.add))
            link(nc.vector.scalar_tensor_tensor(count[:, :, :], tile_f[:, :, :], float(P), within[:, :, :], ALU.mult, ALU.add))
            link(nc.vector.tensor_tensor(K.degree[:, :], count[:, 0, :], count[:, 1, :], ALU.subtract))
            link(nc.vector.tensor_scalar(K.has[:, :], K.degree[:, :], 0.0, None, ALU.is_gt))
            link(nc.vector.tensor_scalar(tmp[:, :], count[:, 0, :], -1.0, 0.0, ALU.add, ALU.max))
            link(nc.vector.tensor_copy(K.end[:, :], tmp[:, :]))
            link(nc.vector.scalar_tensor_tensor(start[:, :], K.has[:, :], -FAR, count[:, 1, :], ALU.mult, ALU.add))
            link(nc.vector.tensor_scalar(start[:, :], start[:, :], FAR, None, ALU.add))
            link(nc.vector.tensor_copy(K.start[:, :], start[:, :]))


def clear_edge_rows(nc, D):
    per = EP // P // 8
    with Stage(nc, "clr") as s:
        zeroed, stored = s.sem("zeroed"), s.sem("stored")
        zero = s.sb("zero", [P, per * P])
        block = s.block()

        @block.vector
        def _(dve):
            nc.vector.memset(zero[:, :], 0.0).then_inc(zeroed, 1)

        @block.sync
        def _(sp):
            sp.wait_ge(zeroed, 1)
            q = D.query_rows.rearrange("(p c) d -> p (c d)", p=P)
            for k in range(8):
                sp.dma_start(q[:, k * per * P:(k + 1) * per * P], zero[:, :]).then_inc(stored, 16)
            sp.wait_ge(stored, 8 * 16)


def to_rows(nc, K, tag, x, rows=None, dram=None, width=P, col=0, start=None, limit=None):
    with Stage(nc, tag) as s:
        turned, copied, stored = s.sem("turned"), s.sem("copied"), s.sem("stored")
        rows = rows or s.sb("rows", [P, NT, P])
        bank = [s.ps(f"bank{i}") for i in range(2)]
        n = -(-NT // J)
        block = s.block()

        @block.tensor
        def _(pe):
            for k in range(n):
                if k >= 2:
                    pe.wait_ge(copied, k - 1)
                for t in range(k * J, min(NT, k * J + J)):
                    last = nc.tensor.transpose(bank[k % 2][:, (t - k * J) * P:(t - k * J + 1) * P],
                                               x[:, t * P:(t + 1) * P], K.ident[:, :])
                last.then_inc(turned, 1)

        @block.scalar
        def _(act):
            for k in range(n):
                m = min(NT, k * J + J) - k * J
                act.wait_ge(turned, k + 1)
                nc.scalar.activation(rows[:, k * J:k * J + m, :].rearrange("p t d -> p (t d)"),
                                     bank[k % 2][:, 0:m * P], ACT.Copy).then_inc(copied, 1)

        if dram is not None and start is None:
            @block.sync
            def _(sp):
                view = dram.rearrange("(t p) d -> p t d", p=P)
                for k in range(n):
                    m = min(NT, k * J + J) - k * J
                    sp.wait_ge(copied, k + 1)
                    sp.dma_start(view[:, k * J:k * J + m, col:col + P], rows[:, k * J:k * J + m, :]).then_inc(stored, 16)
                sp.wait_ge(stored, 16 * n)

        if start is not None:
            @block.gpsimd
            def _(pool):
                for t in range(NT):
                    if t % J == 0:
                        pool.wait_ge(copied, t // J + 1)
                    nc.gpsimd.indirect_dma_start(dram, bass.IndirectOffsetOnAxis(ap=start[:, t:t + 1], axis=0),
                                                 rows[:, t, :], None, bounds_check=limit,
                                                 oob_is_err=False).then_inc(stored, 16)
                pool.wait_ge(stored, 16 * NT)


def ends(nc, K, D, tag, out, per_head=False):
    src, width = (D.att_sums, P + HEADS) if per_head else (D.sums, P)
    with Stage(nc, tag) as s:
        fetched, ready, turned, copied, made = (s.sem(x) for x in ("fetched", "ready", "turned", "copied", "made"))
        rows = s.sb("rows", [P, NT, width])
        scaled = s.sb("scaled", [P, NT, P])
        inv = s.sb("inv", [P, NT, HEADS])
        bank = [s.ps(f"bank{i}") for i in range(2)]
        n = -(-NT // J)
        block = s.block()

        @block.gpsimd
        def _(pool):
            for t in range(NT):
                nc.gpsimd.indirect_dma_start(rows[:, t, :], None, src,
                                             bass.IndirectOffsetOnAxis(ap=K.end[:, t:t + 1], axis=0)).then_inc(fetched, 16)

        @block.vector
        def _(dve):
            link = linked(dve, made)
            dve.wait_ge(fetched, 16 * NT)
            if per_head:
                link(nc.vector.reciprocal(inv[:, :, :], rows[:, :, P:P + HEADS]))
                link(nc.vector.tensor_tensor(inv[:, :, :], inv[:, :, :],
                                             K.has[:, :].unsqueeze(2).broadcast_to([P, NT, HEADS]), ALU.mult))
                nc.vector.tensor_tensor(scaled[:, :, :].rearrange("p t (h c) -> p t h c", c=HS),
                                        rows[:, :, 0:P].rearrange("p t (h c) -> p t h c", c=HS),
                                        inv[:, :, :].unsqueeze(3).broadcast_to([P, NT, HEADS, HS]),
                                        ALU.mult).then_inc(ready, 1)
            else:
                nc.vector.tensor_tensor(scaled[:, :, :], rows[:, :, :],
                                        K.has[:, :].unsqueeze(2).broadcast_to([P, NT, P]), ALU.mult).then_inc(ready, 1)

        @block.tensor
        def _(pe):
            pe.wait_ge(ready, 1)
            for k in range(n):
                if k >= 2:
                    pe.wait_ge(copied, k - 1)
                for t in range(k * J, min(NT, k * J + J)):
                    last = nc.tensor.transpose(bank[k % 2][:, (t - k * J) * P:(t - k * J + 1) * P],
                                               scaled[:, t, :], K.ident[:, :])
                last.then_inc(turned, 1)

        @block.scalar
        def _(act):
            for k in range(n):
                m = min(NT, k * J + J) - k * J
                act.wait_ge(turned, k + 1)
                nc.scalar.activation(out[:, k * W:k * W + m * P], bank[k % 2][:, 0:m * P], ACT.Copy).then_inc(copied, 1)


def linear(nc, K, tag, out, terms, bias=None, func=ACT.Identity, row_term=None, prepare=None):
    with Stage(nc, tag) as s:
        loaded, summed, done = s.sem("loaded"), s.sem("summed"), s.sem("done")
        w = [s.sb(f"w{i}", [P, P]) for i in range(len(terms))]
        b = s.sb("b", [P, 1])
        rw = s.sb("rw", [1, P])
        rx = s.sb("rx", [1, NP])
        acc = [s.ps(f"acc{i}") for i in range(2)]
        loads = 16 * (len(terms) + (bias is not None) + 2 * (row_term is not None))
        block = s.block()

        @block.sync
        def _(sp):
            for i, (wd, _) in enumerate(terms):
                sp.dma_start(w[i][:, :], wd[:, :]).then_inc(loaded, 16)
            if bias is not None:
                sp.dma_start(b[:, :], bias.rearrange("(p o) -> p o", o=1)).then_inc(loaded, 16)
            if row_term is not None:
                sp.dma_start(rw[:, :], row_term[0].rearrange("(o p) -> o p", o=1)).then_inc(loaded, 16)
                sp.dma_start(rx[:, :], row_term[1].rearrange("(o p) -> o p", o=1)).then_inc(loaded, 16)

        @block.tensor
        def _(pe):
            pe.wait_ge(loaded, loads)
            for c in range(NC):
                if c >= 2:
                    pe.wait_ge(done, c - 1)
                for i, (_, x) in enumerate(terms):
                    last = nc.tensor.matmul(acc[c % 2][:, 0:CH], w[i][:, :], x[:, c * CH:(c + 1) * CH], start=i == 0,
                                            stop=i == len(terms) - 1 and row_term is None)
                if row_term is not None:
                    last = nc.tensor.matmul(acc[c % 2][:, 0:CH], rw[:, :], rx[:, c * CH:(c + 1) * CH], start=False, stop=True)
                last.then_inc(summed, 1)

        @block.scalar
        def _(act):
            if bias is not None:
                act.wait_ge(loaded, loads)
            for c in range(NC):
                act.wait_ge(summed, c + 1)
                nc.scalar.activation(out[:, c * CH:(c + 1) * CH], acc[c % 2][:, 0:CH], func,
                                     bias=b[:, 0:1] if bias is not None else 0.0).then_inc(done, 1)


def layernorm(nc, K, tag, x, out, gain=None, shift=None, add=None, mix=None):
    with Stage(nc, tag) as s:
        loaded, added, meaned, centred, squared, varied, rooted, inverted, scaled = (
            s.sem(x) for x in ("loaded", "added", "meaned", "centred", "squared", "varied", "rooted", "inverted", "scaled"))
        gb = s.sb("gb", [P, 2])
        sm = s.sb("sm", [P, 2, CH])
        xc = s.sb("xc", [P, 2, CH])
        sq = s.sb("sq", [P, 2, CH])
        sd = s.sb("sd", [P, 2, CH])
        inv = s.sb("inv", [P, 2, CH])
        nrm = s.sb("nrm", [P, 2, CH])
        mean = [s.ps(f"mean{i}") for i in range(2)]
        var = [s.ps(f"var{i}") for i in range(2)]
        affine = gain is not None
        block = s.block()

        def part(c):
            return slice(c * CH, (c + 1) * CH)

        @block.sync
        def _(sp):
            if affine:
                sp.dma_start(gb[:, 0:1], gain.rearrange("(p o) -> p o", o=1)).then_inc(loaded, 16)
                sp.dma_start(gb[:, 1:2], shift.rearrange("(p o) -> p o", o=1)).then_inc(loaded, 16)

        @block.tensor
        def _(pe):
            for c in range(NC + 1):
                if c < NC:
                    pe.wait_ge(added, c + 1)
                    if c >= 2:
                        pe.wait_ge(centred, c - 1)
                    nc.tensor.matmul(mean[c % 2][:, 0:CH], K.mean[:, :], sm[:, c % 2, :], start=True, stop=True).then_inc(meaned, 1)
                if c >= 1:
                    pe.wait_ge(squared, c)
                    if c >= 3:
                        pe.wait_ge(rooted, c - 2)
                    nc.tensor.matmul(var[(c - 1) % 2][:, 0:CH], K.mean[:, :], sq[:, (c - 1) % 2, :], start=True, stop=True).then_inc(varied, 1)

        @block.scalar
        def _(act):
            if affine:
                act.wait_ge(loaded, 32)
            for c in range(NC + 1):
                if c < NC:
                    act.wait_ge(centred, c + 1)
                    if c >= 2:
                        act.wait_ge(varied, c - 1)
                    nc.scalar.activation(sq[:, c % 2, :], xc[:, c % 2, :], ACT.Square).then_inc(squared, 1)
                if c >= 1:
                    d = c - 1
                    act.wait_ge(varied, c)
                    if d >= 2:
                        act.wait_ge(inverted, d - 1)
                    nc.scalar.activation(sd[:, d % 2, :], var[d % 2][:, 0:CH], ACT.Sqrt, bias=K.eps[:, 0:1]).then_inc(rooted, 1)

        @block.vector
        def _(dve):
            for c in range(NC + 2):
                if c < NC:
                    if c >= 2:
                        dve.wait_ge(meaned, c - 1)
                        dve.wait_ge(centred, c - 1)
                    if add is not None:
                        nc.vector.tensor_tensor(sm[:, c % 2, :], x[:, part(c)], add[:, part(c)], ALU.add).then_inc(added, 1)
                    else:
                        nc.vector.tensor_copy(sm[:, c % 2, :], x[:, part(c)]).then_inc(added, 1)
                    dve.wait_ge(meaned, c + 1)
                    dve.wait_ge(added, c + 1)
                    if c >= 2:
                        dve.wait_ge(squared, c - 1)
                        dve.wait_ge(scaled, c - 1)
                    nc.vector.tensor_tensor(xc[:, c % 2, :], sm[:, c % 2, :], mean[c % 2][:, 0:CH], ALU.subtract).then_inc(centred, 1)
                if 1 <= c <= NC:
                    d = c - 1
                    dve.wait_ge(rooted, c)
                    if d >= 2:
                        dve.wait_ge(scaled, d - 1)
                    nc.vector.reciprocal(inv[:, d % 2, :], sd[:, d % 2, :]).then_inc(inverted, 1)
                    dve.wait_ge(inverted, c)
                    dve.wait_ge(centred, c)
                    dst = nrm[:, d % 2, :] if affine else out[:, part(d)]
                    nc.vector.tensor_tensor(dst, xc[:, d % 2, :], inv[:, d % 2, :], ALU.mult).then_inc(scaled, 1)
                    if affine:
                        if d == 0:
                            dve.wait_ge(loaded, 32)
                        dve.wait_ge(scaled, c)
                        nc.vector.tensor_scalar(out[:, part(d)], nrm[:, d % 2, :], gb[:, 0:1], gb[:, 1:2], ALU.mult, ALU.add).then_inc(loaded, 1)
            if affine:
                dve.wait_ge(loaded, 32 + NC)


def typed_linear(nc, K, tag, x, weights, outs):
    M = len(weights)
    with Stage(nc, tag) as s:
        loaded, masked, used, summed, copied = (s.sem(x) for x in ("loaded", "masked", "used", "summed", "copied"))
        w = s.sb("w", [P, M, NTYPES, P])
        xm = s.sb("xm", [P, 2, CH])
        acc = [s.ps(f"acc{m}") for m in range(M)]
        block = s.block()

        @block.sync
        def _(sp):
            for m in range(M):
                sp.dma_start(w[:, m, :, :], weights[m].rearrange("t d o -> d t o")).then_inc(loaded, 16)

        @block.vector
        def _(dve):
            def chunk(c):
                for t in range(NTYPES):
                    if not (isinstance(c, int) and t < 2):
                        dve.wait_ge(used, c * NTYPES + t - 1)
                    nc.vector.scalar_tensor_tensor(xm[:, t % 2, :], K.ntype[:, bass.ds(c * CH, CH)], float(t),
                                                   x[:, bass.ds(c * CH, CH)], ALU.is_equal, ALU.mult).then_inc(masked, 1)
            chunk(0)
            with dve.Fori(1, NC) as c:
                chunk(c)

        @block.tensor
        def _(pe):
            pe.wait_ge(loaded, 16 * M)

            def chunk(c):
                if not isinstance(c, int):
                    pe.wait_ge(copied, c * M)
                for t in range(NTYPES):
                    pe.wait_ge(masked, c * NTYPES + t + 1)
                    for m in range(M):
                        last = nc.tensor.matmul(acc[m][:, 0:CH], w[:, m, t, :], xm[:, t % 2, :], start=t == 0, stop=t == NTYPES - 1)
                    last.then_inc(used, 1)
            chunk(0)
            with pe.Fori(1, NC) as c:
                chunk(c)

        @block.scalar
        def _(act):
            with act.Fori(0, NC) as c:
                act.wait_ge(used, (c + 1) * NTYPES)
                for m in range(M):
                    nc.scalar.activation(outs[m][:, bass.ds(c * CH, CH)], acc[m][:, 0:CH], ACT.Copy).then_inc(copied, 1)


def sum_edges(nc, K, D, tag, table=None, linear_in=None):
    with Stage(nc, tag) as s:
        idx_in = [s.sem(f"idx_in{u}") for u in range(2)]
        msg_in = [s.sem(f"msg_in{u}") for u in range(2)]
        stored = [s.sem(f"stored{u}") for u in range(2)]
        began, turned, scanned, turned_back, copied = (s.sem(x) for x in ("began", "turned", "scanned", "turned_back", "copied"))
        idx = [s.sb(f"idx{u}", [P, J], I32) for u in range(2)]
        rows = [s.sb(f"rows{u}", [P, W]) for u in range(2)]
        run = [s.sb(f"run{u}", [P, W]) for u in range(2)]
        out = [s.sb(f"out{u}", [P, J, P]) for u in range(2)]
        msg = [s.ps(f"msg{u}") for u in range(2)]
        back = [s.ps(f"back{u}") for u in range(2)]
        sums = D.sums.rearrange("(g j p) d -> g p j d", j=J, p=P)
        block = s.block()

        def store(sp, it, u, g):
            sp.wait_ge(copied, g + 1)
            sp.dma_start(sums[bass.ds(g, 1), :, :, :].rearrange("g p j d -> (g p) j d"), out[u][:, :, :]).then_inc(stored[u], 16)

        @block.sync
        def _(sp):
            def step(it, u):
                g = it * 2 + u
                if table is not None:
                    if not first(it, u, 2):
                        sp.wait_ge(msg_in[u], it * 64)
                    sp.dma_start(idx[u][:, :], D.src4[bass.ds(g, 1), :, :].rearrange("g p j -> (g p) j")).then_inc(idx_in[u], 16)
                else:
                    if not first(it, u, 2):
                        sp.wait_ge(scanned, g - 1)
                    sp.dma_start(rows[u][:, :], linear_in[:, bass.ds(g * W, W)]).then_inc(msg_in[u], 16)
                if not first(it, u, 2):
                    store(sp, it, u, g - 2)
            pairs(sp, step)
            store(sp, 0, 0, G - 2)
            store(sp, 0, 1, G - 1)
            for u in range(2):
                sp.wait_ge(stored[u], 16 * G // 2)

        if table is not None:
            @block.gpsimd
            def _(pool):
                def step(it, u):
                    g = it * 2 + u
                    pool.wait_ge(idx_in[u], it * 16 + 16)
                    if not first(it, u, 2):
                        pool.wait_ge(turned, g - 1)
                    pool.sem_inc(began, 1)
                    for j in range(J):
                        nc.gpsimd.indirect_dma_start(rows[u][:, j * P:(j + 1) * P], None, table,
                                                     bass.IndirectOffsetOnAxis(ap=idx[u][:, j:j + 1], axis=0)).then_inc(msg_in[u], 16)
                pairs(pool, step)

        @block.tensor
        def _(pe):
            def step(it, u):
                g = it * 2 + u
                if table is not None:
                    pe.wait_ge(msg_in[u], it * 64 + 64)
                    if not first(it, u, 2):
                        pe.wait_ge(scanned, g - 1)
                    for j in range(J):
                        last = nc.tensor.transpose(msg[u][:, j * P:(j + 1) * P], rows[u][:, j * P:(j + 1) * P], K.ident[:, :])
                    last.then_inc(turned, 1)
                if not first(it, u, 1):
                    turn_back(g - 1, 1 - u, first(it, u, 3))

            def turn_back(h, v, early):
                pe.wait_ge(scanned, h + 1)
                if not early:
                    pe.wait_ge(copied, h - 1)
                for j in range(J):
                    last = nc.tensor.transpose(back[v][:, j * P:(j + 1) * P], run[v][:, j * P:(j + 1) * P], K.ident[:, :])
                last.then_inc(turned_back, 1)
            pairs(pe, step)
            turn_back(G - 1, 1, False)

        @block.vector
        def _(dve):
            def step(it, u):
                g = it * 2 + u
                if table is not None:
                    dve.wait_ge(turned, g + 1)
                    data = msg[u]
                else:
                    dve.wait_ge(msg_in[u], it * 16 + 16)
                    data = rows[u]
                if not first(it, u, 2):
                    dve.wait_ge(turned_back, g - 1)
                if not first(it, u, 1):
                    dve.wait_ge(scanned, g)
                nc.vector.tensor_tensor_scan(run[u][:, :], K.same[:, bass.ds(g * W, W)], data[:, :],
                                             0.0 if first(it, u, 1) else run[1 - u][:, W - 1:W],
                                             ALU.mult, ALU.add).then_inc(scanned, 1)
            pairs(dve, step)

        @block.scalar
        def _(act):
            def step(it, u):
                g = it * 2 + u
                act.wait_ge(turned_back, g + 1)
                if not first(it, u, 2):
                    act.wait_ge(stored[u], it * 16)
                nc.scalar.activation(out[u][:, :, :].rearrange("p j d -> p (j d)"), back[u][:, :], ACT.Copy).then_inc(copied, 1)
            pairs(act, step)


def relation_table(nc, K, D, tag, layer, key, value):
    Q = 4
    with Stage(nc, tag) as s:
        loaded, zeroed, put, ready, product, evac_k, evac_v = (
            s.sem(x) for x in ("loaded", "zeroed", "put", "ready", "product", "evac_k", "evac_v"))
        node_in = s.sem("node_in")
        stored = [s.sem(f"stored{q}") for q in range(Q)]
        wk = s.sb("wk", [P, RELS, P])
        wv = s.sb("wv", [P, RELS, P])
        pri = s.sb("pri", [P, RELS])
        kv = s.sb("kv", [P, 2, P])
        part = [s.sb(f"part{q}", [P, RELS // Q, 2 * P]) for q in range(Q)]
        bank = [s.ps(f"bank{i}") for i in range(8)]
        table = D.table.rearrange("(t p r) d -> t p r d", p=P, r=RELS)
        block = s.block()

        @block.gpsimd
        def _(pool):
            nc.gpsimd.memset(wk[:, :, :], 0.0).then_inc(zeroed, 1)
            nc.gpsimd.memset(wv[:, :, :], 0.0).then_inc(zeroed, 1)

        @block.sync
        def _(sp):
            for h in range(HEADS):
                sp.dma_start(pri[h * HS:(h + 1) * HS, :], D.L0_gnn_pri[layer, h, :].partition_broadcast(HS)).then_inc(loaded, 16)
            sp.wait_ge(zeroed, 2)
            for h in range(HEADS):
                f = slice(h * HS, (h + 1) * HS)
                sp.dma_start(wk[f, :, f], D.L0_gnn_Watt[layer, h, :, :, :].rearrange("t d o -> d t o")).then_inc(put, 16)
                sp.dma_start(wv[f, :, f], D.L0_gnn_Wmsg[layer, h, :, :, :].rearrange("t d o -> d t o")).then_inc(put, 16)

            def tile(t):
                for q in range(Q):
                    sp.wait_ge(evac_k, t * 8 + 2 * q + 2)
                    sp.wait_ge(evac_v, t * 8 + 2 * q + 2)
                    sp.dma_start(table[bass.ds(t, 1), :, q * 8:q * 8 + 8, :].rearrange("t p r d -> (t p) r d"),
                                 part[q][:, :, :]).then_inc(stored[q], 16)
            with sp.Fori(0, NT) as t:
                tile(t)
            for q in range(Q):
                sp.wait_ge(stored[q], 16 * NT)

        @block.vector
        def _(dve):
            dve.wait_ge(loaded, 16 * HEADS)
            dve.wait_ge(put, 32 * HEADS)
            nc.vector.scalar_tensor_tensor(wk[:, :, :], wk[:, :, :], float(HS) ** -0.5,
                                           pri[:, :].unsqueeze(2).broadcast_to([P, RELS, P]), ALU.mult, ALU.mult).then_inc(ready, 1)

            def tile(t):
                for c in range(8):
                    dve.wait_ge(product, t * 16 + 2 * c + 1)
                    if not isinstance(t, int):
                        dve.wait_ge(stored[c // 2], t * 16)
                    nc.vector.tensor_copy(part[c // 2][:, (c % 2) * 4:(c % 2) * 4 + 4, 0:P],
                                          bank[(2 * c) % 8][:, :].rearrange("p (r d) -> p r d", d=P)).then_inc(evac_k, 1)
            tile(0)
            with dve.Fori(1, NT) as t:
                tile(t)

        @block.scalar
        def _(act):
            def tile(t):
                if not isinstance(t, int):
                    act.wait_ge(product, t * 16)
                nc.scalar.activation(kv[:, 0, :], key[:, bass.ds(t * P, P)], ACT.Copy).then_inc(node_in, 1)
                nc.scalar.activation(kv[:, 1, :], value[:, bass.ds(t * P, P)], ACT.Copy).then_inc(node_in, 1)
                for c in range(8):
                    act.wait_ge(product, t * 16 + 2 * c + 2)
                    if not isinstance(t, int):
                        act.wait_ge(stored[c // 2], t * 16)
                    nc.scalar.activation(part[c // 2][:, (c % 2) * 4:(c % 2) * 4 + 4, P:2 * P],
                                         bank[(2 * c + 1) % 8][:, :].rearrange("p (r d) -> p r d", d=P), ACT.Copy).then_inc(evac_v, 1)
            tile(0)
            with act.Fori(1, NT) as t:
                tile(t)

        @block.tensor
        def _(pe):
            pe.wait_ge(ready, 1)

            def tile(t):
                pe.wait_ge(node_in, t * 2 + 2)
                for c in range(8):
                    for k, (w, evac) in enumerate(((wk, evac_k), (wv, evac_v))):
                        if not (isinstance(t, int) and c < 4):
                            pe.wait_ge(evac, t * 8 + c - 3)
                        nc.tensor.matmul(bank[(2 * c + k) % 8][:, :], kv[:, k, :],
                                         w[:, c * 4:c * 4 + 4, :].rearrange("p r d -> p (r d)"), start=True, stop=True).then_inc(product, 1)
            tile(0)
            with pe.Fori(1, NT) as t:
                tile(t)


def attention(nc, K, D, tag):
    V = P + HEADS
    with Stage(nc, tag) as s:
        idx_in, rows_in, query_in, bias_in, stored = ([s.sem(f"{x}{u}") for u in range(2)] for x in
                                                      ("idx_in", "rows_in", "query_in", "bias_in", "stored"))
        q_turned, k_turned, v_turned, v_copied, spread, multiplied, edged, largest, difference, relued, weighted = (
            s.sem(x) for x in ("q_turned", "k_turned", "v_turned", "v_copied", "spread", "multiplied", "edged", "largest",
                               "difference", "relued", "weighted"))
        began = s.sem("began")
        before, messaged, summed, turned_back, copied = (s.sem(x) for x in ("before", "messaged", "summed", "turned_back", "copied"))
        idx = [s.sb(f"idx{u}", [P, J], I32) for u in range(2)]
        rows = [s.sb(f"rows{u}", [P, J, 2 * P]) for u in range(2)]
        query = [s.sb(f"query{u}", [P, J, P]) for u in range(2)]
        bias = [s.sb(f"bias{u}", [P, W], BF16) for u in range(2)]
        qx = [s.sb(f"qx{u}", [P, W]) for u in range(2)]
        prod = [s.sb(f"prod{u}", [P, W + 1]) for u in range(2)]
        b = [s.sb(f"b{u}", [P, W]) for u in range(2)]
        up = s.sb("up", [P, W])
        down = s.sb("down", [P, W])
        decay = [s.sb(f"decay{u}", [P, W]) for u in range(2)]
        weight = [s.sb(f"weight{u}", [P, W]) for u in range(2)]
        value = [s.sb(f"value{u}", [P, W]) for u in range(2)]
        message = s.sb("message", [P, W])
        run = [s.sb(f"run{u}", [P, W]) for u in range(2)]
        den = [s.sb(f"den{u}", [P, W]) for u in range(2)]
        out = [s.sb(f"out{u}", [P, J, V]) for u in range(2)]
        pq, pk, pv, pshift, pdiff, pback, pden = (s.ps(x) for x in ("pq", "pk", "pv", "pshift", "pdiff", "pback", "pden"))
        rows_d = D.query_rows.rearrange("(g j p) d -> g p j d", j=J, p=P)
        sums = D.att_sums.rearrange("(g j p) d -> g p j d", j=J, p=P)
        kvrow = D.kvrow.rearrange("(g j p) -> g p j", j=J, p=P)
        block = s.block()

        @block.sync
        def _(sp):
            def store(u, g):
                sp.wait_ge(copied, 2 * (g + 1))
                sp.dma_start(sums[bass.ds(g, 1), :, :, :].rearrange("g p j d -> (g p) j d"), out[u][:, :, :]).then_inc(stored[u], 16)

            def step(it, u):
                g = it * 2 + u
                at = sp.snap(g * W) if not isinstance(g, int) else g * W
                if not first(it, u, 2):
                    sp.wait_ge(rows_in[u], it * 64)
                with nc.allow_non_contiguous_dma(reason="one index per partition and tile"):
                    sp.dma_start(idx[u][:, :], kvrow[bass.ds(g, 1), :, :].rearrange("g p j -> (g p) j")).then_inc(idx_in[u], 16)
                if not first(it, u, 2):
                    sp.wait_ge(q_turned, g - 1)
                    sp.wait_ge(largest, g - 1)
                sp.dma_start(query[u][:, :, :], rows_d[bass.ds(g, 1), :, :, :].rearrange("g p j d -> (g p) j d")).then_inc(query_in[u], 16)
                sp.dma_start(bias[u][:, :], D.start_bias[bass.ds(at, W)].partition_broadcast(P)).then_inc(bias_in[u], 16)
                if not first(it, u, 4):
                    store(u, g - 4)
            pairs(sp, step)
            for g in range(G - 4, G):
                store(g % 2, g)
            for u in range(2):
                sp.wait_ge(stored[u], 16 * G // 2)

        @block.gpsimd
        def _(pool):
            def step(it, u):
                g = it * 2 + u
                pool.wait_ge(idx_in[u], it * 16 + 16)
                if not first(it, u, 2):
                    pool.wait_ge(v_turned, g - 1)
                pool.sem_inc(began, 1)
                for j in range(J):
                    nc.gpsimd.indirect_dma_start(rows[u][:, j, :], None, D.table,
                                                 bass.IndirectOffsetOnAxis(ap=idx[u][:, j:j + 1], axis=0)).then_inc(rows_in[u], 16)
            pairs(pool, step)

        @block.tensor
        def _(pe):
            def turn(it, u):
                g = it * 2 + u
                pe.wait_ge(query_in[u], it * 16 + 16)
                if not first(it, u, 1):
                    pe.wait_ge(spread, g)
                for j in range(J):
                    last = nc.tensor.transpose(pq[:, j * P:(j + 1) * P], query[u][:, j, :], K.ident[:, :])
                last.then_inc(q_turned, 1)
                pe.wait_ge(rows_in[u], it * 64 + 64)
                if not first(it, u, 1):
                    pe.wait_ge(multiplied, g)
                for j in range(J):
                    last = nc.tensor.transpose(pk[:, j * P:(j + 1) * P], rows[u][:, j, 0:P], K.ident[:, :])
                last.then_inc(k_turned, 1)
                if not first(it, u, 1):
                    pe.wait_ge(v_copied, g)
                for j in range(J):
                    last = nc.tensor.transpose(pv[:, j * P:(j + 1) * P], rows[u][:, j, P:2 * P], K.ident[:, :])
                last.then_inc(v_turned, 1)

            def turn_back(u, h, early):
                pe.wait_ge(summed, 2 * (h + 1))
                if not early:
                    pe.wait_ge(copied, 2 * h)
                for j in range(J):
                    nc.tensor.transpose(pback[:, j * P:(j + 1) * P], run[u][:, j * P:(j + 1) * P], K.ident[:, :])
                for j in range(J):
                    last = nc.tensor.matmul(pden[:, j * HEADS:(j + 1) * HEADS], den[u][:, j * P:(j + 1) * P],
                                            K.ident[:, 0:P:HS], start=True, stop=True)
                last.then_inc(turned_back, 1)

            def step(it, u, last_group=False):
                g = it * 2 + u
                pe.wait_ge(multiplied, g + 1)
                if not first(it, u, 1):
                    pe.wait_ge(largest, g)
                nc.tensor.matmul(pshift[:, :], K.headsum[:, :], prod[u][:, 0:W], start=True, stop=True).then_inc(edged, 1)
                if not first(it, u, 1):
                    pe.wait_ge(relued, 2 * g)
                nc.tensor.matmul(pdiff[:, :], K.headsum[:, :], prod[u][:, 1:W + 1], start=True, stop=False)
                if not first(it, u, 2):
                    turn_back(u, g - 2, first(it, u, 3))
                if not last_group:
                    turn(it + u, 1 - u)
                pe.wait_ge(largest, g + 1)
                nc.tensor.matmul(pdiff[:, :], K.negid[:, :], b[u][:, :], start=False, stop=True).then_inc(difference, 1)
            turn(0, 0)
            step(0, 0)
            step(0, 1)
            step(1, 0)
            step(1, 1)
            with pe.Fori(2, G // 2 - 1) as it:
                step(it, 0)
                step(it, 1)
            step(G // 2 - 1, 0)
            step(G // 2 - 1, 1, last_group=True)
            turn_back(0, G - 2, False)
            turn_back(1, G - 1, False)

        @block.vector
        def _(dve):
            def accumulate(u, h, early1, early2):
                dve.wait_ge(weighted, 2 * (h + 1))
                dve.wait_ge(v_copied, h + 1)
                if not early1:
                    dve.wait_ge(summed, 2 * h)
                nc.vector.tensor_tensor(message[:, :], value[u][:, :], weight[u][:, :], ALU.mult).then_inc(messaged, 1)
                dve.wait_ge(messaged, h + 1)
                if not early2:
                    dve.wait_ge(turned_back, h - 1)
                nc.vector.tensor_tensor_scan(run[u][:, :], decay[u][:, :], message[:, :],
                                             0.0 if early1 else run[1 - u][:, W - 1:W], ALU.mult, ALU.add).then_inc(summed, 1)
                nc.vector.tensor_tensor_scan(den[u][:, :], decay[u][:, :], weight[u][:, :],
                                             0.0 if early1 else den[1 - u][:, W - 1:W], ALU.mult, ALU.add).then_inc(summed, 1)

            def step(it, u):
                g = it * 2 + u
                dve.wait_ge(q_turned, g + 1)
                if not first(it, u, 2):
                    dve.wait_ge(multiplied, g - 1)
                if not first(it, u, 1):
                    dve.wait_ge(spread, g)
                nc.vector.tensor_tensor_scan(qx[u][:, :], K.same[:, bass.ds(g * W, W)], pq[:, :],
                                             0.0 if first(it, u, 1) else qx[1 - u][:, W - 1:W],
                                             ALU.mult, ALU.add).then_inc(spread, 1)
                if not first(it, u, 2):
                    dve.wait_ge(difference, g - 1)
                if first(it, u, 1):
                    nc.vector.memset(prod[u][:, 0:1], 0.0).then_inc(before, 1)
                else:
                    dve.wait_ge(multiplied, g)
                    nc.vector.tensor_copy(prod[u][:, 0:1], prod[1 - u][:, W:W + 1]).then_inc(before, 1)
                dve.wait_ge(k_turned, g + 1)
                dve.wait_ge(spread, g + 1)
                dve.wait_ge(before, g + 1)
                nc.vector.tensor_tensor(prod[u][:, 1:W + 1], qx[u][:, :], pk[:, :], ALU.mult).then_inc(multiplied, 1)
                if not first(it, u, 2):
                    accumulate(u, g - 2, first(it, u, 3), first(it, u, 4))
                dve.wait_ge(edged, g + 1)
                dve.wait_ge(bias_in[u], it * 16 + 16)
                if not first(it, u, 1):
                    dve.wait_ge(largest, g)
                nc.vector.tensor_tensor_scan(b[u][:, :], pshift[:, :], bias[u][:, :],
                                             0.0 if first(it, u, 1) else b[1 - u][:, W - 1:W],
                                             ALU.max, ALU.add).then_inc(largest, 1)
            pairs(dve, step)
            accumulate(0, G - 2, False, False)
            accumulate(1, G - 1, False, False)

        @block.scalar
        def _(act):
            def copy_out(u, h, early):
                act.wait_ge(turned_back, h + 1)
                if not early:
                    act.wait_ge(stored[u], (h // 2) * 16 if isinstance(h, int) else 0)
                nc.scalar.activation(out[u][:, :, 0:P], pback[:, :].rearrange("p (j d) -> p j d", j=J), ACT.Copy).then_inc(copied, 1)
                nc.scalar.activation(out[u][:, :, P:V], pden[:, 0:J * HEADS].rearrange("p (j d) -> p j d", j=J), ACT.Copy).then_inc(copied, 1)

            def step(it, u):
                g = it * 2 + u
                act.wait_ge(v_turned, g + 1)
                if not first(it, u, 2):
                    act.wait_ge(messaged, g - 1)
                nc.scalar.activation(value[u][:, :], pv[:, :], ACT.Copy).then_inc(v_copied, 1)
                if not first(it, u, 2):
                    if not first(it, u, 4):
                        act.wait_ge(stored[u], (it - 1) * 16)
                    copy_out(u, g - 2, True)
                act.wait_ge(difference, g + 1)
                if not first(it, u, 1):
                    act.wait_ge(weighted, 2 * g)
                nc.scalar.activation(up[:, :], pdiff[:, :], ACT.Relu).then_inc(relued, 1)
                nc.scalar.activation(down[:, :], pdiff[:, :], ACT.Relu, scale=-1.0).then_inc(relued, 1)
                if not first(it, u, 2):
                    act.wait_ge(summed, 2 * (g - 1))
                act.wait_ge(relued, 2 * g + 1)
                nc.scalar.activation(decay[u][:, :], up[:, :], ACT.Exp, scale=-1.0).then_inc(weighted, 1)
                act.wait_ge(relued, 2 * g + 2)
                nc.scalar.activation(weight[u][:, :], down[:, :], ACT.Exp, scale=-1.0).then_inc(weighted, 1)
            pairs(act, step)
            copy_out(0, G - 2, False)
            copy_out(1, G - 1, False)


def mix_with_input(nc, K, D, tag, layer, new, old, out):
    with Stage(nc, tag) as s:
        loaded, gated, hot, spread_, lit, done, mixed = (
            s.sem(x) for x in ("loaded", "gated", "hot", "spread", "lit", "done", "mixed"))
        skip = s.sb("skip", [NTYPES, 1])
        gate = s.sb("gate", [NTYPES, 1])
        gates = s.sb("gates", [NTYPES, P])
        onehot = s.sb("onehot", [NTYPES, NP])
        lifted = s.sb("lifted", [P, 2, CH])
        diff = s.sb("diff", [P, 2, CH])
        alpha = [s.ps(f"alpha{i}") for i in range(2)]
        block = s.block()

        @block.sync
        def _(sp):
            sp.dma_start(skip[:, :], D.L0_gnn_skip[layer, :].rearrange("(p o) -> p o", o=1)).then_inc(loaded, 16)

        @block.tensor
        def _(pe):
            pe.wait_ge(hot, 2)
            for c in range(NC):
                if c >= 2:
                    pe.wait_ge(mixed, 2 * (c - 1))
                nc.tensor.matmul(alpha[c % 2][:, 0:CH], gates[:, :], onehot[:, c * CH:(c + 1) * CH], start=True, stop=True).then_inc(spread_, 1)

        @block.scalar
        def _(act):
            act.wait_ge(loaded, 16)
            nc.scalar.activation(gate[:, :], skip[:, :], ACT.Sigmoid).then_inc(gated, 1)
            for c in range(NC):
                if c >= 2:
                    act.wait_ge(mixed, 2 * (c - 1))
                nc.scalar.activation(lifted[:, c % 2, :], new[:, c * CH:(c + 1) * CH], ACT.Silu).then_inc(lit, 1)

        @block.vector
        def _(dve):
            dve.wait_ge(gated, 1)
            nc.vector.tensor_copy(gates[:, :], gate[:, :].broadcast_to([NTYPES, P])).then_inc(hot, 1)
            nc.vector.tensor_scalar(onehot[:, :], K.ntype[0:NTYPES, :], K.pid[0:NTYPES, 0:1], None, ALU.is_equal).then_inc(hot, 1)
            for c in range(NC):
                part = slice(c * CH, (c + 1) * CH)
                dve.wait_ge(lit, c + 1)
                if c >= 2:
                    dve.wait_ge(done, c - 1)
                nc.vector.tensor_tensor(diff[:, c % 2, :], lifted[:, c % 2, :], old[:, part], ALU.subtract).then_inc(mixed, 1)
                dve.wait_ge(spread_, c + 1)
                dve.wait_ge(mixed, 2 * c + 1)
                nc.vector.tensor_tensor(diff[:, c % 2, :], diff[:, c % 2, :], alpha[c % 2][:, 0:CH], ALU.mult).then_inc(mixed, 1)
                dve.wait_ge(mixed, 2 * c + 2)
                nc.vector.tensor_tensor(out[:, part], diff[:, c % 2, :], old[:, part], ALU.add).then_inc(done, 1)


def add_nodes(nc, tag, out, a, b, op=None):
    with Stage(nc, tag) as s:
        block = s.block()

        @block.vector
        def _(dve):
            nc.vector.tensor_tensor(out[:, :], a[:, :], b[:, :], op or ALU.add)


def degree_scale(nc, K, D):
    with Stage(nc, "deg") as s:
        loaded, made, rooted = s.sem("loaded"), s.sem("made"), s.sem("rooted")
        deg = s.sb("deg", [P, NP])
        block = s.block()

        @block.sync
        def _(sp):
            sp.dma_start(deg[:, :], D.degree.partition_broadcast(P)).then_inc(loaded, 16)

        @block.scalar
        def _(act):
            act.wait_ge(loaded, 16)
            nc.scalar.activation(deg[:, :], deg[:, :], ACT.Sqrt, bias=K.ones[:, 0:1]).then_inc(rooted, 1)

        @block.vector
        def _(dve):
            dve.wait_ge(rooted, 1)
            nc.vector.reciprocal(K.isd[:, :], deg[:, :]).then_inc(made, 1)


def batch_norm(nc, K, D, tag, sums, own, bias, gain, shift, out, relu):
    with Stage(nc, tag) as s:
        loaded, made, squared, rooted = (s.sem(x) for x in ("loaded", "made", "squared", "rooted"))
        cols = s.sb("cols", [P, 3])
        y = s.sb("y", [P, NP])
        sq = s.sb("sq", [P, N])
        st = s.sb("st", [P, 6])
        block = s.block()

        @block.sync
        def _(sp):
            for i, v in enumerate((bias, gain, shift)):
                sp.dma_start(cols[:, i:i + 1], v.rearrange("(p o) -> p o", o=1)).then_inc(loaded, 16)

        @block.vector
        def _(dve):
            link = linked(dve, made)
            link(nc.vector.tensor_tensor(y[:, :], sums[:, :], own[:, :], ALU.add))
            link(nc.vector.tensor_tensor(y[:, :], y[:, :], K.isd[:, :], ALU.mult))
            dve.wait_ge(loaded, 48)
            link(nc.vector.tensor_scalar(y[:, :], y[:, :], cols[:, 0:1], None, ALU.add))
            link(nc.vector.tensor_reduce(st[:, 0:1], y[:, 0:N], AX.X, ALU.add))
            link(nc.vector.tensor_scalar(st[:, 0:1], st[:, 0:1], 1.0 / N, None, ALU.mult))
            link(nc.vector.tensor_scalar(y[:, :], y[:, :], st[:, 0:1], None, ALU.subtract))
            link(nc.vector.tensor_tensor(sq[:, :], y[:, 0:N], y[:, 0:N], ALU.mult))
            link(nc.vector.tensor_reduce(st[:, 1:2], sq[:, :], AX.X, ALU.add))
            dve.wait_ge(rooted, 1)
            link(nc.vector.reciprocal(st[:, 3:4], st[:, 2:3]))
            link(nc.vector.tensor_tensor(st[:, 4:5], st[:, 3:4], cols[:, 1:2], ALU.mult))
            link(nc.vector.tensor_scalar(y[:, :], y[:, :], st[:, 4:5], cols[:, 2:3], ALU.mult, ALU.add))
            nc.vector.tensor_scalar(out[:, :], y[:, :], 0.0 if relu else -3.0e38, None, ALU.max).then_inc(squared, 1)

        @block.scalar
        def _(act):
            act.wait_ge(made, 8)
            nc.scalar.activation(st[:, 2:3], st[:, 1:2], ACT.Sqrt, scale=1.0 / N, bias=K.eps[:, 0:1]).then_inc(rooted, 1)


def message_weights(nc, K, D, up, down):
    c = 1.0 / (10.0 * (2 * 32) ** 0.5)
    with Stage(nc, "mwt") as s:
        zeroed, loaded, made = s.sem("zeroed"), s.sem("loaded"), s.sem("made")
        tmp = [s.sb(f"tmp{i}", [P, 32]) for i in range(3)]
        block = s.block()

        @block.gpsimd
        def _(pool):
            for m in (*up, *down, *tmp):
                nc.gpsimd.memset(m[:, :], 0.0).then_inc(zeroed, 1)

        @block.sync
        def _(sp):
            sp.wait_ge(zeroed, 8)
            sp.dma_start(up[0][0:32, 0:32], D.L2_gnn_W_up_s).then_inc(loaded, 16)
            sp.dma_start(tmp[0][0:32, :], D.L2_gnn_W_out_s[0:32, :]).then_inc(loaded, 16)
            for i in range(3):
                blk = slice(32 + 32 * i, 64 + 32 * i)
                sp.dma_start(up[0][32 + i:P:3, blk], D.L2_gnn_W_up_v).then_inc(loaded, 16)
                sp.dma_start(up[1][0:32, blk], D.L2_gnn_W_up_s).then_inc(loaded, 16)
                sp.dma_start(tmp[0][blk, :], D.L2_gnn_W_out_v[32:64, :]).then_inc(loaded, 16)
                sp.dma_start(tmp[1][blk, :], D.L2_gnn_W_out_v[0:32, :]).then_inc(loaded, 16)
                sp.dma_start(tmp[2][blk, :], D.L2_gnn_W_out_s[32:64, :]).then_inc(loaded, 16)

        @block.vector
        def _(dve):
            dve.wait_ge(loaded, 16 * 17)
            link = linked(dve, made)
            for m in up:
                link(nc.vector.tensor_scalar(m[:, :], m[:, :], 32 ** -0.5, None, ALU.mult))
            link(nc.vector.tensor_scalar(down[0][0:32, 0:32], tmp[0][0:32, :], c, None, ALU.mult))
            for i in range(3):
                blk = slice(32 + 32 * i, 64 + 32 * i)
                link(nc.vector.tensor_scalar(down[0][blk, 32 + i:P:3], tmp[0][blk, :], c, None, ALU.mult))
                link(nc.vector.tensor_scalar(down[1][blk, 32 + i:P:3], tmp[1][blk, :], c, None, ALU.mult))
                link(nc.vector.tensor_scalar(down[2][blk, 0:32], tmp[2][blk, :], c * 3 ** -0.5, None, ALU.mult))


def messages(nc, K, D, tag, down):
    with Stage(nc, tag) as s:
        idx_in, rows_in, edge_in, stored = ([s.sem(f"{x}{u}") for u in range(2)] for x in
                                            ("idx_in", "rows_in", "edge_in", "stored"))
        loaded, hidden, lit, radial, turned, upcopied, graded, multiplied, mapped, scanned, turned_back, copied = (
            s.sem(x) for x in ("loaded", "hidden", "lit", "radial", "turned", "upcopied", "graded", "multiplied", "mapped",
                               "scanned", "turned_back", "copied"))
        began, zeroed = s.sem("began"), s.sem("zeroed")
        a1 = s.sb("a1", [8, 64])
        a2 = s.sb("a2", [64, P])
        a3 = [s.sb(f"a3{k}", [64, P]) for k in range(3)]
        bb = s.sb("bb", [64, 2])
        idx = [s.sb(f"idx{u}", [P, J], I32) for u in range(2)]
        rows = [s.sb(f"rows{u}", [P, J, 2 * P]) for u in range(2)]
        ef = [s.sb(f"ef{u}", [8, W]) for u in range(2)]
        ya = [s.sb(f"ya{u}", [P, W]) for u in range(2)]
        yb = [s.sb(f"yb{u}", [P, W]) for u in range(2)]
        h1 = s.sb("h1", [64, W])
        h2 = s.sb("h2", [64, W])
        un = [s.sb(f"un{k}", [P, W]) for k in range(2)]
        graded_ = [s.sb(f"graded{k}", [P, W]) for k in range(3)]
        prod = [s.sb(f"prod{k}", [P, W]) for k in range(3)]
        run = [s.sb(f"run{u}", [P, W]) for u in range(2)]
        out = [s.sb(f"out{u}", [P, J, P]) for u in range(2)]
        ph, pm, pback = s.ps("ph"), s.ps("pm"), s.ps("pback")
        pr = [s.ps(f"pr{k}") for k in range(3)]
        pu = [s.ps(f"pu{k}") for k in range(2)]
        sums = D.sums.rearrange("(g j p) d -> g p j d", j=J, p=P)
        block = s.block()
        EIN = 6 * 16

        @block.sync
        def _(sp):
            sp.dma_start(a1[:, :], D.L2_gnn_A1).then_inc(loaded, 16)
            sp.dma_start(a2[:, 0:64], D.L2_gnn_A2).then_inc(loaded, 16)
            sp.dma_start(bb[:, 0:1], D.L2_gnn_b1.rearrange("(p o) -> p o", o=1)).then_inc(loaded, 16)
            sp.dma_start(bb[:, 1:2], D.L2_gnn_b2.rearrange("(p o) -> p o", o=1)).then_inc(loaded, 16)
            for k, which in enumerate(((0, 2, 2, 2), (1, 1, 1, 1), (3, 3, 3, 3))):
                for n, w in enumerate(which):
                    sp.dma_start(a3[k][:, n * 32:(n + 1) * 32], D.L2_gnn_A3[:, w * 32:(w + 1) * 32]).then_inc(loaded, 16)

            def store(u, g):
                sp.wait_ge(copied, g + 1)
                sp.dma_start(sums[bass.ds(g, 1), :, :, :].rearrange("g p j d -> (g p) j d"), out[u][:, :, :]).then_inc(stored[u], 16)

            def step(it, u):
                g = it * 2 + u
                at = sp.snap(g * W) if not isinstance(g, int) else g * W
                if not first(it, u, 2):
                    sp.wait_ge(rows_in[u], it * 64)
                sp.dma_start(idx[u][:, :], D.src4[bass.ds(g, 1), :, :].rearrange("g p j -> (g p) j")).then_inc(idx_in[u], 16)
                if not first(it, u, 2):
                    sp.wait_ge(graded, 3 * (g - 1))
                sp.dma_start(ef[u][:, :], D.ea8[:, bass.ds(at, W)]).then_inc(edge_in[u], 16)
                sp.dma_start(ya[u][:, :], D.ea4[0, bass.ds(at, W)].partition_broadcast(P)).then_inc(edge_in[u], 16)
                for n in range(4):
                    sp.dma_start(yb[u][n * 32:(n + 1) * 32, :],
                                 D.ea4[n, bass.ds(at, W)].partition_broadcast(32)).then_inc(edge_in[u], 16)
                if not first(it, u, 2):
                    store(u, g - 2)
            pairs(sp, step)
            store(0, G - 2)
            store(1, G - 1)
            for u in range(2):
                sp.wait_ge(stored[u], 16 * G // 2)

        @block.gpsimd
        def _(pool):
            def step(it, u):
                g = it * 2 + u
                pool.wait_ge(idx_in[u], it * 16 + 16)
                if not first(it, u, 2):
                    pool.wait_ge(turned, 2 * (g - 1))
                pool.sem_inc(began, 1)
                for j in range(J):
                    nc.gpsimd.indirect_dma_start(rows[u][:, j, :], None, D.utable,
                                                 bass.IndirectOffsetOnAxis(ap=idx[u][:, j:j + 1], axis=0)).then_inc(rows_in[u], 16)
            pairs(pool, step)

        @block.tensor
        def _(pe):
            pe.wait_ge(loaded, 16 * 16)
            pe.wait_ge(zeroed, 1)

            def radial_weights(it, u):
                g = it * 2 + u
                pe.wait_ge(edge_in[u], it * EIN + EIN)
                if not first(it, u, 1):
                    pe.wait_ge(lit, 2 * g)
                nc.tensor.matmul(ph[0:64, :], a1[:, :], ef[u][:, :], start=True, stop=True).then_inc(hidden, 1)
                pe.wait_ge(lit, 2 * g + 1)
                nc.tensor.matmul(ph[:, :], a2[:, :], h1[:, :], start=True, stop=True).then_inc(hidden, 1)
                pe.wait_ge(rows_in[u], it * 64 + 64)
                for k in range(2):
                    if not first(it, u, 1):
                        pe.wait_ge(upcopied, 2 * g - 1 + k)
                    for j in range(J):
                        last = nc.tensor.transpose(pu[k][:, j * P:(j + 1) * P], rows[u][:, j, k * P:(k + 1) * P], K.ident[:, :])
                    last.then_inc(turned, 1)
                pe.wait_ge(lit, 2 * g + 2)
                for k in range(3):
                    if not first(it, u, 1):
                        pe.wait_ge(graded, 3 * g - 2 + k)
                    nc.tensor.matmul(pr[k][:, :], a3[k][:, :], h2[:, :], start=True, stop=True).then_inc(radial, 1)

            def map_products(u, g, early):
                if not early:
                    pe.wait_ge(scanned, g)
                for k in range(3):
                    pe.wait_ge(multiplied, 3 * g + k + 1)
                    last = nc.tensor.matmul(pm[:, :], down[k][:, :], prod[k][:, :], start=k == 0, stop=k == 2)
                last.then_inc(mapped, 1)

            def turn_back(u, g, early):
                pe.wait_ge(scanned, g + 1)
                if not early:
                    pe.wait_ge(copied, g)
                for j in range(J):
                    last = nc.tensor.transpose(pback[:, j * P:(j + 1) * P], run[u][:, j * P:(j + 1) * P], K.ident[:, :])
                last.then_inc(turned_back, 1)

            def step(it, u):
                g = it * 2 + u
                radial_weights(it, u)
                if not first(it, u, 2):
                    turn_back(u, g - 2, first(it, u, 3))
                if not first(it, u, 1):
                    map_products(1 - u, g - 1, first(it, u, 2))
            pairs(pe, step)
            turn_back(0, G - 2, False)
            map_products(1, G - 1, False)
            turn_back(1, G - 1, False)

        @block.scalar
        def _(act):
            act.wait_ge(loaded, 16 * 16)

            def step(it, u):
                g = it * 2 + u
                act.wait_ge(hidden, 2 * g + 1)
                nc.scalar.activation(h1[:, :], ph[0:64, :], ACT.Silu, bias=bb[:, 0:1]).then_inc(lit, 1)
                act.wait_ge(hidden, 2 * g + 2)
                if not first(it, u, 1):
                    act.wait_ge(radial, 3 * g)
                nc.scalar.activation(h2[:, :], ph[0:64, :], ACT.Silu, bias=bb[:, 1:2]).then_inc(lit, 1)
                for k in range(2):
                    act.wait_ge(turned, 2 * g + k + 1)
                    if not first(it, u, 1):
                        act.wait_ge(multiplied, 3 * g)
                    nc.scalar.activation(un[k][:, :], pu[k][:, :], ACT.Copy).then_inc(upcopied, 1)
                if not first(it, u, 2):
                    copy_out(u, g - 2, it)

            def copy_out(u, h, it):
                act.wait_ge(turned_back, h + 1)
                if not (isinstance(it, int) and it < 2):
                    act.wait_ge(stored[u], (it - 1) * 16)
                nc.scalar.activation(out[u][:, :, :].rearrange("p j d -> p (j d)"), pback[:, :], ACT.Copy).then_inc(copied, 1)
            pairs(act, step)
            copy_out(0, G - 2, G // 2)
            copy_out(1, G - 1, G // 2)

        @block.vector
        def _(dve):
            nc.vector.memset(a2[:, 64:P], 0.0).then_inc(zeroed, 1)

            def scan(u, g, early):
                dve.wait_ge(mapped, g + 1)
                if not early:
                    dve.wait_ge(scanned, g)
                nc.vector.tensor_tensor_scan(run[u][:, :], K.same[:, bass.ds(g * W, W)], pm[:, :],
                                             0.0 if early else run[1 - u][:, W - 1:W], ALU.mult, ALU.add).then_inc(scanned, 1)

            def step(it, u):
                g = it * 2 + u
                dve.wait_ge(edge_in[u], it * EIN + EIN)
                for k, y in enumerate((ya, yb, yb)):
                    dve.wait_ge(radial, 3 * g + k + 1)
                    if not first(it, u, 1):
                        dve.wait_ge(multiplied, 3 * g - 2 + k)
                    nc.vector.tensor_tensor(graded_[k][:, :], pr[k][:, :], y[u][:, :], ALU.mult).then_inc(graded, 1)
                if not first(it, u, 1):
                    if not first(it, u, 3):
                        dve.wait_ge(turned_back, g - 2)
                    scan(1 - u, g - 1, first(it, u, 2))
                for k in range(3):
                    dve.wait_ge(graded, 3 * g + k + 1)
                    dve.wait_ge(upcopied, 2 * g + 1 + k % 2)
                    if not first(it, u, 1):
                        dve.wait_ge(mapped, g)
                    nc.vector.tensor_tensor(prod[k][:, :], graded_[k][:, :], un[k % 2][:, :], ALU.mult).then_inc(multiplied, 1)
            pairs(dve, step)
            dve.wait_ge(turned_back, G - 2)
            scan(1, G - 1, False)


class Names:
    pass


def build(nc, D, out):
    def dram(name, shape, dt=F32):
        return nc.dram_tensor(name, shape, dt).ap()

    D.coarse = dram("coarse", (TILES,), I32)
    D.same = dram("same", (EP,), U8)
    D.start_bias = dram("start_bias", (EP,), BF16)
    D.kvrow = dram("kvrow", (EP,), I32)
    D.degree = dram("degree", (NP,))
    D.query_rows = dram("query_rows", (EP, P))
    D.table = dram("table", (NP * RELS, 2 * P))
    D.att_sums = dram("att_sums", (EP, P + HEADS))
    D.sums = dram("sums", (EP, P))
    D.rows = dram("rows", (NP, P))
    D.utable = dram("utable", (NP, 2 * P))

    K = Names()
    with ExitStack() as stack:
        def sb(name, shape, dt=F32, st=stack):
            return st.enter_context(nc.sbuf_tensor(name, shape, dt))
        K.ident, K.negid, K.mean, K.headsum = (sb(x, [P, P]) for x in ("ident", "negid", "meanm", "headsum"))
        K.eps, K.ones, K.pid = sb("eps", [P, 1]), sb("ones", [P, 1]), sb("pid", [P, 1])
        K.end, K.start = sb("end", [P, NT], I32), sb("start", [P, NT], I32)
        K.degree, K.has = sb("degree_sb", [P, NT]), sb("has", [P, NT])
        K.x = sb("x", [P, NP])
        constants(nc, K)
        K.same = sb("same_sb", [P, EP], U8)
        graph_index(nc, K, D)
        clear_edge_rows(nc, D)
        a, b, c = (sb(x, [P, NP]) for x in ("a", "b", "c"))

        with ExitStack() as inner:
            h = sb("h", [P, NP], st=inner)
            K.ntype = sb("ntype", [P, NP], st=inner)
            load_nodes(nc, K, D, h)
            for l in range(LAYERS):
                typed_linear(nc, K, f"qkv{l}", h, [D.L0_gnn_Wq[l], D.L0_gnn_Wk[l], D.L0_gnn_Wv[l]], [a, b, c])
                to_rows(nc, K, f"qr{l}", a, dram=D.query_rows, start=K.start, limit=EP - 1)
                relation_table(nc, K, D, f"tab{l}", l, b, c)
                attention(nc, K, D, f"att{l}")
                ends(nc, K, D, f"agg{l}", a, per_head=True)
                typed_linear(nc, K, f"wa{l}", a, [D.L0_gnn_Wa[l]], [b])
                mix_with_input(nc, K, D, f"mix{l}", l, b, h, c)
                layernorm(nc, K, f"ln{l}", c, h, D.L0_gnn_ln_g[l], D.L0_gnn_ln_b[l])
            linear(nc, K, "ff", a, [(D.L0_gnn_ff_w, h)], D.L0_gnn_ff_b)
        layernorm(nc, K, "norm0", K.x, K.x, add=a)

        sum_edges(nc, K, D, "ea", linear_in=D.ea128)
        ends(nc, K, D, "eae", a)
        linear(nc, K, "emb", b, [(D.L1_gnn_We, a)], row_term=(D.L1_gnn_be, D.degree))
        linear(nc, K, "w1", a, [(D.L1_gnn_W1[0:P, :], K.x), (D.L1_gnn_W1[P:2 * P, :], b)])
        to_rows(nc, K, "yr", a, dram=D.rows)
        sum_edges(nc, K, D, "nb", table=D.rows)
        ends(nc, K, D, "nbe", b)
        add_nodes(nc, "nba", b, a, b)
        relu_bias(nc, K, "act1", b, D.L1_gnn_b1)
        linear(nc, K, "w2", a, [(D.L1_gnn_W2, b)], D.L1_gnn_b2)
        layernorm(nc, K, "norm1", K.x, K.x, add=a)

        with ExitStack() as inner:
            up = [sb(f"up{k}", [P, P], st=inner) for k in range(2)]
            down = [sb(f"down{k}", [P, P], st=inner) for k in range(3)]
            message_weights(nc, K, D, up, down)
            for k in range(2):
                linear(nc, K, f"up{k}l", a, [(up[k], K.x)])
                to_rows(nc, K, f"ur{k}", a, dram=D.utable, col=k * P)
            messages(nc, K, D, "msg", down)
        ends(nc, K, D, "mse", a)
        layernorm(nc, K, "norm2", K.x, K.x, add=a)

        K.isd = sb("isd", [P, NP])
        degree_scale(nc, K, D)
        source = K.x
        for l in range(2):
            w, bias, gain, shift = D.l3[l]
            linear(nc, K, f"gcn{l}", a, [(w, source)])
            add_nodes(nc, f"gs{l}", b, a, K.isd, ALU.mult)
            to_rows(nc, K, f"gr{l}", b, dram=D.rows)
            sum_edges(nc, K, D, f"gsum{l}", table=D.rows)
            ends(nc, K, D, f"ge{l}", a)
            batch_norm(nc, K, D, f"bn{l}", a, b, bias, gain, shift, c, relu=l == 0)
            source = c
        layernorm(nc, K, "norm3", K.x, K.x, add=c)
        store_nodes(nc, K, out)


def load_nodes(nc, K, D, h):
    with Stage(nc, "ldn") as s:
        loaded, cast = s.sem("loaded"), s.sem("cast")
        nt = s.sb("nt", [P, NP], I32)
        block = s.block()

        @block.sync
        def _(sp):
            sp.dma_start(nt[:, :], D.ntype.partition_broadcast(P)).then_inc(loaded, 16)
            sp.dma_start(K.x[:, :], D.x).then_inc(loaded, 16)
            sp.dma_start(h[:, :], D.x).then_inc(loaded, 16)
            sp.wait_ge(loaded, 48)

        @block.vector
        def _(dve):
            dve.wait_ge(loaded, 48)
            nc.vector.tensor_copy(K.ntype[:, :], nt[:, :]).then_inc(cast, 1)


def relu_bias(nc, K, tag, x, bias):
    with Stage(nc, tag) as s:
        loaded, done = s.sem("loaded"), s.sem("done")
        b = s.sb("b", [P, 1])
        block = s.block()

        @block.sync
        def _(sp):
            sp.dma_start(b[:, :], bias.rearrange("(p o) -> p o", o=1)).then_inc(loaded, 16)

        @block.vector
        def _(dve):
            dve.wait_ge(loaded, 16)
            nc.vector.tensor_scalar(x[:, :], x[:, :], b[:, 0:1], 0.0, ALU.add, ALU.max).then_inc(done, 1)


def store_nodes(nc, K, out):
    with Stage(nc, "sto") as s:
        rows = s.sb("rows", [P, NT, P])
        to_rows(nc, K, "outr", K.x, rows=rows)
        stored = s.sem("stored")
        block = s.block()
        full = N // P

        @block.sync
        def _(sp):
            sp.dma_start(out[0:full * P, :].rearrange("(t p) d -> p t d", p=P), rows[:, 0:full, :]).then_inc(stored, 16)
            sp.dma_start(out[full * P:N, :], rows[0:N - full * P, full, :]).then_inc(stored, 16)
            sp.wait_ge(stored, 32)


_WEIGHTS = ['L0_gnn_Wk', 'L0_gnn_Wq', 'L0_gnn_Wv', 'L0_gnn_Wa', 'L0_gnn_Watt', 'L0_gnn_Wmsg', 'L0_gnn_pri', 'L0_gnn_skip',
            'L0_gnn_ln_g', 'L0_gnn_ln_b', 'L0_gnn_ff_w', 'L0_gnn_ff_b', 'L1_gnn_We', 'L1_gnn_be', 'L1_gnn_W1', 'L1_gnn_b1',
            'L1_gnn_W2', 'L1_gnn_b2', 'L2_gnn_W_up_s', 'L2_gnn_W_up_v', 'L2_gnn_A1', 'L2_gnn_b1', 'L2_gnn_A2', 'L2_gnn_b2',
            'L2_gnn_A3', 'L2_gnn_W_out_s', 'L2_gnn_W_out_v', 'L3_gnn_W1', 'L3_gnn_b1', 'L3_gnn_g1', 'L3_gnn_bt1',
            'L3_gnn_W2', 'L3_gnn_b2', 'L3_gnn_g2', 'L3_gnn_bt2']


def kernel(**inputs):
    import numpy as np
    import concourse.bacc as bacc
    from concourse.bass_utils import run_bass_kernel_spmd

    def padded(a, n, fill=0):
        wide = np.full(a.shape[:-1] + (n,), fill, a.dtype)
        wide[..., :a.shape[-1]] = a
        return wide

    given = {k: np.asarray(v) for k, v in inputs.items()}
    src, dst = padded(given["src"], EP), padded(given["dst"], EP, N)
    arrays = {
        "x": padded(given["x"].T, NP), "ntype": padded(given["node_type_16"], NP),
        "dst": dst, "dst_before": np.concatenate([np.full(1, -1, dst.dtype), dst[:-1]]),
        "src_flat": src, "src4": np.ascontiguousarray(src.reshape(G, J, P).transpose(0, 2, 1)),
        "etype_flat": padded(given["edge_type_32"], EP),
        "ea128": padded(given["edge_attr_128"].T, EP), "ea4": padded(given["edge_attr_4"].T, EP),
        "ea8": padded(given["edge_attr_8"].T, EP),
    }
    arrays.update({k: given[k] for k in _WEIGHTS})
    nc = bacc.Bacc("TRN2", target_bir_lowering=False, num_devices=1)
    D = Names()
    for name, a in arrays.items():
        ap = nc.dram_tensor(f"in_{name}", a.shape, mybir.dt.from_np(a.dtype), kind="ExternalInput").ap()
        D.__dict__[name] = ap
    D.l3 = [(D.L3_gnn_W1, D.L3_gnn_b1, D.L3_gnn_g1, D.L3_gnn_bt1), (D.L3_gnn_W2, D.L3_gnn_b2, D.L3_gnn_g2, D.L3_gnn_bt2)]
    out = nc.dram_tensor("out", (N, P), F32, kind="ExternalOutput").ap()
    build(nc, D, out)
    r = run_bass_kernel_spmd(nc, [{f"in_{k}": v for k, v in arrays.items()}], core_ids=[0])
    return r.results[0]["out"]
```

```python
from contextlib import ExitStack

import concourse.bass as bass
import concourse.mybir as mybir

F32, I32, BF16, U8 = mybir.dt.float32, mybir.dt.int32, mybir.dt.bfloat16, mybir.dt.uint8
ALU = mybir.AluOpType
ACT = mybir.ActivationFunctionType
AX = mybir.AxisListType

P = 128
N, E = 3125, 50000
NT = -(-N // P)
NP = NT * P
W = 512
J = W // P
G = 98
EP = G * W
CH = 400
NC = NP // CH
TILES = EP // P
NTYPES, RELS, HEADS, HS, LAYERS = 16, 32, 8, 16, 2
BIG = 1.0e30
FAR = 1.0e6


class Stage:

    def __init__(self, nc, tag):
        self.nc, self.tag = nc, tag
        self.stack = ExitStack()
        self.sems = []

    def sb(self, name, shape, dt=F32):
        return self.stack.enter_context(self.nc.sbuf_tensor(f"{self.tag}_{name}", shape, dt))

    def ps(self, name, shape=(P, W)):
        return self.stack.enter_context(self.nc.psum_tensor(f"{self.tag}_{name}", list(shape), F32))

    def sem(self, name):
        s = self.nc.alloc_semaphore(f"{self.tag}_{name}")
        self.sems.append(s)
        return s

    def block(self):
        return self.stack.enter_context(self.nc.Block())

    def __enter__(self):
        return self

    def __exit__(self, *exc):
        self.stack.close()
        if exc[0] is None:
            self.nc.clear_and_free_semaphores(self.sems)
            self.nc.all_engine_barrier()
        return False


def groups(eng, step, tail=None):
    for g in range(6):
        step(g // 4, g % 4)
    turns = (G - 2) // 4
    with eng.Fori(1, turns if tail is None else turns - 1) as q:
        step(q, 2)
        step(q, 3)
        step(q + 1, 0)
        step(q + 1, 1)
    if tail is not None:
        for g in range(G - 4, G):
            tail(g // 4, g % 4, g == G - 1)


def first(q, k, n):
    return isinstance(q, int) and 4 * q + k < n


def linked(eng, sem):
    done = [0]

    def link(ins):
        done[0] += 1
        ins.then_inc(sem, 1)
        eng.wait_ge(sem, done[0])
    return link


def constants(nc, K):
    with Stage(nc, "cst") as s:
        made = s.sem("made")
        hid = s.sb("hid", [P, P], I32)
        pid = s.sb("pid", [P, 1], I32)
        hidf = s.sb("hidf", [P, P])
        pidf = s.sb("pidf", [P, 1])
        block = s.block()

        @block.gpsimd
        def _(pool):
            link = linked(pool, made)
            link(nc.gpsimd.memset(K.ident[:, :], 0.0))
            link(nc.gpsimd.affine_select(out=K.ident[:, :], in_=K.ident[:, :], compare_op=ALU.not_equal,
                                         fill=1.0, base=0, pattern=[[-1, P]], channel_multiplier=1))
            link(nc.gpsimd.memset(K.mean[:, :], 1.0 / P))
            link(nc.gpsimd.memset(K.eps[:, :], 1e-5))
            link(nc.gpsimd.memset(K.ones[:, :], 1.0))
            link(nc.gpsimd.iota(hid[:, :], pattern=[[1, P]], base=0, channel_multiplier=0))
            link(nc.gpsimd.iota(pid[:, :], pattern=[[0, 1]], base=0, channel_multiplier=1))

        @block.vector
        def _(dve):
            dve.wait_ge(made, 7)
            done = [7]

            def link(ins):
                done[0] += 1
                ins.then_inc(made, 1)
                dve.wait_ge(made, done[0])
            link(nc.vector.tensor_scalar(K.negid[:, :], K.ident[:, :], -1.0, None, ALU.mult))
            link(nc.vector.tensor_scalar(hid[:, :], hid[:, :], 4, None, ALU.arith_shift_right))
            link(nc.vector.tensor_copy(hidf[:, :], hid[:, :]))
            link(nc.vector.tensor_copy(K.pid[:, :], pid[:, :]))
            link(nc.vector.tensor_scalar(pid[:, :], pid[:, :], 4, None, ALU.arith_shift_right))
            link(nc.vector.tensor_copy(pidf[:, :], pid[:, :]))
            link(nc.vector.tensor_scalar(K.headsum[:, :], hidf[:, :], pidf[:, 0:1], None, ALU.is_equal))


def graph_index(nc, K, D):
    C = EP // P
    with Stage(nc, "idx") as s:
        loaded, made, coarse_in, fetched, back = (s.sem(x) for x in ("loaded", "made", "coarse", "fetched", "back"))
        fine_in = s.sem("fine_in")
        dst = s.sb("dst", [P, C], I32)
        prev = s.sb("prev", [P, C], I32)
        src = s.sb("src", [P, C], I32)
        ety = s.sb("ety", [P, C], I32)
        same = s.sb("same", [P, C])
        same8 = s.sb("same8", [P, C], U8)
        bias = s.sb("bias", [P, C], BF16)
        row = s.sb("row", [P, C], I32)
        coarse_i = s.sb("coarse_i", [P, TILES], I32)
        node_i = s.sb("node_i", [P, NT], I32)
        node = s.sb("node", [P, NT])
        cmp = s.sb("cmp", [P, NT, TILES], BF16)
        tile_f = s.sb("tile_f", [P, 2, NT])
        tile_i = s.sb("tile_i", [P, 2, NT], I32)
        fine = s.sb("fine", [P, 2, NT, P], I32)
        within = s.sb("within", [P, 2, NT])
        count = s.sb("count", [P, 2, NT])
        start = s.sb("start", [P, NT])
        tmp = s.sb("tmp", [P, NT])
        block = s.block()

        @block.sync
        def _(sp):
            sp.dma_start(dst[:, :], D.dst.rearrange("(p c) -> p c", p=P)).then_inc(loaded, 16)
            sp.dma_start(prev[:, :], D.dst_before.rearrange("(p c) -> p c", p=P)).then_inc(loaded, 16)
            sp.dma_start(src[:, :], D.src_flat.rearrange("(p c) -> p c", p=P)).then_inc(loaded, 16)
            sp.dma_start(ety[:, :], D.etype_flat.rearrange("(p c) -> p c", p=P)).then_inc(loaded, 16)
            with nc.allow_non_contiguous_dma(reason="one number of each tile"):
                sp.dma_start(D.coarse.rearrange("(t o) -> t o", o=1),
                             D.dst.rearrange("(t c) -> t c", c=P)[:, P - 1:P]).then_inc(coarse_in, 16)
            sp.wait_ge(coarse_in, 16)
            sp.dma_start(coarse_i[:, :], D.coarse.partition_broadcast(P)).then_inc(coarse_in, 16)
            sp.wait_ge(made, 6)
            sp.dma_start(D.same.rearrange("(p c) -> p c", p=P), same8[:, :]).then_inc(back, 16)
            sp.dma_start(D.start_bias.rearrange("(p c) -> p c", p=P), bias[:, :]).then_inc(back, 16)
            sp.dma_start(D.kvrow.rearrange("(p c) -> p c", p=P), row[:, :]).then_inc(back, 16)
            sp.wait_ge(back, 48)
            sp.dma_start(K.same[:, :], D.same.partition_broadcast(P)).then_inc(back, 16)
            sp.wait_ge(made, 24)
            with nc.allow_non_contiguous_dma(reason="one number of each node"):
                sp.dma_start(D.degree.rearrange("(t p) -> p t", p=P), K.degree[:, :]).then_inc(back, 16)
            sp.wait_ge(back, 80)

        @block.gpsimd
        def _(pool):
            nc.gpsimd.iota(node_i[:, :], pattern=[[P, NT]], base=0, channel_multiplier=1).then_inc(fetched, 1)
            pool.wait_ge(made, 12)
            for k in range(2):
                for t in range(NT):
                    nc.gpsimd.indirect_dma_start(
                        fine[:, k, t, :], None, D.dst.rearrange("(t c) -> t c", c=P),
                        bass.IndirectOffsetOnAxis(ap=tile_i[:, k, t:t + 1], axis=0)).then_inc(fine_in, 16)

        @block.vector
        def _(dve):
            link = linked(dve, made)
            dve.wait_ge(loaded, 64)
            link(nc.vector.tensor_tensor(same[:, :], dst[:, :], prev[:, :], ALU.is_equal))
            link(nc.vector.tensor_copy(same8[:, :], same[:, :]))
            link(nc.vector.tensor_scalar(bias[:, :], same[:, :], -1.0, BIG, ALU.add, ALU.mult))
            link(nc.vector.tensor_scalar(row[:, :], src[:, :], RELS, None, ALU.mult))
            link(nc.vector.tensor_tensor(row[:, :], row[:, :], ety[:, :], ALU.add))
            dve.wait_ge(fetched, 1)
            link(nc.vector.tensor_copy(node[:, :], node_i[:, :]))
            dve.wait_ge(coarse_in, 32)
            for k, op in enumerate((ALU.is_le, ALU.is_lt)):
                link(nc.vector.tensor_tensor(cmp[:, :, :],
                                             coarse_i[:, :].unsqueeze(1).broadcast_to([P, NT, TILES]),
                                             node[:, :].unsqueeze(2).broadcast_to([P, NT, TILES]), op))
                link(nc.vector.tensor_reduce(tile_f[:, k, :], cmp[:, :, :], AX.X, ALU.add))
            link(nc.vector.tensor_scalar(tile_f[:, :, :], tile_f[:, :, :], TILES - 1.0, None, ALU.min))
            link(nc.vector.tensor_copy(tile_i[:, :, :], tile_f[:, :, :]))
            dve.wait_ge(fine_in, 2 * NT * 16)
            for k, op in enumerate((ALU.is_le, ALU.is_lt)):
                link(nc.vector.tensor_tensor(cmp[:, :, 0:P], fine[:, k, :, :],
                                             node[:, :].unsqueeze(2).broadcast_to([P, NT, P]), op))
                link(nc.vector.tensor_reduce(within[:, k, :], cmp[:, :, 0:P], AX.X, ALU.add))
            link(nc.vector.scalar_tensor_tensor(count[:, :, :], tile_f[:, :, :], float(P), within[:, :, :], ALU.mult, ALU.add))
            link(nc.vector.tensor_tensor(K.degree[:, :], count[:, 0, :], count[:, 1, :], ALU.subtract))
            link(nc.vector.tensor_scalar(K.has[:, :], K.degree[:, :], 0.0, None, ALU.is_gt))
            link(nc.vector.tensor_scalar(tmp[:, :], count[:, 0, :], -1.0, 0.0, ALU.add, ALU.max))
            link(nc.vector.tensor_copy(K.end[:, :], tmp[:, :]))
            link(nc.vector.scalar_tensor_tensor(start[:, :], K.has[:, :], -FAR, count[:, 1, :], ALU.mult, ALU.add))
            link(nc.vector.tensor_scalar(start[:, :], start[:, :], FAR, None, ALU.add))
            link(nc.vector.tensor_copy(K.start[:, :], start[:, :]))


def clear_edge_rows(nc, D):
    per = EP // P // 8
    with Stage(nc, "clr") as s:
        zeroed, stored = s.sem("zeroed"), s.sem("stored")
        zero = s.sb("zero", [P, per * P])
        block = s.block()

        @block.vector
        def _(dve):
            nc.vector.memset(zero[:, :], 0.0).then_inc(zeroed, 1)

        @block.sync
        def _(sp):
            sp.wait_ge(zeroed, 1)
            q = D.query_rows.rearrange("(p c) d -> p (c d)", p=P)
            for k in range(8):
                sp.dma_start(q[:, k * per * P:(k + 1) * per * P], zero[:, :]).then_inc(stored, 16)
            sp.wait_ge(stored, 8 * 16)


def to_rows(nc, K, tag, x, rows=None, dram=None, width=P, col=0, start=None, limit=None):
    with Stage(nc, tag) as s:
        turned, copied, stored = s.sem("turned"), s.sem("copied"), s.sem("stored")
        rows = rows or s.sb("rows", [P, NT, P])
        bank = [s.ps(f"bank{i}") for i in range(2)]
        n = -(-NT // J)
        block = s.block()

        @block.tensor
        def _(pe):
            for k in range(n):
                if k >= 2:
                    pe.wait_ge(copied, k - 1)
                for t in range(k * J, min(NT, k * J + J)):
                    last = nc.tensor.transpose(bank[k % 2][:, (t - k * J) * P:(t - k * J + 1) * P],
                                               x[:, t * P:(t + 1) * P], K.ident[:, :])
                last.then_inc(turned, 1)

        @block.scalar
        def _(act):
            for k in range(n):
                m = min(NT, k * J + J) - k * J
                act.wait_ge(turned, k + 1)
                nc.scalar.activation(rows[:, k * J:k * J + m, :].rearrange("p t d -> p (t d)"),
                                     bank[k % 2][:, 0:m * P], ACT.Copy).then_inc(copied, 1)

        if dram is not None and start is None:
            @block.sync
            def _(sp):
                view = dram.rearrange("(t p) d -> p t d", p=P)
                for k in range(n):
                    m = min(NT, k * J + J) - k * J
                    sp.wait_ge(copied, k + 1)
                    sp.dma_start(view[:, k * J:k * J + m, col:col + P], rows[:, k * J:k * J + m, :]).then_inc(stored, 16)
                sp.wait_ge(stored, 16 * n)

        if start is not None:
            @block.gpsimd
            def _(pool):
                for t in range(NT):
                    if t % J == 0:
                        pool.wait_ge(copied, t // J + 1)
                    nc.gpsimd.indirect_dma_start(dram, bass.IndirectOffsetOnAxis(ap=start[:, t:t + 1], axis=0),
                                                 rows[:, t, :], None, bounds_check=limit,
                                                 oob_is_err=False).then_inc(stored, 16)
                pool.wait_ge(stored, 16 * NT)


def ends(nc, K, D, tag, out, per_head=False):
    src, width = (D.att_sums, P + HEADS) if per_head else (D.sums, P)
    with Stage(nc, tag) as s:
        fetched, ready, turned, copied, made = (s.sem(x) for x in ("fetched", "ready", "turned", "copied", "made"))
        rows = s.sb("rows", [P, NT, width])
        scaled = s.sb("scaled", [P, NT, P])
        inv = s.sb("inv", [P, NT, HEADS])
        bank = [s.ps(f"bank{i}") for i in range(2)]
        n = -(-NT // J)
        block = s.block()

        @block.gpsimd
        def _(pool):
            for t in range(NT):
                nc.gpsimd.indirect_dma_start(rows[:, t, :], None, src,
                                             bass.IndirectOffsetOnAxis(ap=K.end[:, t:t + 1], axis=0)).then_inc(fetched, 16)

        @block.vector
        def _(dve):
            link = linked(dve, made)
            dve.wait_ge(fetched, 16 * NT)
            if per_head:
                link(nc.vector.reciprocal(inv[:, :, :], rows[:, :, P:P + HEADS]))
                link(nc.vector.tensor_tensor(inv[:, :, :], inv[:, :, :],
                                             K.has[:, :].unsqueeze(2).broadcast_to([P, NT, HEADS]), ALU.mult))
                nc.vector.tensor_tensor(scaled[:, :, :].rearrange("p t (h c) -> p t h c", c=HS),
                                        rows[:, :, 0:P].rearrange("p t (h c) -> p t h c", c=HS),
                                        inv[:, :, :].unsqueeze(3).broadcast_to([P, NT, HEADS, HS]),
                                        ALU.mult).then_inc(ready, 1)
            else:
                nc.vector.tensor_tensor(scaled[:, :, :], rows[:, :, :],
                                        K.has[:, :].unsqueeze(2).broadcast_to([P, NT, P]), ALU.mult).then_inc(ready, 1)

        @block.tensor
        def _(pe):
            pe.wait_ge(ready, 1)
            for k in range(n):
                if k >= 2:
                    pe.wait_ge(copied, k - 1)
                for t in range(k * J, min(NT, k * J + J)):
                    last = nc.tensor.transpose(bank[k % 2][:, (t - k * J) * P:(t - k * J + 1) * P],
                                               scaled[:, t, :], K.ident[:, :])
                last.then_inc(turned, 1)

        @block.scalar
        def _(act):
            for k in range(n):
                m = min(NT, k * J + J) - k * J
                act.wait_ge(turned, k + 1)
                nc.scalar.activation(out[:, k * W:k * W + m * P], bank[k % 2][:, 0:m * P], ACT.Copy).then_inc(copied, 1)


def linear(nc, K, tag, out, terms, bias=None, func=ACT.Identity, row_term=None, prepare=None):
    with Stage(nc, tag) as s:
        loaded, summed, done = s.sem("loaded"), s.sem("summed"), s.sem("done")
        held = [i for i, (wd, _) in enumerate(terms) if not isinstance(wd, bass.AP)]
        w = [terms[i][0] if i in held else s.sb(f"w{i}", [P, P]) for i in range(len(terms))]
        b = s.sb("b", [P, 1])
        rw = s.sb("rw", [1, P])
        rx = s.sb("rx", [1, NP])
        acc = [s.ps(f"acc{i}") for i in range(2)]
        loads = 16 * (len(terms) - len(held) + (bias is not None) + 2 * (row_term is not None))
        block = s.block()

        @block.sync
        def _(sp):
            for i, (wd, _) in enumerate(terms):
                if i in held:
                    continue
                sp.dma_start(w[i][:, :], wd[:, :]).then_inc(loaded, 16)
            if bias is not None:
                sp.dma_start(b[:, :], bias.rearrange("(p o) -> p o", o=1)).then_inc(loaded, 16)
            if row_term is not None:
                sp.dma_start(rw[:, :], row_term[0].rearrange("(o p) -> o p", o=1)).then_inc(loaded, 16)
                sp.dma_start(rx[:, :], row_term[1].rearrange("(o p) -> o p", o=1)).then_inc(loaded, 16)

        @block.tensor
        def _(pe):
            if loads:
                pe.wait_ge(loaded, loads)
            for c in range(NC):
                if c >= 2:
                    pe.wait_ge(done, c - 1)
                for i, (_, x) in enumerate(terms):
                    last = nc.tensor.matmul(acc[c % 2][:, 0:CH], w[i][:, :], x[:, c * CH:(c + 1) * CH], start=i == 0,
                                            stop=i == len(terms) - 1 and row_term is None)
                if row_term is not None:
                    last = nc.tensor.matmul(acc[c % 2][:, 0:CH], rw[:, :], rx[:, c * CH:(c + 1) * CH], start=False, stop=True)
                last.then_inc(summed, 1)

        @block.scalar
        def _(act):
            if bias is not None:
                act.wait_ge(loaded, loads)
            for c in range(NC):
                act.wait_ge(summed, c + 1)
                nc.scalar.activation(out[:, c * CH:(c + 1) * CH], acc[c % 2][:, 0:CH], func,
                                     bias=b[:, 0:1] if bias is not None else 0.0).then_inc(done, 1)


def layernorm(nc, K, tag, x, out, gain=None, shift=None, add=None, mix=None):
    with Stage(nc, tag) as s:
        loaded, added, meaned, centred, squared, varied, rooted, inverted, scaled = (
            s.sem(x) for x in ("loaded", "added", "meaned", "centred", "squared", "varied", "rooted", "inverted", "scaled"))
        gb = s.sb("gb", [P, 2])
        sm = s.sb("sm", [P, 2, CH])
        xc = s.sb("xc", [P, 2, CH])
        sq = s.sb("sq", [P, 2, CH])
        sd = s.sb("sd", [P, 2, CH])
        inv = s.sb("inv", [P, 2, CH])
        nrm = s.sb("nrm", [P, 2, CH])
        mean = [s.ps(f"mean{i}") for i in range(2)]
        var = [s.ps(f"var{i}") for i in range(2)]
        affine = gain is not None
        block = s.block()

        def part(c):
            return slice(c * CH, (c + 1) * CH)

        @block.sync
        def _(sp):
            if affine:
                sp.dma_start(gb[:, 0:1], gain.rearrange("(p o) -> p o", o=1)).then_inc(loaded, 16)
                sp.dma_start(gb[:, 1:2], shift.rearrange("(p o) -> p o", o=1)).then_inc(loaded, 16)

        @block.tensor
        def _(pe):
            for c in range(NC + 1):
                if c < NC:
                    pe.wait_ge(added, c + 1)
                    if c >= 2:
                        pe.wait_ge(centred, c - 1)
                    nc.tensor.matmul(mean[c % 2][:, 0:CH], K.mean[:, :], sm[:, c % 2, :], start=True, stop=True).then_inc(meaned, 1)
                if c >= 1:
                    pe.wait_ge(squared, c)
                    if c >= 3:
                        pe.wait_ge(rooted, c - 2)
                    nc.tensor.matmul(var[(c - 1) % 2][:, 0:CH], K.mean[:, :], sq[:, (c - 1) % 2, :], start=True, stop=True).then_inc(varied, 1)

        @block.scalar
        def _(act):
            if affine:
                act.wait_ge(loaded, 32)
            for c in range(NC + 1):
                if c < NC:
                    act.wait_ge(centred, c + 1)
                    if c >= 2:
                        act.wait_ge(varied, c - 1)
                    nc.scalar.activation(sq[:, c % 2, :], xc[:, c % 2, :], ACT.Square).then_inc(squared, 1)
                if c >= 1:
                    d = c - 1
                    act.wait_ge(varied, c)
                    if d >= 2:
                        act.wait_ge(inverted, d - 1)
                    nc.scalar.activation(sd[:, d % 2, :], var[d % 2][:, 0:CH], ACT.Sqrt, bias=K.eps[:, 0:1]).then_inc(rooted, 1)

        @block.vector
        def _(dve):
            for c in range(NC + 2):
                if c < NC:
                    if c >= 2:
                        dve.wait_ge(meaned, c - 1)
                        dve.wait_ge(centred, c - 1)
                    if add is not None:
                        nc.vector.tensor_tensor(sm[:, c % 2, :], x[:, part(c)], add[:, part(c)], ALU.add).then_inc(added, 1)
                    else:
                        nc.vector.tensor_copy(sm[:, c % 2, :], x[:, part(c)]).then_inc(added, 1)
                    dve.wait_ge(meaned, c + 1)
                    dve.wait_ge(added, c + 1)
                    if c >= 2:
                        dve.wait_ge(squared, c - 1)
                        dve.wait_ge(scaled, c - 1)
                    nc.vector.tensor_tensor(xc[:, c % 2, :], sm[:, c % 2, :], mean[c % 2][:, 0:CH], ALU.subtract).then_inc(centred, 1)
                if 1 <= c <= NC:
                    d = c - 1
                    dve.wait_ge(rooted, c)
                    if d >= 2:
                        dve.wait_ge(scaled, d - 1)
                    nc.vector.reciprocal(inv[:, d % 2, :], sd[:, d % 2, :]).then_inc(inverted, 1)
                    dve.wait_ge(inverted, c)
                    dve.wait_ge(centred, c)
                    dst = nrm[:, d % 2, :] if affine else out[:, part(d)]
                    nc.vector.tensor_tensor(dst, xc[:, d % 2, :], inv[:, d % 2, :], ALU.mult).then_inc(scaled, 1)
                    if affine:
                        if d == 0:
                            dve.wait_ge(loaded, 32)
                        dve.wait_ge(scaled, c)
                        nc.vector.tensor_scalar(out[:, part(d)], nrm[:, d % 2, :], gb[:, 0:1], gb[:, 1:2], ALU.mult, ALU.add).then_inc(loaded, 1)
            if affine:
                dve.wait_ge(loaded, 32 + NC)


def typed_linear(nc, K, tag, x, weights, outs):
    M = len(weights)
    with Stage(nc, tag) as s:
        loaded, masked, used, summed, copied = (s.sem(x) for x in ("loaded", "masked", "used", "summed", "copied"))
        w = s.sb("w", [P, M, NTYPES, P])
        xm = s.sb("xm", [P, 4, CH])
        acc = [s.ps(f"acc{m}") for m in range(M)]
        block = s.block()

        @block.sync
        def _(sp):
            for m in range(M):
                sp.dma_start(w[:, m, :, :], weights[m].rearrange("t d o -> d t o")).then_inc(loaded, 16)

        @block.vector
        def _(dve):
            def chunk(c):
                for t in range(NTYPES):
                    if not (isinstance(c, int) and t < 4):
                        dve.wait_ge(used, c * NTYPES + t - 3)
                    nc.vector.scalar_tensor_tensor(xm[:, t % 4, :], K.ntype[:, bass.ds(c * CH, CH)], float(t),
                                                   x[:, bass.ds(c * CH, CH)], ALU.is_equal, ALU.mult).then_inc(masked, 1)
            chunk(0)
            with dve.Fori(1, NC) as c:
                chunk(c)

        @block.tensor
        def _(pe):
            pe.wait_ge(loaded, 16 * M)

            def chunk(c):
                if not isinstance(c, int):
                    pe.wait_ge(copied, c * M)
                for t in range(NTYPES):
                    pe.wait_ge(masked, c * NTYPES + t + 1)
                    for m in range(M):
                        last = nc.tensor.matmul(acc[m][:, 0:CH], w[:, m, t, :], xm[:, t % 4, :], start=t == 0, stop=t == NTYPES - 1)
                    last.then_inc(used, 1)
            chunk(0)
            with pe.Fori(1, NC) as c:
                chunk(c)

        @block.scalar
        def _(act):
            with act.Fori(0, NC) as c:
                act.wait_ge(used, (c + 1) * NTYPES)
                for m in range(M):
                    nc.scalar.activation(outs[m][:, bass.ds(c * CH, CH)], acc[m][:, 0:CH], ACT.Copy).then_inc(copied, 1)


def sum_edges(nc, K, D, tag, table=None, linear_in=None, radial=False):
    with Stage(nc, tag) as s:
        idx_in = [s.sem(f"idx_in{k}") for k in range(4)]
        msg_in = [s.sem(f"msg_in{k}") for k in range(4)]
        stored = [s.sem(f"stored{k}") for k in range(4)]
        began, turned, scanned, turned_back, copied = (s.sem(x) for x in ("began", "turned", "scanned", "turned_back", "copied"))
        idx = [s.sb(f"idx{k}", [P, J], I32) for k in range(4)]
        rows = [s.sb(f"rows{k}", [P, W]) for k in range(4)]
        run = [s.sb(f"run{u}", [P, W]) for u in range(2)]
        out = [s.sb(f"out{k}", [P, J, P]) for k in range(4)]
        msg = [s.ps(f"msg{u}") for u in range(2)]
        back = [s.ps(f"back{u}") for u in range(2)]
        if radial:
            loaded, zeroed, hid1, lit1, hid2, lit2 = (s.sem(x) for x in ("loaded", "zeroed", "hid1", "lit1", "hid2", "lit2"))
            feat_in = [s.sem(f"feat_in{k}") for k in range(4)]
            hid_out = [s.sem(f"hid_out{k}") for k in range(4)]
            a1 = s.sb("a1", [8, 64])
            a2 = s.sb("a2", [64, P])
            bb = s.sb("bb", [64, 2])
            feat = [s.sb(f"feat{k}", [8, W]) for k in range(4)]
            h1 = [s.sb(f"h1{u}", [64, W]) for u in range(2)]
            h2 = [s.sb(f"h2{k}", [64, W]) for k in range(4)]
            ph1, ph2 = s.ps("ph1"), s.ps("ph2")
        sums = D.sums.rearrange("(g j p) d -> g p j d", j=J, p=P)
        block = s.block()

        def store(sp, k, g):
            sp.wait_ge(copied, g + 1)
            sp.dma_start(sums[bass.ds(g, 1), :, :, :].rearrange("g p j d -> (g p) j d"), out[k][:, :, :]).then_inc(stored[k], 16)

        def store_hidden(sp, k, g):
            sp.wait_ge(lit2, g + 1)
            sp.dma_start(D.hidden[:, bass.ds(g * W, W)], h2[k][:, :]).then_inc(hid_out[k], 16)

        @block.sync
        def _(sp):
            if radial:
                sp.dma_start(a1[:, :], D.L2_gnn_A1).then_inc(loaded, 16)
                sp.dma_start(a2[:, 0:64], D.L2_gnn_A2).then_inc(loaded, 16)
                sp.dma_start(bb[:, 0:1], D.L2_gnn_b1.rearrange("(p o) -> p o", o=1)).then_inc(loaded, 16)
                sp.dma_start(bb[:, 1:2], D.L2_gnn_b2.rearrange("(p o) -> p o", o=1)).then_inc(loaded, 16)

            def step(q, k):
                g = q * 4 + k
                if table is not None:
                    if not first(q, k, 4):
                        sp.wait_ge(msg_in[k], q * 64)
                    sp.dma_start(idx[k][:, :], D.src4[bass.ds(g, 1), :, :].rearrange("g p j -> (g p) j")).then_inc(idx_in[k], 16)
                else:
                    if not first(q, k, 4):
                        sp.wait_ge(scanned, g - 3)
                    sp.dma_start(rows[k][:, :], linear_in[:, bass.ds(g * W, W)]).then_inc(msg_in[k], 16)
                if radial:
                    if not first(q, k, 4):
                        sp.wait_ge(hid1, g - 3)
                    sp.dma_start(feat[k][:, :], D.ea8[:, bass.ds(g * W, W)]).then_inc(feat_in[k], 16)
                if not first(q, k, 3):
                    store(sp, (k + 1) % 4, g - 3)
                    if radial:
                        store_hidden(sp, (k + 1) % 4, g - 3)
            groups(sp, step)
            for g in range(G - 3, G):
                store(sp, g % 4, g)
                if radial:
                    store_hidden(sp, g % 4, g)
            if radial:
                for k in range(4):
                    sp.wait_ge(hid_out[k], 16 * len(range(k, G, 4)))
            for k in range(4):
                sp.wait_ge(stored[k], 16 * len(range(k, G, 4)))

        if table is not None:
            @block.gpsimd
            def _(pool):
                def step(q, k):
                    g = q * 4 + k
                    pool.wait_ge(idx_in[k], q * 16 + 16)
                    if not first(q, k, 4):
                        pool.wait_ge(turned, g - 3)
                    pool.sem_inc(began, 1)
                    for j in range(J):
                        nc.gpsimd.indirect_dma_start(rows[k][:, j * P:(j + 1) * P], None, table,
                                                     bass.IndirectOffsetOnAxis(ap=idx[k][:, j:j + 1], axis=0)).then_inc(msg_in[k], 16)
                groups(pool, step)

        @block.tensor
        def _(pe):
            def step(q, k):
                g = q * 4 + k
                u = k % 2
                if table is not None:
                    pe.wait_ge(msg_in[k], q * 64 + 64)
                    if not first(q, k, 2):
                        pe.wait_ge(scanned, g - 1)
                    for j in range(J):
                        last = nc.tensor.transpose(msg[u][:, j * P:(j + 1) * P], rows[k][:, j * P:(j + 1) * P], K.ident[:, :])
                    last.then_inc(turned, 1)
                if not first(q, k, 1):
                    turn_back(g - 1, 1 - u, first(q, k, 3))
                if radial:
                    pe.wait_ge(feat_in[k], q * 16 + 16)
                    if not first(q, k, 1):
                        pe.wait_ge(lit1, g)
                    nc.tensor.matmul(ph1[0:64, :], a1[:, :], feat[k][:, :], start=True, stop=True).then_inc(hid1, 1)
                    if not first(q, k, 1):
                        second_layer(g - 1, 1 - u, first(q, k, 2))

            def second_layer(h, v, early):
                pe.wait_ge(lit1, h + 1)
                if not early:
                    pe.wait_ge(lit2, h)
                nc.tensor.matmul(ph2[:, :], a2[:, :], h1[v][:, :], start=True, stop=True).then_inc(hid2, 1)

            def turn_back(h, v, early):
                pe.wait_ge(scanned, h + 1)
                if not early:
                    pe.wait_ge(copied, h - 1)
                for j in range(J):
                    last = nc.tensor.transpose(back[v][:, j * P:(j + 1) * P], run[v][:, j * P:(j + 1) * P], K.ident[:, :])
                last.then_inc(turned_back, 1)
            if radial:
                pe.wait_ge(loaded, 64)
                pe.wait_ge(zeroed, 1)
            groups(pe, step)
            turn_back(G - 1, 1, False)
            if radial:
                second_layer(G - 1, 1, False)

        @block.vector
        def _(dve):
            if radial:
                nc.vector.memset(a2[:, 64:P], 0.0).then_inc(zeroed, 1)

            def step(q, k):
                g = q * 4 + k
                u = k % 2
                if table is not None:
                    dve.wait_ge(turned, g + 1)
                    data = msg[u]
                else:
                    dve.wait_ge(msg_in[k], q * 16 + 16)
                    data = rows[k]
                if not first(q, k, 2):
                    dve.wait_ge(turned_back, g - 1)
                if not first(q, k, 1):
                    dve.wait_ge(scanned, g)
                nc.vector.tensor_tensor_scan(run[u][:, :], K.same[:, bass.ds(g * W, W)], data[:, :],
                                             0.0 if first(q, k, 1) else run[1 - u][:, W - 1:W],
                                             ALU.mult, ALU.add).then_inc(scanned, 1)
            groups(dve, step)

        @block.scalar
        def _(act):
            def step(q, k):
                g = q * 4 + k
                act.wait_ge(turned_back, g + 1)
                if not first(q, k, 4):
                    act.wait_ge(stored[k], q * 16)
                nc.scalar.activation(out[k][:, :, :].rearrange("p j d -> p (j d)"), back[k % 2][:, :], ACT.Copy).then_inc(copied, 1)

            def first_lit(q, k):
                g = q * 4 + k
                act.wait_ge(hid1, g + 1)
                if not first(q, k, 2):
                    act.wait_ge(hid2, g - 1)
                nc.scalar.activation(h1[k % 2][:, :], ph1[0:64, :], ACT.Silu, bias=bb[:, 0:1]).then_inc(lit1, 1)

            def second_lit(k, h, uses):
                act.wait_ge(hid2, h + 1)
                if not (isinstance(uses, int) and uses == 0):
                    act.wait_ge(hid_out[k], uses * 16)
                nc.scalar.activation(h2[k][:, :], ph2[0:64, :], ACT.Silu, bias=bb[:, 1:2]).then_inc(lit2, 1)

            def step_radial(q, k):
                first_lit(q, k)
                if not first(q, k, 1):
                    second_lit((k + 3) % 4, q * 4 + k - 1, q if k >= 1 else q - 1)
                step_out(q, k)

            def step_out(q, k):
                if not first(q, k, 1):
                    step(q if k >= 1 else q - 1, (k + 3) % 4)
            if radial:
                act.wait_ge(loaded, 64)
                groups(act, step_radial)
                second_lit((G - 1) % 4, G - 1, (G - 1) // 4)
                step((G - 1) // 4, (G - 1) % 4)
            else:
                groups(act, step)


def relation_table(nc, K, D, tag, layer, key, value):
    Q = 4
    with Stage(nc, tag) as s:
        loaded, zeroed, put, ready, product, evac_k, evac_v = (
            s.sem(x) for x in ("loaded", "zeroed", "put", "ready", "product", "evac_k", "evac_v"))
        node_in = s.sem("node_in")
        stored = [s.sem(f"stored{q}") for q in range(Q)]
        wk = s.sb("wk", [P, RELS, P])
        wv = s.sb("wv", [P, RELS, P])
        pri = s.sb("pri", [P, RELS])
        kv = s.sb("kv", [P, 2, P])
        part = [s.sb(f"part{q}", [P, RELS // Q, 2 * P]) for q in range(Q)]
        bank = [s.ps(f"bank{i}") for i in range(8)]
        table = D.table.rearrange("(t p r) d -> t p r d", p=P, r=RELS)
        block = s.block()

        @block.gpsimd
        def _(pool):
            nc.gpsimd.memset(wk[:, :, :], 0.0).then_inc(zeroed, 1)
            nc.gpsimd.memset(wv[:, :, :], 0.0).then_inc(zeroed, 1)

        @block.sync
        def _(sp):
            for h in range(HEADS):
                sp.dma_start(pri[h * HS:(h + 1) * HS, :], D.L0_gnn_pri[layer, h, :].partition_broadcast(HS)).then_inc(loaded, 16)
            sp.wait_ge(zeroed, 2)
            for h in range(HEADS):
                f = slice(h * HS, (h + 1) * HS)
                sp.dma_start(wk[f, :, f], D.L0_gnn_Watt[layer, h, :, :, :].rearrange("t d o -> d t o")).then_inc(put, 16)
                sp.dma_start(wv[f, :, f], D.L0_gnn_Wmsg[layer, h, :, :, :].rearrange("t d o -> d t o")).then_inc(put, 16)

            def tile(t):
                for q in range(Q):
                    sp.wait_ge(evac_k, t * 8 + 2 * q + 2)
                    sp.wait_ge(evac_v, t * 8 + 2 * q + 2)
                    sp.dma_start(table[bass.ds(t, 1), :, q * 8:q * 8 + 8, :].rearrange("t p r d -> (t p) r d"),
                                 part[q][:, :, :]).then_inc(stored[q], 16)
            with sp.Fori(0, NT) as t:
                tile(t)
            for q in range(Q):
                sp.wait_ge(stored[q], 16 * NT)

        @block.vector
        def _(dve):
            dve.wait_ge(loaded, 16 * HEADS)
            dve.wait_ge(put, 32 * HEADS)
            nc.vector.scalar_tensor_tensor(wk[:, :, :], wk[:, :, :], float(HS) ** -0.5,
                                           pri[:, :].unsqueeze(2).broadcast_to([P, RELS, P]), ALU.mult, ALU.mult).then_inc(ready, 1)

            def tile(t):
                for c in range(8):
                    dve.wait_ge(product, t * 16 + 2 * c + 1)
                    if not isinstance(t, int):
                        dve.wait_ge(stored[c // 2], t * 16)
                    nc.vector.tensor_copy(part[c // 2][:, (c % 2) * 4:(c % 2) * 4 + 4, 0:P],
                                          bank[(2 * c) % 8][:, :].rearrange("p (r d) -> p r d", d=P)).then_inc(evac_k, 1)
            tile(0)
            with dve.Fori(1, NT) as t:
                tile(t)

        @block.scalar
        def _(act):
            def tile(t):
                if not isinstance(t, int):
                    act.wait_ge(product, t * 16)
                nc.scalar.activation(kv[:, 0, :], key[:, bass.ds(t * P, P)], ACT.Copy).then_inc(node_in, 1)
                nc.scalar.activation(kv[:, 1, :], value[:, bass.ds(t * P, P)], ACT.Copy).then_inc(node_in, 1)
                for c in range(8):
                    act.wait_ge(product, t * 16 + 2 * c + 2)
                    if not isinstance(t, int):
                        act.wait_ge(stored[c // 2], t * 16)
                    nc.scalar.activation(part[c // 2][:, (c % 2) * 4:(c % 2) * 4 + 4, P:2 * P],
                                         bank[(2 * c + 1) % 8][:, :].rearrange("p (r d) -> p r d", d=P), ACT.Copy).then_inc(evac_v, 1)
            tile(0)
            with act.Fori(1, NT) as t:
                tile(t)

        @block.tensor
        def _(pe):
            pe.wait_ge(ready, 1)

            def tile(t):
                pe.wait_ge(node_in, t * 2 + 2)
                for c in range(8):
                    for k, (w, evac) in enumerate(((wk, evac_k), (wv, evac_v))):
                        if not (isinstance(t, int) and c < 4):
                            pe.wait_ge(evac, t * 8 + c - 3)
                        nc.tensor.matmul(bank[(2 * c + k) % 8][:, :], kv[:, k, :],
                                         w[:, c * 4:c * 4 + 4, :].rearrange("p r d -> p (r d)"), start=True, stop=True).then_inc(product, 1)
            tile(0)
            with pe.Fori(1, NT) as t:
                tile(t)


def attention(nc, K, D, tag):
    V = P + HEADS
    with Stage(nc, tag) as s:
        idx_in, rows_in, query_in, bias_in, stored = ([s.sem(f"{x}{k}") for k in range(4)] for x in
                                                      ("idx_in", "rows_in", "query_in", "bias_in", "stored"))
        q_turned, k_turned, v_turned, v_copied, spread, multiplied, shifted, largest, difference, relued, weighted = (
            s.sem(x) for x in ("q_turned", "k_turned", "v_turned", "v_copied", "spread", "multiplied", "shifted",
                               "largest", "difference", "relued", "weighted"))
        began = s.sem("began")
        before, messaged, summed, turned_back, copied = (s.sem(x) for x in ("before", "messaged", "summed", "turned_back", "copied"))
        idx = [s.sb(f"idx{k}", [P, J], I32) for k in range(4)]
        rows = [s.sb(f"rows{k}", [P, J, 2 * P]) for k in range(4)]
        query = [s.sb(f"query{k}", [P, J, P]) for k in range(4)]
        bias = [s.sb(f"bias{k}", [P, W], BF16) for k in range(4)]
        qx = [s.sb(f"qx{u}", [P, W]) for u in range(2)]
        prod = [s.sb(f"prod{u}", [P, W + 1]) for u in range(2)]
        b = [s.sb(f"b{u}", [P, W]) for u in range(2)]
        up = s.sb("up", [P, W])
        down = s.sb("down", [P, W])
        decay = [s.sb(f"decay{u}", [P, W]) for u in range(2)]
        weight = [s.sb(f"weight{u}", [P, W]) for u in range(2)]
        value = [s.sb(f"value{u}", [P, W]) for u in range(2)]
        message = s.sb("message", [P, W])
        run = [s.sb(f"run{u}", [P, W]) for u in range(2)]
        den = [s.sb(f"den{u}", [P, W]) for u in range(2)]
        out = [s.sb(f"out{k}", [P, J, V]) for k in range(4)]
        pq, pk, pv, pshift, pback, pden = (s.ps(x) for x in ("pq", "pk", "pv", "pshift", "pback", "pden"))
        pdiff = [s.ps(f"pdiff{u}") for u in range(2)]
        rows_d = D.query_rows.rearrange("(g j p) d -> g p j d", j=J, p=P)
        sums = D.att_sums.rearrange("(g j p) d -> g p j d", j=J, p=P)
        kvrow = D.kvrow.rearrange("(g j p) -> g p j", j=J, p=P)
        block = s.block()

        @block.sync
        def _(sp):
            def store(k, g):
                sp.wait_ge(copied, 2 * (g + 1))
                sp.dma_start(sums[bass.ds(g, 1), :, :, :].rearrange("g p j d -> (g p) j d"), out[k][:, :, :]).then_inc(stored[k], 16)

            def step(q, k):
                g = q * 4 + k
                at = sp.snap(g * W) if not isinstance(g, int) else g * W
                if not first(q, k, 4):
                    sp.wait_ge(rows_in[k], q * 64)
                with nc.allow_non_contiguous_dma(reason="one index per partition and tile"):
                    sp.dma_start(idx[k][:, :], kvrow[bass.ds(g, 1), :, :].rearrange("g p j -> (g p) j")).then_inc(idx_in[k], 16)
                if not first(q, k, 4):
                    sp.wait_ge(q_turned, g - 3)
                    sp.wait_ge(largest, g - 3)
                sp.dma_start(query[k][:, :, :], rows_d[bass.ds(g, 1), :, :, :].rearrange("g p j d -> (g p) j d")).then_inc(query_in[k], 16)
                sp.dma_start(bias[k][:, :], D.start_bias[bass.ds(at, W)].partition_broadcast(P)).then_inc(bias_in[k], 16)
                if not first(q, k, 5):
                    store((k + 3) % 4, g - 5)
            groups(sp, step)
            for g in range(G - 5, G):
                store(g % 4, g)
            for k in range(4):
                sp.wait_ge(stored[k], 16 * len(range(k, G, 4)))

        @block.gpsimd
        def _(pool):
            def step(q, k):
                g = q * 4 + k
                pool.wait_ge(idx_in[k], q * 16 + 16)
                if not first(q, k, 4):
                    pool.wait_ge(v_turned, g - 3)
                pool.sem_inc(began, 1)
                for j in range(J):
                    nc.gpsimd.indirect_dma_start(rows[k][:, j, :], None, D.table,
                                                 bass.IndirectOffsetOnAxis(ap=idx[k][:, j:j + 1], axis=0)).then_inc(rows_in[k], 16)
            groups(pool, step)

        @block.tensor
        def _(pe):
            def turn_pair(q, k):
                g = q * 4 + k
                pe.wait_ge(query_in[k], q * 16 + 16)
                if not first(q, k, 1):
                    pe.wait_ge(spread, g)
                for j in range(J):
                    last = nc.tensor.transpose(pq[:, j * P:(j + 1) * P], query[k][:, j, :], K.ident[:, :])
                last.then_inc(q_turned, 1)
                pe.wait_ge(rows_in[k], q * 64 + 64)
                if not first(q, k, 1):
                    pe.wait_ge(multiplied, g)
                for j in range(J):
                    last = nc.tensor.transpose(pk[:, j * P:(j + 1) * P], rows[k][:, j, 0:P], K.ident[:, :])
                last.then_inc(k_turned, 1)

            def turn_value(q, k):
                if not first(q, k, 1):
                    pe.wait_ge(v_copied, q * 4 + k)
                for j in range(J):
                    last = nc.tensor.transpose(pv[:, j * P:(j + 1) * P], rows[k][:, j, P:2 * P], K.ident[:, :])
                last.then_inc(v_turned, 1)

            def turn_back(u, h, early):
                pe.wait_ge(summed, 2 * (h + 1))
                if not early:
                    pe.wait_ge(copied, 2 * h)
                for j in range(J):
                    nc.tensor.transpose(pback[:, j * P:(j + 1) * P], run[u][:, j * P:(j + 1) * P], K.ident[:, :])
                for j in range(J):
                    last = nc.tensor.transpose(pden[:, j * P:(j + 1) * P], den[u][:, j * P:(j + 1) * P], K.ident[:, :])
                last.then_inc(turned_back, 1)

            def step(q, k, last_group=False):
                g = q * 4 + k
                u = k % 2
                pe.wait_ge(multiplied, g + 1)
                if not first(q, k, 1):
                    pe.wait_ge(largest, g)
                nc.tensor.matmul(pshift[:, :], K.headsum[:, :], prod[u][:, 0:W], start=True, stop=True).then_inc(shifted, 1)
                if not last_group:
                    turn_pair(q + k // 3, (k + 1) % 4)
                if not first(q, k, 2):
                    turn_back(u, g - 2, first(q, k, 3))
                if not first(q, k, 2):
                    pe.wait_ge(relued, 2 * (g - 1))
                nc.tensor.matmul(pdiff[u][:, :], K.headsum[:, :], prod[u][:, 1:W + 1], start=True, stop=False)
                pe.wait_ge(largest, g + 1)
                nc.tensor.matmul(pdiff[u][:, :], K.negid[:, :], b[u][:, :], start=False, stop=True).then_inc(difference, 1)
                if not last_group:
                    turn_value(q + k // 3, (k + 1) % 4)
            turn_pair(0, 0)
            turn_value(0, 0)
            groups(pe, step, tail=step)
            turn_back(0, G - 2, False)
            turn_back(1, G - 1, False)

        @block.vector
        def _(dve):
            def accumulate(u, h, early1, early2):
                dve.wait_ge(weighted, 2 * (h + 1))
                dve.wait_ge(v_copied, h + 1)
                if not early1:
                    dve.wait_ge(summed, 2 * h)
                nc.vector.tensor_tensor(message[:, :], value[u][:, :], weight[u][:, :], ALU.mult).then_inc(messaged, 1)
                dve.wait_ge(messaged, h + 1)
                if not early2:
                    dve.wait_ge(turned_back, h - 1)
                nc.vector.tensor_tensor_scan(run[u][:, :], decay[u][:, :], message[:, :],
                                             0.0 if early1 else run[1 - u][:, W - 1:W], ALU.mult, ALU.add).then_inc(summed, 1)
                nc.vector.tensor_tensor_scan(den[u][:, :], decay[u][:, :], weight[u][:, :],
                                             0.0 if early1 else den[1 - u][:, W - 1:W], ALU.mult, ALU.add).then_inc(summed, 1)

            def step(q, k):
                g = q * 4 + k
                u = k % 2
                dve.wait_ge(q_turned, g + 1)
                if not first(q, k, 2):
                    dve.wait_ge(multiplied, g - 1)
                if not first(q, k, 1):
                    dve.wait_ge(spread, g)
                nc.vector.tensor_tensor_scan(qx[u][:, :], K.same[:, bass.ds(g * W, W)], pq[:, :],
                                             0.0 if first(q, k, 1) else qx[1 - u][:, W - 1:W],
                                             ALU.mult, ALU.add).then_inc(spread, 1)
                if not first(q, k, 2):
                    dve.wait_ge(difference, g - 1)
                if first(q, k, 1):
                    nc.vector.memset(prod[u][:, 0:1], 0.0).then_inc(before, 1)
                else:
                    dve.wait_ge(multiplied, g)
                    nc.vector.tensor_copy(prod[u][:, 0:1], prod[1 - u][:, W:W + 1]).then_inc(before, 1)
                dve.wait_ge(k_turned, g + 1)
                dve.wait_ge(spread, g + 1)
                dve.wait_ge(before, g + 1)
                nc.vector.tensor_tensor(prod[u][:, 1:W + 1], qx[u][:, :], pk[:, :], ALU.mult).then_inc(multiplied, 1)
                if not first(q, k, 2):
                    accumulate(u, g - 2, first(q, k, 3), first(q, k, 4))
                dve.wait_ge(shifted, g + 1)
                if not first(q, k, 1):
                    dve.wait_ge(largest, g)
                dve.wait_ge(bias_in[k], q * 16 + 16)
                nc.vector.tensor_tensor_scan(b[u][:, :], pshift[:, :], bias[k][:, :],
                                             0.0 if first(q, k, 1) else b[1 - u][:, W - 1:W],
                                             ALU.max, ALU.add).then_inc(largest, 1)
            groups(dve, step)
            accumulate(0, G - 2, False, False)
            accumulate(1, G - 1, False, False)

        @block.scalar
        def _(act):
            def copy_out(k, h, uses):
                act.wait_ge(turned_back, h + 1)
                if not (isinstance(uses, int) and uses == 0):
                    act.wait_ge(stored[k], uses * 16)
                nc.scalar.activation(out[k][:, :, 0:P], pback[:, :].rearrange("p (j d) -> p j d", j=J), ACT.Copy).then_inc(copied, 1)
                nc.scalar.activation(out[k][:, :, P:V], pden[:, 0:J * P:HS].rearrange("p (j d) -> p j d", j=J), ACT.Copy).then_inc(copied, 1)

            def step(q, k):
                g = q * 4 + k
                u = k % 2
                act.wait_ge(v_turned, g + 1)
                if not first(q, k, 2):
                    act.wait_ge(messaged, g - 1)
                nc.scalar.activation(value[u][:, :], pv[:, :], ACT.Copy).then_inc(v_copied, 1)
                act.wait_ge(difference, g + 1)
                if not first(q, k, 1):
                    act.wait_ge(weighted, 2 * g)
                nc.scalar.activation(up[:, :], pdiff[u][:, :], ACT.Relu).then_inc(relued, 1)
                nc.scalar.activation(down[:, :], pdiff[u][:, :], ACT.Relu, scale=-1.0).then_inc(relued, 1)
                if not first(q, k, 2):
                    act.wait_ge(summed, 2 * (g - 1))
                act.wait_ge(relued, 2 * g + 1)
                nc.scalar.activation(decay[u][:, :], up[:, :], ACT.Exp, scale=-1.0).then_inc(weighted, 1)
                act.wait_ge(relued, 2 * g + 2)
                nc.scalar.activation(weight[u][:, :], down[:, :], ACT.Exp, scale=-1.0).then_inc(weighted, 1)
                if not first(q, k, 2):
                    copy_out((k + 2) % 4, g - 2, q if k >= 2 else q - 1)
            groups(act, step)
            for g in range(G - 2, G):
                copy_out(g % 4, g, g // 4)


def mix_with_input(nc, K, D, tag, layer, new, old, out):
    with Stage(nc, tag) as s:
        loaded, gated, hot, spread_, lit, done, mixed = (
            s.sem(x) for x in ("loaded", "gated", "hot", "spread", "lit", "done", "mixed"))
        skip = s.sb("skip", [NTYPES, 1])
        gate = s.sb("gate", [NTYPES, 1])
        gates = s.sb("gates", [NTYPES, P])
        onehot = s.sb("onehot", [NTYPES, NP])
        lifted = s.sb("lifted", [P, 2, CH])
        diff = s.sb("diff", [P, 2, CH])
        alpha = [s.ps(f"alpha{i}") for i in range(2)]
        block = s.block()

        @block.sync
        def _(sp):
            sp.dma_start(skip[:, :], D.L0_gnn_skip[layer, :].rearrange("(p o) -> p o", o=1)).then_inc(loaded, 16)

        @block.tensor
        def _(pe):
            pe.wait_ge(hot, 2)
            for c in range(NC):
                if c >= 2:
                    pe.wait_ge(mixed, 2 * (c - 1))
                nc.tensor.matmul(alpha[c % 2][:, 0:CH], gates[:, :], onehot[:, c * CH:(c + 1) * CH], start=True, stop=True).then_inc(spread_, 1)

        @block.scalar
        def _(act):
            act.wait_ge(loaded, 16)
            nc.scalar.activation(gate[:, :], skip[:, :], ACT.Sigmoid).then_inc(gated, 1)
            for c in range(NC):
                if c >= 2:
                    act.wait_ge(mixed, 2 * (c - 1))
                nc.scalar.activation(lifted[:, c % 2, :], new[:, c * CH:(c + 1) * CH], ACT.Silu).then_inc(lit, 1)

        @block.vector
        def _(dve):
            dve.wait_ge(gated, 1)
            nc.vector.tensor_copy(gates[:, :], gate[:, :].broadcast_to([NTYPES, P])).then_inc(hot, 1)
            nc.vector.tensor_scalar(onehot[:, :], K.ntype[0:NTYPES, :], K.pid[0:NTYPES, 0:1], None, ALU.is_equal).then_inc(hot, 1)
            for c in range(NC):
                part = slice(c * CH, (c + 1) * CH)
                dve.wait_ge(lit, c + 1)
                if c >= 2:
                    dve.wait_ge(done, c - 1)
                nc.vector.tensor_tensor(diff[:, c % 2, :], lifted[:, c % 2, :], old[:, part], ALU.subtract).then_inc(mixed, 1)
                dve.wait_ge(spread_, c + 1)
                dve.wait_ge(mixed, 2 * c + 1)
                nc.vector.tensor_tensor(diff[:, c % 2, :], diff[:, c % 2, :], alpha[c % 2][:, 0:CH], ALU.mult).then_inc(mixed, 1)
                dve.wait_ge(mixed, 2 * c + 2)
                nc.vector.tensor_tensor(out[:, part], diff[:, c % 2, :], old[:, part], ALU.add).then_inc(done, 1)


def add_nodes(nc, tag, out, a, b, op=None):
    with Stage(nc, tag) as s:
        block = s.block()

        @block.vector
        def _(dve):
            nc.vector.tensor_tensor(out[:, :], a[:, :], b[:, :], op or ALU.add)


def degree_scale(nc, K, D):
    with Stage(nc, "deg") as s:
        loaded, made, rooted = s.sem("loaded"), s.sem("made"), s.sem("rooted")
        deg = s.sb("deg", [P, NP])
        block = s.block()

        @block.sync
        def _(sp):
            sp.dma_start(deg[:, :], D.degree.partition_broadcast(P)).then_inc(loaded, 16)

        @block.scalar
        def _(act):
            act.wait_ge(loaded, 16)
            nc.scalar.activation(deg[:, :], deg[:, :], ACT.Sqrt, bias=K.ones[:, 0:1]).then_inc(rooted, 1)

        @block.vector
        def _(dve):
            dve.wait_ge(rooted, 1)
            nc.vector.reciprocal(K.isd[:, :], deg[:, :]).then_inc(made, 1)


def batch_norm(nc, K, D, tag, sums, own, bias, gain, shift, out, relu):
    with Stage(nc, tag) as s:
        loaded, made, squared, rooted = (s.sem(x) for x in ("loaded", "made", "squared", "rooted"))
        cols = s.sb("cols", [P, 3])
        y = s.sb("y", [P, NP])
        sq = s.sb("sq", [P, N])
        st = s.sb("st", [P, 6])
        block = s.block()

        @block.sync
        def _(sp):
            for i, v in enumerate((bias, gain, shift)):
                sp.dma_start(cols[:, i:i + 1], v.rearrange("(p o) -> p o", o=1)).then_inc(loaded, 16)

        @block.vector
        def _(dve):
            link = linked(dve, made)
            link(nc.vector.tensor_tensor(y[:, :], sums[:, :], own[:, :], ALU.add))
            link(nc.vector.tensor_tensor(y[:, :], y[:, :], K.isd[:, :], ALU.mult))
            dve.wait_ge(loaded, 48)
            link(nc.vector.tensor_scalar(y[:, :], y[:, :], cols[:, 0:1], None, ALU.add))
            link(nc.vector.tensor_reduce(st[:, 0:1], y[:, 0:N], AX.X, ALU.add))
            link(nc.vector.tensor_scalar(st[:, 0:1], st[:, 0:1], 1.0 / N, None, ALU.mult))
            link(nc.vector.tensor_scalar(y[:, :], y[:, :], st[:, 0:1], None, ALU.subtract))
            link(nc.vector.tensor_tensor(sq[:, :], y[:, 0:N], y[:, 0:N], ALU.mult))
            link(nc.vector.tensor_reduce(st[:, 1:2], sq[:, :], AX.X, ALU.add))
            dve.wait_ge(rooted, 1)
            link(nc.vector.reciprocal(st[:, 3:4], st[:, 2:3]))
            link(nc.vector.tensor_tensor(st[:, 4:5], st[:, 3:4], cols[:, 1:2], ALU.mult))
            link(nc.vector.tensor_scalar(y[:, :], y[:, :], st[:, 4:5], cols[:, 2:3], ALU.mult, ALU.add))
            nc.vector.tensor_scalar(out[:, :], y[:, :], 0.0 if relu else -3.0e38, None, ALU.max).then_inc(squared, 1)

        @block.scalar
        def _(act):
            act.wait_ge(made, 8)
            nc.scalar.activation(st[:, 2:3], st[:, 1:2], ACT.Sqrt, scale=1.0 / N, bias=K.eps[:, 0:1]).then_inc(rooted, 1)


def message_weights(nc, K, D, up, down):
    c = 1.0 / (10.0 * (2 * 32) ** 0.5)
    with Stage(nc, "mwt") as s:
        zeroed, loaded, made = s.sem("zeroed"), s.sem("loaded"), s.sem("made")
        tmp = [s.sb(f"tmp{i}", [P, 32]) for i in range(2)]
        block = s.block()

        @block.gpsimd
        def _(pool):
            for m in (up, *down, *tmp):
                nc.gpsimd.memset(m[:, :], 0.0).then_inc(zeroed, 1)

        @block.sync
        def _(sp):
            sp.wait_ge(zeroed, 5)
            sp.dma_start(up[0:32, 0:32], D.L2_gnn_W_up_s).then_inc(loaded, 16)
            sp.dma_start(tmp[0][0:32, :], D.L2_gnn_W_out_s[0:32, :]).then_inc(loaded, 16)
            sp.dma_start(tmp[1][0:32, :], D.L2_gnn_W_out_v[0:32, :]).then_inc(loaded, 16)
            for i in range(3):
                blk = slice(32 + 32 * i, 64 + 32 * i)
                sp.dma_start(up[32 + i:P:3, blk], D.L2_gnn_W_up_v).then_inc(loaded, 16)
                sp.dma_start(tmp[0][blk, :], D.L2_gnn_W_out_v[32:64, :]).then_inc(loaded, 16)
                sp.dma_start(tmp[1][blk, :], D.L2_gnn_W_out_s[32:64, :]).then_inc(loaded, 16)

        @block.vector
        def _(dve):
            dve.wait_ge(loaded, 16 * 12)
            link = linked(dve, made)
            link(nc.vector.tensor_scalar(up[:, :], up[:, :], 32 ** -0.5, None, ALU.mult))
            link(nc.vector.tensor_scalar(down[0][0:32, 0:32], tmp[0][0:32, :], c, None, ALU.mult))
            for i in range(3):
                blk = slice(32 + 32 * i, 64 + 32 * i)
                link(nc.vector.tensor_scalar(down[0][blk, 32 + i:P:3], tmp[0][blk, :], c, None, ALU.mult))
                link(nc.vector.tensor_scalar(down[1][0:32, 32 + i:P:3], tmp[1][0:32, :], c, None, ALU.mult))
                link(nc.vector.tensor_scalar(down[1][blk, 0:32], tmp[1][blk, :], c * 3 ** -0.5, None, ALU.mult))


def messages(nc, K, D, tag, down):
    with Stage(nc, tag) as s:
        idx_in, rows_in, edge_in, hidden_in, out_y_in, stored = ([s.sem(f"{x}{k}") for k in range(4)] for x in
                                                                 ("idx_in", "rows_in", "edge_in", "hidden_in", "out_y_in", "stored"))
        began, loaded, ones_set, scaled, turned, upcopied, radial, multiplied, mapped, graded, added, scanned, turned_back, copied = (
            s.sem(x) for x in ("began", "loaded", "ones_set", "scaled", "turned", "upcopied", "radial", "multiplied", "mapped",
                               "graded", "added", "scanned", "turned_back", "copied"))
        a3 = [s.sb(f"a3{k}", [64, P]) for k in range(2)]
        idx = [s.sb(f"idx{k}", [P, J], I32) for k in range(4)]
        rows = [s.sb(f"rows{k}", [P, J, P]) for k in range(4)]
        edge = [s.sb(f"edge{k}", [P, J, 5]) for k in range(4)]
        hidden = [s.sb(f"hidden{k}", [64, W]) for k in range(4)]
        out_y = [s.sb(f"out_y{k}", [P, W]) for k in range(4)]
        sc = [[s.sb(f"sc{u}{k}", [P, J, P]) for k in range(2)] for u in range(2)]
        un = [[s.sb(f"un{u}{k}", [P, W]) for k in range(2)] for u in range(2)]
        prod = [s.sb(f"prod{k}", [P, W]) for k in range(2)]
        vec = s.sb("vec", [P, W])
        total = s.sb("total", [P, W])
        run = [s.sb(f"run{u}", [P, W]) for u in range(2)]
        out = [s.sb(f"out{k}", [P, J, P]) for k in range(4)]
        pu = [s.ps(f"pu{k}") for k in range(2)]
        pr = [s.ps(f"pr{k}") for k in range(2)]
        pm = [s.ps(f"pm{k}") for k in range(2)]
        pback = s.ps("pback")
        sums = D.sums.rearrange("(g j p) d -> g p j d", j=J, p=P)
        block = s.block()

        @block.sync
        def _(sp):
            for k, which in enumerate(((0, 2, 2, 2), (1, 3, 3, 3))):
                for n, w in enumerate(which):
                    sp.dma_start(a3[k][:, n * 32:(n + 1) * 32], D.L2_gnn_A3[:, w * 32:(w + 1) * 32]).then_inc(loaded, 16)

            def store(k, g):
                sp.wait_ge(copied, g + 1)
                sp.dma_start(sums[bass.ds(g, 1), :, :, :].rearrange("g p j d -> (g p) j d"), out[k][:, :, :]).then_inc(stored[k], 16)

            def step(q, k):
                g = q * 4 + k
                at = sp.snap(g * W) if not isinstance(g, int) else g * W
                if not first(q, k, 4):
                    sp.wait_ge(rows_in[k], q * 64)
                sp.dma_start(idx[k][:, :], D.src4[bass.ds(g, 1), :, :].rearrange("g p j -> (g p) j")).then_inc(idx_in[k], 16)
                if not first(q, k, 4):
                    sp.wait_ge(scaled, 2 * (g - 3))
                sp.dma_start(edge[k][:, :, :], D.ea5[bass.ds(g, 1), :, :].rearrange("g p (j c) -> (g p) j c", c=5)).then_inc(edge_in[k], 16)
                if not first(q, k, 4):
                    sp.wait_ge(graded, g - 3)
                elif q == 0 and k == 0:
                    sp.wait_ge(ones_set, 4)
                sp.dma_start(hidden[k][:, :], D.hidden[:, bass.ds(at, W)]).then_inc(hidden_in[k], 16)
                for i in range(3):
                    sp.dma_start(out_y[k][32 + i:P:3, :], D.ea4[1 + i, bass.ds(at, W)].partition_broadcast(32)).then_inc(out_y_in[k], 16)
                if not first(q, k, 5):
                    store((k + 3) % 4, g - 5)
            groups(sp, step)
            for g in range(G - 5, G):
                store(g % 4, g)
            for k in range(4):
                sp.wait_ge(stored[k], 16 * len(range(k, G, 4)))

        @block.gpsimd
        def _(pool):
            for k in range(4):
                nc.gpsimd.memset(out_y[k][0:32, :], 1.0).then_inc(ones_set, 1)

            def step(q, k):
                g = q * 4 + k
                pool.wait_ge(idx_in[k], q * 16 + 16)
                if not first(q, k, 4):
                    pool.wait_ge(scaled, 2 * (g - 3))
                pool.sem_inc(began, 1)
                for j in range(J):
                    nc.gpsimd.indirect_dma_start(rows[k][:, j, :], None, D.rows,
                                                 bass.IndirectOffsetOnAxis(ap=idx[k][:, j:j + 1], axis=0)).then_inc(rows_in[k], 16)
            groups(pool, step)

        @block.tensor
        def _(pe):
            def turn(q, k):
                g = q * 4 + k
                u = k % 2
                for n in range(2):
                    pe.wait_ge(scaled, 2 * g + n + 1)
                    if not first(q, k, 1):
                        pe.wait_ge(upcopied, 2 * g + n - 1)
                    for j in range(J):
                        last = nc.tensor.transpose(pu[n][:, j * P:(j + 1) * P], sc[u][n][:, j, :], K.ident[:, :])
                    last.then_inc(turned, 1)

            def weigh(q, k):
                g = q * 4 + k
                pe.wait_ge(hidden_in[k], q * 16 + 16)
                for n in range(2):
                    if not first(q, k, 1):
                        pe.wait_ge(multiplied, 2 * g + n - 1)
                    nc.tensor.matmul(pr[n][:, :], a3[n][:, :], hidden[k][:, :], start=True, stop=True).then_inc(radial, 1)

            def turn_back(u, g, early):
                pe.wait_ge(scanned, g + 1)
                if not early:
                    pe.wait_ge(copied, g)
                for j in range(J):
                    last = nc.tensor.transpose(pback[:, j * P:(j + 1) * P], run[u][:, j * P:(j + 1) * P], K.ident[:, :])
                last.then_inc(turned_back, 1)

            def step(q, k, last=False):
                g = q * 4 + k
                for n, free in enumerate((added, graded)):
                    pe.wait_ge(multiplied, 2 * g + n + 1)
                    if not first(q, k, 1):
                        pe.wait_ge(free, g)
                    nc.tensor.matmul(pm[n][:, :], down[n][:, :], prod[n][:, :], start=True, stop=True).then_inc(mapped, 1)
                if not last:
                    weigh(q + k // 3, (k + 1) % 4)
                if not (isinstance(g, int) and g >= G - 2):
                    turn(q + k // 2, (k + 2) % 4)
                turn_back(k % 2, g, first(q, k, 1))
            pe.wait_ge(loaded, 16 * 8)
            turn(0, 0)
            turn(0, 1)
            weigh(0, 0)
            groups(pe, step, tail=step)

        @block.scalar
        def _(act):
            def copy_up(q, k):
                g = q * 4 + k
                for n in range(2):
                    act.wait_ge(turned, 2 * g + n + 1)
                    if not first(q, k, 2):
                        act.wait_ge(multiplied, 2 * (g - 1) + n - 1)
                    nc.scalar.activation(un[k % 2][n][:, :], pu[n][:, :], ACT.Copy).then_inc(upcopied, 1)

            def copy_out(k, h, uses):
                act.wait_ge(turned_back, h + 1)
                if not (isinstance(uses, int) and uses == 0):
                    act.wait_ge(stored[k], uses * 16)
                nc.scalar.activation(out[k][:, :, :].rearrange("p j d -> p (j d)"), pback[:, :], ACT.Copy).then_inc(copied, 1)

            def step(q, k, last=False):
                g = q * 4 + k
                if not (isinstance(g, int) and g >= G - 2):
                    copy_up(q + k // 2, (k + 2) % 4)
                copy_out(k, g, q)
            copy_up(0, 0)
            copy_up(0, 1)
            groups(act, step, tail=step)

        @block.vector
        def _(dve):
            def scale(q, k):
                g = q * 4 + k
                u = k % 2
                dve.wait_ge(rows_in[k], q * 64 + 64)
                dve.wait_ge(edge_in[k], q * 16 + 16)
                if not first(q, k, 2):
                    dve.wait_ge(turned, 2 * (g - 1))
                nc.vector.tensor_tensor(sc[u][0][:, :, :], rows[k][:, :, :],
                                        edge[k][:, :, 0:1].broadcast_to([P, J, P]), ALU.mult).then_inc(scaled, 1)
                nc.vector.tensor_tensor(sc[u][1][:, :, :].rearrange("p j (b c) -> p j b c", c=32),
                                        rows[k][:, :, :].rearrange("p j (b c) -> p j b c", c=32),
                                        edge[k][:, :, 1:5].unsqueeze(3).broadcast_to([P, J, 4, 32]), ALU.mult).then_inc(scaled, 1)

            def finish(q, k, u, g, early):
                dve.wait_ge(out_y_in[k], q * 48 + 48)
                dve.wait_ge(mapped, 2 * g + 2)
                if not early:
                    dve.wait_ge(added, g)
                nc.vector.tensor_tensor(vec[:, :], pm[1][:, :], out_y[k][:, :], ALU.mult).then_inc(graded, 1)
                dve.wait_ge(graded, g + 1)
                if not early:
                    dve.wait_ge(scanned, g)
                nc.vector.tensor_tensor(total[:, :], pm[0][:, :], vec[:, :], ALU.add).then_inc(added, 1)
                dve.wait_ge(added, g + 1)
                if not (isinstance(g, int) and g < 2):
                    dve.wait_ge(turned_back, g - 1)
                nc.vector.tensor_tensor_scan(run[u][:, :], K.same[:, bass.ds(g * W, W)], total[:, :],
                                             0.0 if early else run[1 - u][:, W - 1:W], ALU.mult, ALU.add).then_inc(scanned, 1)

            def step(q, k, last_group=False):
                g = q * 4 + k
                u = k % 2
                for n in range(2):
                    dve.wait_ge(upcopied, 2 * g + n + 1)
                    dve.wait_ge(radial, 2 * g + n + 1)
                    if not first(q, k, 1):
                        dve.wait_ge(mapped, 2 * g + n - 1)
                    nc.vector.tensor_tensor(prod[n][:, :], pr[n][:, :], un[u][n][:, :], ALU.mult).then_inc(multiplied, 1)
                if not (isinstance(g, int) and g >= G - 2):
                    scale(q + k // 2, (k + 2) % 4)
                finish(q, k, u, g, first(q, k, 1))
            scale(0, 0)
            scale(0, 1)
            groups(dve, step, tail=step)


class Names:
    pass


def build(nc, D, out):
    def dram(name, shape, dt=F32):
        return nc.dram_tensor(name, shape, dt).ap()

    D.coarse = dram("coarse", (TILES,), I32)
    D.same = dram("same", (EP,), U8)
    D.start_bias = dram("start_bias", (EP,), BF16)
    D.kvrow = dram("kvrow", (EP,), I32)
    D.degree = dram("degree", (NP,))
    D.query_rows = dram("query_rows", (EP, P))
    D.table = dram("table", (NP * RELS, 2 * P))
    D.att_sums = dram("att_sums", (EP, P + HEADS))
    D.sums = dram("sums", (EP, P))
    D.rows = dram("rows", (NP, P))
    D.hidden = dram("hidden", (64, EP))

    K = Names()
    with ExitStack() as stack:
        def sb(name, shape, dt=F32, st=stack):
            return st.enter_context(nc.sbuf_tensor(name, shape, dt))
        K.ident, K.negid, K.mean, K.headsum = (sb(x, [P, P]) for x in ("ident", "negid", "meanm", "headsum"))
        K.eps, K.ones, K.pid = sb("eps", [P, 1]), sb("ones", [P, 1]), sb("pid", [P, 1])
        K.end, K.start = sb("end", [P, NT], I32), sb("start", [P, NT], I32)
        K.degree, K.has = sb("degree_sb", [P, NT]), sb("has", [P, NT])
        K.x = sb("x", [P, NP])
        constants(nc, K)
        K.same = sb("same_sb", [P, EP], U8)
        graph_index(nc, K, D)
        clear_edge_rows(nc, D)
        a, b, c = (sb(x, [P, NP]) for x in ("a", "b", "c"))

        with ExitStack() as inner:
            h = sb("h", [P, NP], st=inner)
            K.ntype = sb("ntype", [P, NP], st=inner)
            load_nodes(nc, K, D, h)
            for l in range(LAYERS):
                typed_linear(nc, K, f"qkv{l}", h, [D.L0_gnn_Wq[l], D.L0_gnn_Wk[l], D.L0_gnn_Wv[l]], [a, b, c])
                to_rows(nc, K, f"qr{l}", a, dram=D.query_rows, start=K.start, limit=EP - 1)
                relation_table(nc, K, D, f"tab{l}", l, b, c)
                attention(nc, K, D, f"att{l}")
                ends(nc, K, D, f"agg{l}", a, per_head=True)
                typed_linear(nc, K, f"wa{l}", a, [D.L0_gnn_Wa[l]], [b])
                mix_with_input(nc, K, D, f"mix{l}", l, b, h, c)
                layernorm(nc, K, f"ln{l}", c, h, D.L0_gnn_ln_g[l], D.L0_gnn_ln_b[l])
            linear(nc, K, "ff", a, [(D.L0_gnn_ff_w, h)], D.L0_gnn_ff_b)
        layernorm(nc, K, "norm0", K.x, K.x, add=a)

        sum_edges(nc, K, D, "ea", linear_in=D.ea128, radial=True)
        ends(nc, K, D, "eae", a)
        linear(nc, K, "emb", b, [(D.L1_gnn_We, a)], row_term=(D.L1_gnn_be, D.degree))
        linear(nc, K, "w1", a, [(D.L1_gnn_W1[0:P, :], K.x), (D.L1_gnn_W1[P:2 * P, :], b)])
        to_rows(nc, K, "yr", a, dram=D.rows)
        sum_edges(nc, K, D, "nb", table=D.rows)
        ends(nc, K, D, "nbe", b)
        add_nodes(nc, "nba", b, a, b)
        relu_bias(nc, K, "act1", b, D.L1_gnn_b1)
        linear(nc, K, "w2", a, [(D.L1_gnn_W2, b)], D.L1_gnn_b2)
        layernorm(nc, K, "norm1", K.x, K.x, add=a)

        with ExitStack() as inner:
            up = sb("up", [P, P], st=inner)
            down = [sb(f"down{k}", [P, P], st=inner) for k in range(2)]
            message_weights(nc, K, D, up, down)
            linear(nc, K, "upl", a, [(up, K.x)])
            to_rows(nc, K, "ur", a, dram=D.rows)
            messages(nc, K, D, "msg", down)
        ends(nc, K, D, "mse", a)
        layernorm(nc, K, "norm2", K.x, K.x, add=a)

        K.isd = sb("isd", [P, NP])
        degree_scale(nc, K, D)
        source = K.x
        for l in range(2):
            w, bias, gain, shift = D.l3[l]
            linear(nc, K, f"gcn{l}", a, [(w, source)])
            add_nodes(nc, f"gs{l}", b, a, K.isd, ALU.mult)
            to_rows(nc, K, f"gr{l}", b, dram=D.rows)
            sum_edges(nc, K, D, f"gsum{l}", table=D.rows)
            ends(nc, K, D, f"ge{l}", a)
            batch_norm(nc, K, D, f"bn{l}", a, b, bias, gain, shift, c, relu=l == 0)
            source = c
        layernorm(nc, K, "norm3", K.x, K.x, add=c)
        store_nodes(nc, K, out)


def load_nodes(nc, K, D, h):
    with Stage(nc, "ldn") as s:
        loaded, cast = s.sem("loaded"), s.sem("cast")
        nt = s.sb("nt", [P, NP], I32)
        block = s.block()

        @block.sync
        def _(sp):
            sp.dma_start(nt[:, :], D.ntype.partition_broadcast(P)).then_inc(loaded, 16)
            sp.dma_start(K.x[:, :], D.x).then_inc(loaded, 16)
            sp.dma_start(h[:, :], D.x).then_inc(loaded, 16)
            sp.wait_ge(loaded, 48)

        @block.vector
        def _(dve):
            dve.wait_ge(loaded, 48)
            nc.vector.tensor_copy(K.ntype[:, :], nt[:, :]).then_inc(cast, 1)


def relu_bias(nc, K, tag, x, bias):
    with Stage(nc, tag) as s:
        loaded, done = s.sem("loaded"), s.sem("done")
        b = s.sb("b", [P, 1])
        block = s.block()

        @block.sync
        def _(sp):
            sp.dma_start(b[:, :], bias.rearrange("(p o) -> p o", o=1)).then_inc(loaded, 16)

        @block.vector
        def _(dve):
            dve.wait_ge(loaded, 16)
            nc.vector.tensor_scalar(x[:, :], x[:, :], b[:, 0:1], 0.0, ALU.add, ALU.max).then_inc(done, 1)


def store_nodes(nc, K, out):
    with Stage(nc, "sto") as s:
        rows = s.sb("rows", [P, NT, P])
        to_rows(nc, K, "outr", K.x, rows=rows)
        stored = s.sem("stored")
        block = s.block()
        full = N // P

        @block.sync
        def _(sp):
            sp.dma_start(out[0:full * P, :].rearrange("(t p) d -> p t d", p=P), rows[:, 0:full, :]).then_inc(stored, 16)
            sp.dma_start(out[full * P:N, :], rows[0:N - full * P, full, :]).then_inc(stored, 16)
            sp.wait_ge(stored, 32)


_WEIGHTS = ['L0_gnn_Wk', 'L0_gnn_Wq', 'L0_gnn_Wv', 'L0_gnn_Wa', 'L0_gnn_Watt', 'L0_gnn_Wmsg', 'L0_gnn_pri', 'L0_gnn_skip',
            'L0_gnn_ln_g', 'L0_gnn_ln_b', 'L0_gnn_ff_w', 'L0_gnn_ff_b', 'L1_gnn_We', 'L1_gnn_be', 'L1_gnn_W1', 'L1_gnn_b1',
            'L1_gnn_W2', 'L1_gnn_b2', 'L2_gnn_W_up_s', 'L2_gnn_W_up_v', 'L2_gnn_A1', 'L2_gnn_b1', 'L2_gnn_A2', 'L2_gnn_b2',
            'L2_gnn_A3', 'L2_gnn_W_out_s', 'L2_gnn_W_out_v', 'L3_gnn_W1', 'L3_gnn_b1', 'L3_gnn_g1', 'L3_gnn_bt1',
            'L3_gnn_W2', 'L3_gnn_b2', 'L3_gnn_g2', 'L3_gnn_bt2']


def kernel(**inputs):
    import numpy as np
    import concourse.bacc as bacc
    from concourse.bass_utils import run_bass_kernel_spmd

    def padded(a, n, fill=0):
        wide = np.full(a.shape[:-1] + (n,), fill, a.dtype)
        wide[..., :a.shape[-1]] = a
        return wide

    given = {k: np.asarray(v) for k, v in inputs.items()}
    src, dst = padded(given["src"], EP), padded(given["dst"], EP, N)
    by_edge = np.ones((EP, 5), np.float32)
    by_edge[:E, [0, 2, 3, 4]] = given["edge_attr_4"]
    arrays = {
        "x": padded(given["x"].T, NP), "ntype": padded(given["node_type_16"], NP),
        "dst": dst, "dst_before": np.concatenate([np.full(1, -1, dst.dtype), dst[:-1]]),
        "src_flat": src, "src4": np.ascontiguousarray(src.reshape(G, J, P).transpose(0, 2, 1)),
        "etype_flat": padded(given["edge_type_32"], EP),
        "ea128": padded(given["edge_attr_128"].T, EP), "ea4": padded(given["edge_attr_4"].T, EP),
        "ea8": padded(given["edge_attr_8"].T, EP),
        "ea5": np.ascontiguousarray(by_edge.reshape(G, J, P, 5).transpose(0, 2, 1, 3)).reshape(G, P, J * 5),
    }
    arrays.update({k: given[k] for k in _WEIGHTS})
    nc = bacc.Bacc("TRN2", target_bir_lowering=False, num_devices=1)
    D = Names()
    for name, a in arrays.items():
        ap = nc.dram_tensor(f"in_{name}", a.shape, mybir.dt.from_np(a.dtype), kind="ExternalInput").ap()
        D.__dict__[name] = ap
    D.l3 = [(D.L3_gnn_W1, D.L3_gnn_b1, D.L3_gnn_g1, D.L3_gnn_bt1), (D.L3_gnn_W2, D.L3_gnn_b2, D.L3_gnn_g2, D.L3_gnn_bt2)]
    out = nc.dram_tensor("out", (N, P), F32, kind="ExternalOutput").ap()
    build(nc, D, out)
    r = run_bass_kernel_spmd(nc, [{f"in_{k}": v for k, v in arrays.items()}], core_ids=[0])
    return r.results[0]["out"]
```

```python
from contextlib import ExitStack

import concourse.bass as bass
import concourse.mybir as mybir

F32, I32, BF16, U8 = mybir.dt.float32, mybir.dt.int32, mybir.dt.bfloat16, mybir.dt.uint8
ALU = mybir.AluOpType
ACT = mybir.ActivationFunctionType
AX = mybir.AxisListType

P = 128
N, E = 3125, 50000
NT = -(-N // P)
NP = NT * P
W = 512
J = W // P
G = 98
EP = G * W
CH = 400
NC = NP // CH
TILES = EP // P
NTYPES, RELS, HEADS, HS, LAYERS = 16, 32, 8, 16, 2
BIG = 1.0e30
FAR = 1.0e6


class Stage:

    def __init__(self, nc, tag):
        self.nc, self.tag = nc, tag
        self.stack = ExitStack()
        self.sems = []

    def sb(self, name, shape, dt=F32):
        return self.stack.enter_context(self.nc.sbuf_tensor(f"{self.tag}_{name}", shape, dt))

    def ps(self, name, shape=(P, W)):
        return self.stack.enter_context(self.nc.psum_tensor(f"{self.tag}_{name}", list(shape), F32))

    def sem(self, name):
        s = self.nc.alloc_semaphore(f"{self.tag}_{name}")
        self.sems.append(s)
        return s

    def block(self):
        return self.stack.enter_context(self.nc.Block())

    def __enter__(self):
        return self

    def __exit__(self, *exc):
        self.stack.close()
        if exc[0] is None:
            self.nc.clear_and_free_semaphores(self.sems)
            self.nc.all_engine_barrier()
        return False


def groups(eng, step, tail=None):
    for g in range(6):
        step(g // 4, g % 4)
    turns = (G - 2) // 4
    with eng.Fori(1, turns if tail is None else turns - 1) as q:
        step(q, 2)
        step(q, 3)
        step(q + 1, 0)
        step(q + 1, 1)
    if tail is not None:
        for g in range(G - 4, G):
            tail(g // 4, g % 4, G - 1 - g)


def first(q, k, n):
    return isinstance(q, int) and 4 * q + k < n


def at(q, k, d):
    return q + (k + d) // 4, (k + d) % 4


def linked(eng, sem):
    done = [0]

    def link(ins):
        done[0] += 1
        ins.then_inc(sem, 1)
        eng.wait_ge(sem, done[0])
    return link


def constants(nc, K):
    with Stage(nc, "cst") as s:
        made = s.sem("made")
        hid = s.sb("hid", [P, P], I32)
        pid = s.sb("pid", [P, 1], I32)
        hidf = s.sb("hidf", [P, P])
        pidf = s.sb("pidf", [P, 1])
        block = s.block()

        @block.gpsimd
        def _(pool):
            link = linked(pool, made)
            link(nc.gpsimd.memset(K.ident[:, :], 0.0))
            link(nc.gpsimd.affine_select(out=K.ident[:, :], in_=K.ident[:, :], compare_op=ALU.not_equal,
                                         fill=1.0, base=0, pattern=[[-1, P]], channel_multiplier=1))
            link(nc.gpsimd.memset(K.mean[:, :], 1.0 / P))
            link(nc.gpsimd.memset(K.eps[:, :], 1e-5))
            link(nc.gpsimd.memset(K.ones[:, :], 1.0))
            link(nc.gpsimd.iota(hid[:, :], pattern=[[1, P]], base=0, channel_multiplier=0))
            link(nc.gpsimd.iota(pid[:, :], pattern=[[0, 1]], base=0, channel_multiplier=1))

        @block.vector
        def _(dve):
            dve.wait_ge(made, 7)
            done = [7]

            def link(ins):
                done[0] += 1
                ins.then_inc(made, 1)
                dve.wait_ge(made, done[0])
            link(nc.vector.tensor_scalar(K.negid[:, :], K.ident[:, :], -1.0, None, ALU.mult))
            link(nc.vector.tensor_scalar(hid[:, :], hid[:, :], 4, None, ALU.arith_shift_right))
            link(nc.vector.tensor_copy(hidf[:, :], hid[:, :]))
            link(nc.vector.tensor_copy(K.pid[:, :], pid[:, :]))
            link(nc.vector.tensor_scalar(pid[:, :], pid[:, :], 4, None, ALU.arith_shift_right))
            link(nc.vector.tensor_copy(pidf[:, :], pid[:, :]))
            link(nc.vector.tensor_scalar(K.headsum[:, :], hidf[:, :], pidf[:, 0:1], None, ALU.is_equal))


def graph_index(nc, K, D, h):
    C = EP // P
    with Stage(nc, "idx") as s:
        loaded, made, coarse_in, fetched, back = (s.sem(x) for x in ("loaded", "made", "coarse", "fetched", "back"))
        nodes_in, types_in, cast = s.sem("nodes_in"), s.sem("types_in"), s.sem("cast")
        fine_in = [s.sem(f"fine_in{k}") for k in range(2)]
        types = s.sb("types", [P, NP], I32)
        dst = s.sb("dst", [P, C], I32)
        prev = s.sb("prev", [P, C], I32)
        src = s.sb("src", [P, C], I32)
        ety = s.sb("ety", [P, C], I32)
        same = s.sb("same", [P, C])
        same8 = s.sb("same8", [P, C], U8)
        bias = s.sb("bias", [P, C], BF16)
        row = s.sb("row", [P, C], I32)
        coarse_i = s.sb("coarse_i", [P, TILES], I32)
        node_i = s.sb("node_i", [P, NT], I32)
        node = s.sb("node", [P, NT])
        cmp = s.sb("cmp", [P, NT, TILES], BF16)
        tile_f = s.sb("tile_f", [P, 2, NT])
        tile_i = s.sb("tile_i", [P, 2, NT], I32)
        fine = s.sb("fine", [P, 2, NT, P], I32)
        within = s.sb("within", [P, 2, NT])
        count = s.sb("count", [P, 2, NT])
        start = s.sb("start", [P, NT])
        tmp = s.sb("tmp", [P, NT])
        block = s.block()

        @block.sync
        def _(sp):
            with nc.allow_non_contiguous_dma(reason="one number of each tile"):
                sp.dma_start(D.coarse.rearrange("(t o) -> t o", o=1),
                             D.dst.rearrange("(t c) -> t c", c=P)[:, P - 1:P]).then_inc(coarse_in, 16)
            sp.dma_start(dst[:, :], D.dst.rearrange("(p c) -> p c", p=P)).then_inc(loaded, 16)
            sp.dma_start(prev[:, :], D.dst_before.rearrange("(p c) -> p c", p=P)).then_inc(loaded, 16)
            sp.dma_start(src[:, :], D.src_flat.rearrange("(p c) -> p c", p=P)).then_inc(loaded, 16)
            sp.dma_start(ety[:, :], D.etype_flat.rearrange("(p c) -> p c", p=P)).then_inc(loaded, 16)
            sp.wait_ge(coarse_in, 16)
            sp.dma_start(coarse_i[:, :], D.coarse.partition_broadcast(P)).then_inc(coarse_in, 16)
            sp.dma_start(types[:, :], D.ntype.partition_broadcast(P)).then_inc(types_in, 16)
            sp.dma_start(h[:, :], D.x).then_inc(nodes_in, 16)
            sp.wait_ge(made, 14)
            sp.dma_start(D.same.rearrange("(p c) -> p c", p=P), same8[:, :]).then_inc(back, 16)
            sp.dma_start(D.start_bias.rearrange("(p c) -> p c", p=P), bias[:, :]).then_inc(back, 16)
            sp.dma_start(D.kvrow.rearrange("(p c) -> p c", p=P), row[:, :]).then_inc(back, 16)
            sp.wait_ge(back, 48)
            sp.dma_start(K.same[:, :], D.same.partition_broadcast(P)).then_inc(back, 16)
            sp.wait_ge(made, 20)
            with nc.allow_non_contiguous_dma(reason="one number of each node"):
                sp.dma_start(D.degree.rearrange("(t p) -> p t", p=P), K.degree[:, :]).then_inc(back, 16)
            sp.wait_ge(back, 80)
            sp.wait_ge(nodes_in, 16)

        @block.gpsimd
        def _(pool):
            nc.gpsimd.iota(node_i[:, :], pattern=[[P, NT]], base=0, channel_multiplier=1).then_inc(fetched, 1)
            for k in range(2):
                pool.wait_ge(made, 5 + 4 * k)
                for t in range(NT):
                    nc.gpsimd.indirect_dma_start(
                        fine[:, k, t, :], None, D.dst.rearrange("(t c) -> t c", c=P),
                        bass.IndirectOffsetOnAxis(ap=tile_i[:, k, t:t + 1], axis=0)).then_inc(fine_in[k], 16)

        @block.vector
        def _(dve):
            link = linked(dve, made)
            dve.wait_ge(fetched, 1)
            link(nc.vector.tensor_copy(node[:, :], node_i[:, :]))
            dve.wait_ge(coarse_in, 32)
            for k, op in enumerate((ALU.is_le, ALU.is_lt)):
                link(nc.vector.tensor_tensor(cmp[:, :, :],
                                             coarse_i[:, :].unsqueeze(1).broadcast_to([P, NT, TILES]),
                                             node[:, :].unsqueeze(2).broadcast_to([P, NT, TILES]), op))
                link(nc.vector.tensor_reduce(tile_f[:, k, :], cmp[:, :, :], AX.X, ALU.add))
                link(nc.vector.tensor_scalar(tile_f[:, k, :], tile_f[:, k, :], TILES - 1.0, None, ALU.min))
                link(nc.vector.tensor_copy(tile_i[:, k, :], tile_f[:, k, :]))
            dve.wait_ge(loaded, 64)
            link(nc.vector.tensor_tensor(same[:, :], dst[:, :], prev[:, :], ALU.is_equal))
            link(nc.vector.tensor_copy(same8[:, :], same[:, :]))
            link(nc.vector.tensor_scalar(bias[:, :], same[:, :], -1.0, BIG, ALU.add, ALU.mult))
            link(nc.vector.tensor_scalar(row[:, :], src[:, :], RELS, None, ALU.mult))
            link(nc.vector.tensor_tensor(row[:, :], row[:, :], ety[:, :], ALU.add))
            dve.wait_ge(types_in, 16)
            nc.vector.tensor_copy(K.ntype[:, :], types[:, :]).then_inc(cast, 1)
            for k, op in enumerate((ALU.is_le, ALU.is_lt)):
                dve.wait_ge(fine_in[k], NT * 16)
                link(nc.vector.tensor_tensor(cmp[:, :, 0:P], fine[:, k, :, :],
                                             node[:, :].unsqueeze(2).broadcast_to([P, NT, P]), op))
                link(nc.vector.tensor_reduce(within[:, k, :], cmp[:, :, 0:P], AX.X, ALU.add))
            link(nc.vector.scalar_tensor_tensor(count[:, :, :], tile_f[:, :, :], float(P), within[:, :, :], ALU.mult, ALU.add))
            link(nc.vector.tensor_tensor(K.degree[:, :], count[:, 0, :], count[:, 1, :], ALU.subtract))
            link(nc.vector.tensor_scalar(K.has[:, :], K.degree[:, :], 0.0, None, ALU.is_gt))
            link(nc.vector.tensor_scalar(tmp[:, :], count[:, 0, :], -1.0, 0.0, ALU.add, ALU.max))
            link(nc.vector.tensor_copy(K.end[:, :], tmp[:, :]))
            link(nc.vector.scalar_tensor_tensor(start[:, :], K.has[:, :], -FAR, count[:, 1, :], ALU.mult, ALU.add))
            link(nc.vector.tensor_scalar(start[:, :], start[:, :], FAR, None, ALU.add))
            link(nc.vector.tensor_copy(K.start[:, :], start[:, :]))


def to_rows(nc, K, tag, x, rows=None, dram=None):
    with Stage(nc, tag) as s:
        turned, copied, stored = s.sem("turned"), s.sem("copied"), s.sem("stored")
        rows = rows or s.sb("rows", [P, NT, P])
        bank = [s.ps(f"bank{i}") for i in range(2)]
        n = -(-NT // J)
        block = s.block()

        @block.tensor
        def _(pe):
            for k in range(n):
                if k >= 2:
                    pe.wait_ge(copied, k - 1)
                for t in range(k * J, min(NT, k * J + J)):
                    last = nc.tensor.transpose(bank[k % 2][:, (t - k * J) * P:(t - k * J + 1) * P],
                                               x[:, t * P:(t + 1) * P], K.ident[:, :])
                last.then_inc(turned, 1)

        @block.scalar
        def _(act):
            for k in range(n):
                m = min(NT, k * J + J) - k * J
                act.wait_ge(turned, k + 1)
                nc.scalar.activation(rows[:, k * J:k * J + m, :].rearrange("p t d -> p (t d)"),
                                     bank[k % 2][:, 0:m * P], ACT.Copy).then_inc(copied, 1)

        if dram is not None:
            @block.sync
            def _(sp):
                view = dram.rearrange("(t p) d -> p t d", p=P)
                for k in range(n):
                    m = min(NT, k * J + J) - k * J
                    sp.wait_ge(copied, k + 1)
                    sp.dma_start(view[:, k * J:k * J + m, :], rows[:, k * J:k * J + m, :]).then_inc(stored, 16)
                sp.wait_ge(stored, 16 * n)


def ends(nc, K, D, tag, out, per_head=False):
    src, width = (D.att_sums, P + HEADS) if per_head else (D.sums, P)
    with Stage(nc, tag) as s:
        n = -(-NT // J)
        fetched = [s.sem(f"fetched{k}") for k in range(n)]
        ready, turned, copied, inverted = (s.sem(x) for x in ("ready", "turned", "copied", "inverted"))
        rows = s.sb("rows", [P, NT, width])
        scaled = s.sb("scaled", [P, NT, P])
        inv = s.sb("inv", [P, NT, HEADS])
        bank = [s.ps(f"bank{i}") for i in range(2)]
        block = s.block()

        def tiles(k):
            return slice(k * J, min(NT, k * J + J))

        @block.gpsimd
        def _(pool):
            for t in range(NT):
                nc.gpsimd.indirect_dma_start(rows[:, t, :], None, src,
                                             bass.IndirectOffsetOnAxis(ap=K.end[:, t:t + 1], axis=0)).then_inc(fetched[t // J], 16)

        @block.vector
        def _(dve):
            for k in range(n):
                ts = tiles(k)
                m = ts.stop - ts.start
                dve.wait_ge(fetched[k], 16 * m)
                if per_head:
                    nc.vector.reciprocal(inv[:, ts, :], rows[:, ts, P:P + HEADS]).then_inc(inverted, 1)
                    dve.wait_ge(inverted, 2 * k + 1)
                    nc.vector.tensor_tensor(inv[:, ts, :], inv[:, ts, :],
                                            K.has[:, ts].unsqueeze(2).broadcast_to([P, m, HEADS]), ALU.mult).then_inc(inverted, 1)
                    dve.wait_ge(inverted, 2 * k + 2)
                    nc.vector.tensor_tensor(scaled[:, ts, :].rearrange("p t (h c) -> p t h c", c=HS),
                                            rows[:, ts, 0:P].rearrange("p t (h c) -> p t h c", c=HS),
                                            inv[:, ts, :].unsqueeze(3).broadcast_to([P, m, HEADS, HS]),
                                            ALU.mult).then_inc(ready, 1)
                else:
                    nc.vector.tensor_tensor(scaled[:, ts, :], rows[:, ts, :],
                                            K.has[:, ts].unsqueeze(2).broadcast_to([P, m, P]), ALU.mult).then_inc(ready, 1)

        @block.tensor
        def _(pe):
            for k in range(n):
                pe.wait_ge(ready, k + 1)
                if k >= 2:
                    pe.wait_ge(copied, k - 1)
                for t in range(k * J, min(NT, k * J + J)):
                    last = nc.tensor.transpose(bank[k % 2][:, (t - k * J) * P:(t - k * J + 1) * P],
                                               scaled[:, t, :], K.ident[:, :])
                last.then_inc(turned, 1)

        @block.scalar
        def _(act):
            for k in range(n):
                m = min(NT, k * J + J) - k * J
                act.wait_ge(turned, k + 1)
                nc.scalar.activation(out[:, k * W:k * W + m * P], bank[k % 2][:, 0:m * P], ACT.Copy).then_inc(copied, 1)


def linear(nc, K, tag, out, terms, bias=None, row_term=None, times=None):
    with Stage(nc, tag) as s:
        loaded, summed, done = s.sem("loaded"), s.sem("summed"), s.sem("done")
        held = [i for i, (wd, _) in enumerate(terms) if not isinstance(wd, bass.AP)]
        w = [terms[i][0] if i in held else s.sb(f"w{i}", [P, P]) for i in range(len(terms))]
        b = s.sb("b", [P, 1])
        rw = s.sb("rw", [1, P])
        rx = s.sb("rx", [1, NP])
        acc = [s.ps(f"acc{i}") for i in range(2)]
        loads = 16 * (len(terms) - len(held) + (bias is not None) + 2 * (row_term is not None))
        block = s.block()

        @block.sync
        def _(sp):
            for i, (wd, _) in enumerate(terms):
                if i in held:
                    continue
                sp.dma_start(w[i][:, :], wd[:, :]).then_inc(loaded, 16)
            if bias is not None:
                sp.dma_start(b[:, :], bias.rearrange("(p o) -> p o", o=1)).then_inc(loaded, 16)
            if row_term is not None:
                sp.dma_start(rw[:, :], row_term[0].rearrange("(o p) -> o p", o=1)).then_inc(loaded, 16)
                sp.dma_start(rx[:, :], row_term[1].rearrange("(o p) -> o p", o=1)).then_inc(loaded, 16)

        @block.tensor
        def _(pe):
            if loads:
                pe.wait_ge(loaded, loads)
            for c in range(NC):
                if c >= 2:
                    pe.wait_ge(done, c - 1)
                for i, (_, x) in enumerate(terms):
                    last = nc.tensor.matmul(acc[c % 2][:, 0:CH], w[i][:, :], x[:, c * CH:(c + 1) * CH], start=i == 0,
                                            stop=i == len(terms) - 1 and row_term is None)
                if row_term is not None:
                    last = nc.tensor.matmul(acc[c % 2][:, 0:CH], rw[:, :], rx[:, c * CH:(c + 1) * CH], start=False, stop=True)
                last.then_inc(summed, 1)

        if times is not None:
            @block.vector
            def _(dve):
                for c in range(NC):
                    dve.wait_ge(summed, c + 1)
                    nc.vector.tensor_tensor(out[:, c * CH:(c + 1) * CH], acc[c % 2][:, 0:CH], times[:, c * CH:(c + 1) * CH],
                                            ALU.mult).then_inc(done, 1)
            return

        @block.scalar
        def _(act):
            if bias is not None:
                act.wait_ge(loaded, loads)
            for c in range(NC):
                act.wait_ge(summed, c + 1)
                nc.scalar.activation(out[:, c * CH:(c + 1) * CH], acc[c % 2][:, 0:CH], ACT.Identity,
                                     bias=b[:, 0:1] if bias is not None else 0.0).then_inc(done, 1)


def layernorm(nc, K, tag, x, out, gain=None, shift=None, add=None):
    with Stage(nc, tag) as s:
        loaded, added, meaned, centred, squared, varied, rooted, inverted, scaled, shifted = (
            s.sem(x) for x in ("loaded", "added", "meaned", "centred", "squared", "varied", "rooted", "inverted", "scaled", "shifted"))
        gb = s.sb("gb", [P, 2])
        sm, xc, sq, sd, inv, nrm = ([s.sb(f"{x}{k}", [P, CH]) for k in range(4)] for x in ("sm", "xc", "sq", "sd", "inv", "nrm"))
        mean = [s.ps(f"mean{i}") for i in range(4)]
        var = [s.ps(f"var{i}") for i in range(4)]
        affine = gain is not None
        block = s.block()

        def part(c):
            return slice(c * CH, (c + 1) * CH)

        def term(c):
            return sm[c % 4][:, :] if add is not None else x[:, part(c)]

        @block.sync
        def _(sp):
            if affine:
                sp.dma_start(gb[:, 0:1], gain.rearrange("(p o) -> p o", o=1)).then_inc(loaded, 16)
                sp.dma_start(gb[:, 1:2], shift.rearrange("(p o) -> p o", o=1)).then_inc(loaded, 16)

        @block.tensor
        def _(pe):
            for c in range(NC + 2):
                if c < NC:
                    if add is not None:
                        pe.wait_ge(added, c + 1)
                    if c >= 4:
                        pe.wait_ge(centred, c - 3)
                    nc.tensor.matmul(mean[c % 4][:, 0:CH], K.mean[:, :], term(c), start=True, stop=True).then_inc(meaned, 1)
                d = c - 2
                if d >= 0:
                    pe.wait_ge(squared, d + 1)
                    if d >= 4:
                        pe.wait_ge(rooted, d - 3)
                    nc.tensor.matmul(var[d % 4][:, 0:CH], K.mean[:, :], sq[d % 4][:, :], start=True, stop=True).then_inc(varied, 1)

        @block.scalar
        def _(act):
            for c in range(NC + 2):
                if c < NC:
                    act.wait_ge(centred, c + 1)
                    if c >= 4:
                        act.wait_ge(varied, c - 3)
                    nc.scalar.activation(sq[c % 4][:, :], xc[c % 4][:, :], ACT.Square).then_inc(squared, 1)
                d = c - 2
                if d >= 0:
                    act.wait_ge(varied, d + 1)
                    if d >= 4:
                        act.wait_ge(inverted, d - 3)
                    nc.scalar.activation(sd[d % 4][:, :], var[d % 4][:, 0:CH], ACT.Sqrt, bias=K.eps[:, 0:1]).then_inc(rooted, 1)

        @block.vector
        def _(dve):
            def total(c):
                if c >= 4:
                    dve.wait_ge(meaned, c - 3)
                    dve.wait_ge(centred, c - 3)
                nc.vector.tensor_tensor(sm[c % 4][:, :], x[:, part(c)], add[:, part(c)], ALU.add).then_inc(added, 1)

            def centre(c):
                dve.wait_ge(meaned, c + 1)
                if add is not None:
                    dve.wait_ge(added, c + 1)
                if c >= 4:
                    dve.wait_ge(squared, c - 3)
                    dve.wait_ge(scaled, c - 3)
                nc.vector.tensor_tensor(xc[c % 4][:, :], term(c), mean[c % 4][:, 0:CH], ALU.subtract).then_inc(centred, 1)

            def finish(c):
                dve.wait_ge(rooted, c + 1)
                if c >= 4:
                    dve.wait_ge(scaled, c - 3)
                nc.vector.reciprocal(inv[c % 4][:, :], sd[c % 4][:, :]).then_inc(inverted, 1)
                dve.wait_ge(inverted, c + 1)
                dve.wait_ge(centred, c + 1)
                if affine and c >= 4:
                    dve.wait_ge(shifted, c - 3)
                nc.vector.tensor_tensor(nrm[c % 4][:, :] if affine else out[:, part(c)], xc[c % 4][:, :], inv[c % 4][:, :],
                                        ALU.mult).then_inc(scaled, 1)
                if affine:
                    if c == 0:
                        dve.wait_ge(loaded, 32)
                    dve.wait_ge(scaled, c + 1)
                    nc.vector.tensor_scalar(out[:, part(c)], nrm[c % 4][:, :], gb[:, 0:1], gb[:, 1:2],
                                            ALU.mult, ALU.add).then_inc(shifted, 1)

            for c in range(NC + 4):
                if add is not None and c < NC:
                    total(c)
                if 1 <= c <= NC:
                    centre(c - 1)
                if c >= 4:
                    finish(c - 4)


def typed_linear(nc, K, tag, x, weights, outs, clear=None, edges=None, relations=None):
    M = len(weights)
    pieces = 14
    PER = G // NC // 4 * 4
    with Stage(nc, tag) as s:
        masked, used, copied = (s.sem(x) for x in ("masked", "used", "copied"))
        loaded = [s.sem(f"loaded{i}") for i in range(NTYPES // 4)]
        w = s.sb("w", [P, M, NTYPES, P])
        xm = s.sb("xm", [P, 4, CH])
        acc = [[s.ps(f"acc{u}{m}") for m in range(M)] for u in range(2)]
        if relations is not None:
            D, layer, wk, wv = relations
            w_zeroed, w_put, w_scaled = s.sem("w_zeroed"), s.sem("w_put"), s.sem("w_scaled")
            pri = s.sb("pri", [P, RELS])
        if clear is not None:
            zeroed, cleared = s.sem("zeroed"), s.sem("cleared")
            zero = s.sb("zero", [P, EP // pieces])
        if edges is not None:
            edge_in, stored = ([s.sem(f"{x}{k}") for k in range(4)] for x in ("edge_in", "stored"))
            scanned, turned_back, out_copied = (s.sem(x) for x in ("scanned", "turned_back", "out_copied"))
            cols, run = ([s.sb(f"{x}{k}", [P, W]) for k in range(4)] for x in ("cols", "run"))
            out = [s.sb(f"out{k}", [P, J, P]) for k in range(4)]
            back = [s.ps(f"back{u}") for u in range(2)]
            sums = edges[1].rearrange("(g j p) d -> g p j d", j=J, p=P)
        block = s.block()

        def chunks(eng, chunk):
            chunk(0, 0)
            chunk(1, 1)
            with eng.Fori(1, NC // 2) as q:
                chunk(q * 2, 0)
                chunk(q * 2 + 1, 1)

        def opening(c):
            return isinstance(c, int) and c == 0

        def group(c, i, d=0):
            return at(c * (PER // 4), i, d)

        @block.sync
        def _(sp):
            for t in range(0, NTYPES, 4):
                for m in range(M):
                    sp.dma_start(w[:, m, t:t + 4, :], weights[m][t:t + 4].rearrange("t d o -> d t o")).then_inc(loaded[t // 4], 16)
            if relations is not None:
                for h in range(HEADS):
                    sp.dma_start(pri[h * HS:(h + 1) * HS, :], D.L0_gnn_pri[layer, h, :].partition_broadcast(HS)).then_inc(w_put, 16)
                sp.wait_ge(w_zeroed, 2)
                for h in range(HEADS):
                    f = slice(h * HS, (h + 1) * HS)
                    sp.dma_start(wk[f, :, f], D.L0_gnn_Watt[layer, h, :, :, :].rearrange("t d o -> d t o")).then_inc(w_put, 16)
                    sp.dma_start(wv[f, :, f], D.L0_gnn_Wmsg[layer, h, :, :, :].rearrange("t d o -> d t o")).then_inc(w_put, 16)
            if clear is not None:
                sp.wait_ge(zeroed, 1)
                rows = clear.rearrange("(p c) d -> p (c d)", p=P)
                for i in range(pieces):
                    sp.dma_start(rows[:, i * (EP // pieces):(i + 1) * (EP // pieces)], zero[:, :]).then_inc(cleared, 16)
                sp.wait_ge(cleared, 16 * pieces)
            if edges is not None:
                def step(q, k):
                    g = q * 4 + k
                    if not first(q, k, 4):
                        sp.wait_ge(scanned, g - 3)
                    sp.dma_start(cols[k][:, :], edges[0][:, bass.ds(g * W, W)]).then_inc(edge_in[k], 16)
                groups(sp, step)

        @block.gpsimd
        def _(pool):
            if relations is not None:
                nc.gpsimd.memset(wk[:, :, :], 0.0).then_inc(w_zeroed, 1)
                nc.gpsimd.memset(wv[:, :, :], 0.0).then_inc(w_zeroed, 1)
            if clear is not None:
                nc.gpsimd.memset(zero[:, :], 0.0).then_inc(zeroed, 1)

        @block.vector
        def _(dve):
            def scan(q, k):
                g = q * 4 + k
                dve.wait_ge(edge_in[k], q * 16 + 16)
                if not first(q, k, 4):
                    dve.wait_ge(turned_back, g - 3)
                if not first(q, k, 1):
                    dve.wait_ge(scanned, g)
                nc.vector.tensor_tensor_scan(run[k][:, :], K.same[:, bass.ds(g * W, W)], cols[k][:, :],
                                             0.0 if first(q, k, 1) else run[(k + 3) % 4][:, W - 1:W],
                                             ALU.mult, ALU.add).then_inc(scanned, 1)

            def chunk(c, u):
                for t in range(NTYPES):
                    if not (opening(c) and t < 4):
                        dve.wait_ge(used, c * NTYPES + t - 3)
                    nc.vector.scalar_tensor_tensor(xm[:, t % 4, :], K.ntype[:, bass.ds(c * CH, CH)], float(t),
                                                   x[:, bass.ds(c * CH, CH)], ALU.is_equal, ALU.mult).then_inc(masked, 1)
                    if edges is not None and t < PER:
                        scan(*group(c, t))
            chunks(dve, chunk)
            if edges is not None:
                for g in range(NC * PER, G):
                    scan(g // 4, g % 4)
            if relations is not None:
                dve.wait_ge(w_put, 16 * 3 * HEADS)
                nc.vector.scalar_tensor_tensor(wk[:, :, :], wk[:, :, :], float(HS) ** -0.5,
                                               pri[:, :].unsqueeze(2).broadcast_to([P, RELS, P]), ALU.mult, ALU.mult).then_inc(w_scaled, 1)

        @block.tensor
        def _(pe):
            def turn_back(q, k):
                h = q * 4 + k
                pe.wait_ge(scanned, h + 1)
                if not first(q, k, 2):
                    pe.wait_ge(out_copied, h - 1)
                for j in range(J):
                    last = nc.tensor.transpose(back[k % 2][:, j * P:(j + 1) * P], run[k][:, j * P:(j + 1) * P], K.ident[:, :])
                last.then_inc(turned_back, 1)

            def chunk(c, u):
                if not isinstance(c, int):
                    pe.wait_ge(copied, (c - 1) * M)
                for t in range(NTYPES):
                    if opening(c) and t % 4 == 0:
                        pe.wait_ge(loaded[t // 4], 16 * M)
                    pe.wait_ge(masked, c * NTYPES + t + 1)
                    for m in range(M):
                        last = nc.tensor.matmul(acc[u][m][:, 0:CH], w[:, m, t, :], xm[:, t % 4, :], start=t == 0, stop=t == NTYPES - 1)
                    last.then_inc(used, 1)
                    if edges is not None and t < PER and not (opening(c) and t < 2):
                        turn_back(*group(c, t, -2))
            chunks(pe, chunk)
            if edges is not None:
                for h in range(NC * PER - 2, G):
                    turn_back(h // 4, h % 4)

        @block.scalar
        def _(act):
            def put_out(q, k):
                h = q * 4 + k
                act.wait_ge(turned_back, h + 1)
                if not first(q, k, 4):
                    act.wait_ge(stored[k], q * 16)
                nc.scalar.activation(out[k][:, :, :].rearrange("p j d -> p (j d)"), back[k % 2][:, :], ACT.Copy).then_inc(out_copied, 1)
                act.wait_ge(out_copied, h + 1)
                act.dma_start(sums[bass.ds(h, 1), :, :, :].rearrange("g p j d -> (g p) j d"), out[k][:, :, :]).then_inc(stored[k], 16)

            def chunk(c, u):
                if edges is not None:
                    for t in range(PER):
                        if not (opening(c) and t < 2):
                            put_out(*group(c, t, -2))
                act.wait_ge(used, (c + 1) * NTYPES)
                for m in range(M):
                    nc.scalar.activation(outs[m][:, bass.ds(c * CH, CH)], acc[u][m][:, 0:CH], ACT.Copy).then_inc(copied, 1)
            chunks(act, chunk)
            if edges is not None:
                for h in range(NC * PER - 2, G):
                    put_out(h // 4, h % 4)
                for k in range(4):
                    act.wait_ge(stored[k], 16 * len(range(k, G, 4)))


def sum_edges(nc, K, D, tag, table, radial=False):
    with Stage(nc, tag) as s:
        idx_in = [s.sem(f"idx_in{k}") for k in range(4)]
        msg_in = [s.sem(f"msg_in{k}") for k in range(4)]
        stored = [s.sem(f"stored{k}") for k in range(4)]
        began, turned, scanned, turned_back, copied = (s.sem(x) for x in ("began", "turned", "scanned", "turned_back", "copied"))
        idx = [s.sb(f"idx{k}", [P, J], I32) for k in range(4)]
        rows = [s.sb(f"rows{k}", [P, W]) for k in range(4)]
        run = [s.sb(f"run{u}", [P, W]) for u in range(2)]
        out = [s.sb(f"out{k}", [P, J, P]) for k in range(4)]
        msg = [s.ps(f"msg{u}") for u in range(2)]
        back = [s.ps(f"back{u}") for u in range(2)]
        if radial:
            loaded, zeroed, hid1, lit1, hid2, lit2 = (s.sem(x) for x in ("loaded", "zeroed", "hid1", "lit1", "hid2", "lit2"))
            feat_in = [s.sem(f"feat_in{v}") for v in range(2)]
            hid_out = [s.sem(f"hid_out{v}") for v in range(2)]
            a1 = s.sb("a1", [16, P])
            a2 = s.sb("a2", [P, P])
            bb = s.sb("bb", [P, 2])
            feat = [s.sb(f"feat{v}", [16, W]) for v in range(2)]
            h1 = [s.sb(f"h1{v}", [P, W]) for v in range(2)]
            h2 = [s.sb(f"h2{v}", [P, W]) for v in range(2)]
            ph1, ph2 = s.ps("ph1"), s.ps("ph2")
        sums = D.sums.rearrange("(g j p) d -> g p j d", j=J, p=P)
        block = s.block()

        @block.sync
        def _(sp):
            if radial:
                sp.wait_ge(zeroed, 2)
                for n in range(2):
                    h = slice(n * 64, n * 64 + 64)
                    sp.dma_start(a1[n * 8:n * 8 + 8, h], D.L2_gnn_A1).then_inc(loaded, 16)
                    sp.dma_start(a2[h, h], D.L2_gnn_A2).then_inc(loaded, 16)
                    sp.dma_start(bb[h, 0:1], D.L2_gnn_b1.rearrange("(p o) -> p o", o=1)).then_inc(loaded, 16)
                    sp.dma_start(bb[h, 1:2], D.L2_gnn_b2.rearrange("(p o) -> p o", o=1)).then_inc(loaded, 16)

            def step(q, k):
                g = q * 4 + k
                v, pair = k // 2, q * 2 + k // 2
                if radial and k % 2:
                    here = sp.snap(pair * W) if not isinstance(g, int) else pair * W
                if not first(q, k, 4):
                    sp.wait_ge(msg_in[k], q * 64)
                sp.dma_start(idx[k][:, :], D.src4[bass.ds(g, 1), :, :].rearrange("g p j -> (g p) j")).then_inc(idx_in[k], 16)
                if radial and k % 2:
                    if not first(q, k, 4):
                        sp.wait_ge(hid1, pair - 1)
                    sp.dma_start(feat[v][:, :], D.ea8[:, bass.ds(here, W)]).then_inc(feat_in[v], 16)
            groups(sp, step)

        @block.gpsimd
        def _(pool):
            def step(q, k):
                g = q * 4 + k
                pool.wait_ge(idx_in[k], q * 16 + 16)
                if not first(q, k, 4):
                    pool.wait_ge(turned, g - 3)
                pool.sem_inc(began, 1)
                for j in range(J):
                    nc.gpsimd.indirect_dma_start(rows[k][:, j * P:(j + 1) * P], None, table,
                                                 bass.IndirectOffsetOnAxis(ap=idx[k][:, j:j + 1], axis=0)).then_inc(msg_in[k], 16)
            groups(pool, step)

        @block.tensor
        def _(pe):
            def step(q, k):
                g = q * 4 + k
                u = k % 2
                pe.wait_ge(msg_in[k], q * 64 + 64)
                if not first(q, k, 2):
                    pe.wait_ge(scanned, g - 1)
                for j in range(J):
                    last = nc.tensor.transpose(msg[u][:, j * P:(j + 1) * P], rows[k][:, j * P:(j + 1) * P], K.ident[:, :])
                last.then_inc(turned, 1)
                if not first(q, k, 1):
                    turn_back(g - 1, 1 - u, first(q, k, 3))
                if radial and k % 2:
                    v, pair = k // 2, q * 2 + k // 2
                    pe.wait_ge(feat_in[v], q * 16 + 16)
                    if not first(q, k, 2):
                        pe.wait_ge(lit1, pair)
                    nc.tensor.matmul(ph1[:, :], a1[:, :], feat[v][:, :], start=True, stop=True).then_inc(hid1, 1)
                    if not first(q, k, 2):
                        second_layer(pair - 1, 1 - v, first(q, k, 4))

            def second_layer(pair, v, early):
                pe.wait_ge(lit1, pair + 1)
                if not early:
                    pe.wait_ge(lit2, pair)
                nc.tensor.matmul(ph2[:, :], a2[:, :], h1[v][:, :], start=True, stop=True).then_inc(hid2, 1)

            def turn_back(h, v, early):
                pe.wait_ge(scanned, h + 1)
                if not early:
                    pe.wait_ge(copied, h - 1)
                for j in range(J):
                    last = nc.tensor.transpose(back[v][:, j * P:(j + 1) * P], run[v][:, j * P:(j + 1) * P], K.ident[:, :])
                last.then_inc(turned_back, 1)
            if radial:
                pe.wait_ge(loaded, 128)
            groups(pe, step)
            turn_back(G - 1, 1, False)
            if radial:
                second_layer(G // 2 - 1, (G // 2 - 1) % 2, False)

        @block.vector
        def _(dve):
            if radial:
                nc.vector.memset(a1[:, :], 0.0).then_inc(zeroed, 1)
                nc.vector.memset(a2[:, :], 0.0).then_inc(zeroed, 1)

            def step(q, k):
                g = q * 4 + k
                u = k % 2
                dve.wait_ge(turned, g + 1)
                if not first(q, k, 2):
                    dve.wait_ge(turned_back, g - 1)
                if not first(q, k, 1):
                    dve.wait_ge(scanned, g)
                nc.vector.tensor_tensor_scan(run[u][:, :], K.same[:, bass.ds(g * W, W)], msg[u][:, :],
                                             0.0 if first(q, k, 1) else run[1 - u][:, W - 1:W],
                                             ALU.mult, ALU.add).then_inc(scanned, 1)
            groups(dve, step)

        @block.scalar
        def _(act):
            def step(q, k):
                g = q * 4 + k
                act.wait_ge(turned_back, g + 1)
                if not first(q, k, 4):
                    act.wait_ge(stored[k], q * 16)
                nc.scalar.activation(out[k][:, :, :].rearrange("p j d -> p (j d)"), back[k % 2][:, :], ACT.Copy).then_inc(copied, 1)
                act.wait_ge(copied, g + 1)
                act.dma_start(sums[bass.ds(g, 1), :, :, :].rearrange("g p j d -> (g p) j d"), out[k][:, :, :]).then_inc(stored[k], 16)

            def first_lit(v, pair, early):
                act.wait_ge(hid1, pair + 1)
                if not early:
                    act.wait_ge(hid2, pair - 1)
                nc.scalar.activation(h1[v][:, :], ph1[:, :], ACT.Silu, bias=bb[:, 0:1]).then_inc(lit1, 1)

            def second_lit(v, pair, uses):
                here = pair * W if isinstance(pair, int) else act.snap(pair * W)
                act.wait_ge(hid2, pair + 1)
                if not (isinstance(uses, int) and uses == 0):
                    act.wait_ge(hid_out[v], uses * 16)
                nc.scalar.activation(h2[v][:, :], ph2[:, :], ACT.Silu, bias=bb[:, 1:2]).then_inc(lit2, 1)
                act.wait_ge(lit2, pair + 1)
                act.dma_start(D.hidden[:, bass.ds(here, W)], h2[v][:, :]).then_inc(hid_out[v], 16)

            def step_radial(q, k):
                step(q, k)
                if k % 2:
                    v, pair = k // 2, q * 2 + k // 2
                    first_lit(v, pair, first(q, k, 4))
                    if not first(q, k, 2):
                        second_lit(1 - v, pair - 1, q if v else q - 1)
            if radial:
                act.wait_ge(loaded, 128)
                groups(act, step_radial)
                last = G // 2 - 1
                second_lit(last % 2, last, last // 2)
                for v in range(2):
                    act.wait_ge(hid_out[v], 16 * len(range(v, G // 2, 2)))
            else:
                groups(act, step)
            for k in range(4):
                act.wait_ge(stored[k], 16 * len(range(k, G, 4)))


def relation_table(nc, K, D, tag, wk, wv, key, value, query):
    Q = 4
    with Stage(nc, tag) as s:
        product, evac_k, evac_v = (s.sem(x) for x in ("product", "evac_k", "evac_v"))
        node_in, scattered = s.sem("node_in"), s.sem("scattered")
        stored = [s.sem(f"stored{q}") for q in range(Q)]
        kv = [s.sb(f"kv{u}", [P, 2, P]) for u in range(2)]
        part = [s.sb(f"part{q}", [P, RELS // Q, 2 * P]) for q in range(Q)]
        bank = [s.ps(f"bank{i}") for i in range(8)]
        table = D.table.rearrange("(t p r) d -> t p r d", p=P, r=RELS)
        block = s.block()

        @block.gpsimd
        def _(pool):
            for t in range(NT):
                nc.gpsimd.indirect_dma_start(D.query_rows, bass.IndirectOffsetOnAxis(ap=K.start[:, t:t + 1], axis=0),
                                             query[:, t, :], None, bounds_check=EP - 1,
                                             oob_is_err=False).then_inc(scattered, 16)
            pool.wait_ge(scattered, 16 * NT)

        @block.sync
        def _(sp):
            def tile(t):
                for q in range(Q):
                    sp.wait_ge(evac_k, t * 8 + 2 * q + 2)
                    sp.wait_ge(evac_v, t * 8 + 2 * q + 2)
                    sp.dma_start(table[bass.ds(t, 1), :, q * 8:q * 8 + 8, :].rearrange("t p r d -> (t p) r d"),
                                 part[q][:, :, :]).then_inc(stored[q], 16)
            with sp.Fori(0, NT) as t:
                tile(t)
            for q in range(Q):
                sp.wait_ge(stored[q], 16 * NT)

        def tiles(eng, tile):
            tile(0, 0)
            tile(1, 1)
            with eng.Fori(1, NT // 2) as q:
                tile(2 * q, 0)
                tile(2 * q + 1, 1)
            if NT % 2:
                tile(NT - 1, 0)

        @block.vector
        def _(dve):
            def tile(t, u):
                for c in range(8):
                    dve.wait_ge(product, t * 16 + 2 * c + 1)
                    if not (isinstance(t, int) and t == 0):
                        dve.wait_ge(stored[c // 2], t * 16)
                    nc.vector.tensor_copy(part[c // 2][:, (c % 2) * 4:(c % 2) * 4 + 4, 0:P],
                                          bank[(2 * c) % 8][:, :].rearrange("p (r d) -> p r d", d=P)).then_inc(evac_k, 1)
            tiles(dve, tile)

        @block.scalar
        def _(act):
            def load(t, u):
                if not (isinstance(t, int) and t < 2):
                    act.wait_ge(product, (t - 1) * 16)
                nc.scalar.activation(kv[u][:, 0, :], key[:, bass.ds(t * P, P)], ACT.Copy).then_inc(node_in, 1)
                nc.scalar.activation(kv[u][:, 1, :], value[:, bass.ds(t * P, P)], ACT.Copy).then_inc(node_in, 1)

            def tile(t, u):
                for c in range(8):
                    if c == 1 and not (isinstance(t, int) and t == NT - 1):
                        load(t + 1, 1 - u)
                    act.wait_ge(product, t * 16 + 2 * c + 2)
                    if not (isinstance(t, int) and t == 0):
                        act.wait_ge(stored[c // 2], t * 16)
                    nc.scalar.activation(part[c // 2][:, (c % 2) * 4:(c % 2) * 4 + 4, P:2 * P],
                                         bank[(2 * c + 1) % 8][:, :].rearrange("p (r d) -> p r d", d=P), ACT.Copy).then_inc(evac_v, 1)
            load(0, 0)
            tiles(act, tile)

        @block.tensor
        def _(pe):
            def tile(t, u):
                pe.wait_ge(node_in, t * 2 + 2)
                for c in range(8):
                    for k, (w, evac) in enumerate(((wk, evac_k), (wv, evac_v))):
                        if not (isinstance(t, int) and t == 0 and c < 4):
                            pe.wait_ge(evac, t * 8 + c - 3)
                        nc.tensor.matmul(bank[(2 * c + k) % 8][:, :], kv[u][:, k, :],
                                         w[:, c * 4:c * 4 + 4, :].rearrange("p r d -> p (r d)"), start=True, stop=True).then_inc(product, 1)
            tiles(pe, tile)


def attention(nc, K, D, tag):
    V = P + HEADS
    with Stage(nc, tag) as s:
        idx_in, rows_in, query_in, bias_in, stored = ([s.sem(f"{x}{k}") for k in range(4)] for x in
                                                      ("idx_in", "rows_in", "query_in", "bias_in", "stored"))
        q_turned, k_turned, v_turned, v_copied, spread, multiplied, shifted, largest, difference, relued, weighted = (
            s.sem(x) for x in ("q_turned", "k_turned", "v_turned", "v_copied", "spread", "multiplied", "shifted",
                               "largest", "difference", "relued", "weighted"))
        began = s.sem("began")
        before, messaged, summed, turned_back, copied = (s.sem(x) for x in ("before", "messaged", "summed", "turned_back", "copied"))
        idx = [s.sb(f"idx{k}", [P, J], I32) for k in range(4)]
        rows = [s.sb(f"rows{k}", [P, J, 2 * P]) for k in range(4)]
        query = [s.sb(f"query{k}", [P, J, P]) for k in range(4)]
        bias = [s.sb(f"bias{k}", [P, W], BF16) for k in range(4)]
        qx = [s.sb(f"qx{u}", [P, W]) for u in range(2)]
        prod = [s.sb(f"prod{k}", [P, W + 1]) for k in range(4)]
        b = [s.sb(f"b{u}", [P, W]) for u in range(2)]
        up = s.sb("up", [P, W])
        down = s.sb("down", [P, W])
        decay = [s.sb(f"decay{u}", [P, W]) for u in range(2)]
        weight = [s.sb(f"weight{u}", [P, W]) for u in range(2)]
        value = [s.sb(f"value{k}", [P, W]) for k in range(4)]
        message = s.sb("message", [P, W])
        run = [s.sb(f"run{u}", [P, W]) for u in range(2)]
        den = [s.sb(f"den{u}", [P, W]) for u in range(2)]
        out = [s.sb(f"out{k}", [P, J, V]) for k in range(4)]
        pq, pk, pv, pshift, pback, pden = (s.ps(x) for x in ("pq", "pk", "pv", "pshift", "pback", "pden"))
        pdiff = [s.ps(f"pdiff{u}") for u in range(2)]
        rows_d = D.query_rows.rearrange("(g j p) d -> g p j d", j=J, p=P)
        sums = D.att_sums.rearrange("(g j p) d -> g p j d", j=J, p=P)
        kvrow = D.kvrow.rearrange("(g j p) -> g p j", j=J, p=P)
        block = s.block()

        @block.sync
        def _(sp):
            def marks(q, k, here):
                g = q * 4 + k
                if not first(q, k, 4):
                    sp.wait_ge(largest, g - 3)
                sp.dma_start(bias[k][:, :], D.start_bias[bass.ds(here, W)].partition_broadcast(P)).then_inc(bias_in[k], 16)

            def step(q, k):
                g = q * 4 + k
                here = sp.snap((g - 2) * W) if not isinstance(g, int) else (g - 2) * W
                if not first(q, k, 4):
                    sp.wait_ge(rows_in[k], q * 64)
                with nc.allow_non_contiguous_dma(reason="one index per partition and tile"):
                    sp.dma_start(idx[k][:, :], kvrow[bass.ds(g, 1), :, :].rearrange("g p j -> (g p) j")).then_inc(idx_in[k], 16)
                if not first(q, k, 4):
                    sp.wait_ge(q_turned, g - 3)
                sp.dma_start(query[k][:, :, :], rows_d[bass.ds(g, 1), :, :, :].rearrange("g p j d -> (g p) j d")).then_inc(query_in[k], 16)
                if not first(q, k, 2):
                    marks(*at(q, k, -2), here)
            groups(sp, step)
            for g in (G - 2, G - 1):
                marks(g // 4, g % 4, g * W)

        @block.gpsimd
        def _(pool):
            def step(q, k):
                g = q * 4 + k
                pool.wait_ge(idx_in[k], q * 16 + 16)
                if not first(q, k, 4):
                    pool.wait_ge(k_turned, g - 3)
                pool.sem_inc(began, 1)
                for j in range(J):
                    nc.gpsimd.indirect_dma_start(rows[k][:, j, :], None, D.table,
                                                 bass.IndirectOffsetOnAxis(ap=idx[k][:, j:j + 1], axis=0)).then_inc(rows_in[k], 16)
            groups(pool, step)

        @block.tensor
        def _(pe):
            def turn_in(q, k):
                g = q * 4 + k
                pe.wait_ge(query_in[k], q * 16 + 16)
                if not first(q, k, 1):
                    pe.wait_ge(spread, g)
                for j in range(J):
                    last = nc.tensor.transpose(pq[:, j * P:(j + 1) * P], query[k][:, j, :], K.ident[:, :])
                last.then_inc(q_turned, 1)
                pe.wait_ge(rows_in[k], q * 64 + 64)
                if not first(q, k, 1):
                    pe.wait_ge(v_copied, g)
                for j in range(J):
                    last = nc.tensor.transpose(pv[:, j * P:(j + 1) * P], rows[k][:, j, P:2 * P], K.ident[:, :])
                last.then_inc(v_turned, 1)
                if not first(q, k, 1):
                    pe.wait_ge(multiplied, g)
                for j in range(J):
                    last = nc.tensor.transpose(pk[:, j * P:(j + 1) * P], rows[k][:, j, 0:P], K.ident[:, :])
                last.then_inc(k_turned, 1)

            def subtract(k, h, early):
                if not early:
                    pe.wait_ge(relued, 2 * (h - 1))
                nc.tensor.matmul(pdiff[k % 2][:, :], K.headsum[:, :], prod[k][:, 1:W + 1], start=True, stop=False)
                pe.wait_ge(largest, h + 1)
                nc.tensor.matmul(pdiff[k % 2][:, :], K.negid[:, :], b[k % 2][:, :], start=False, stop=True).then_inc(difference, 1)

            def turn_back(k, h, early):
                u = k % 2
                pe.wait_ge(summed, 2 * (h + 1))
                if not early:
                    pe.wait_ge(copied, 2 * h)
                for j in range(J):
                    nc.tensor.transpose(pback[:, j * P:(j + 1) * P], run[u][:, j * P:(j + 1) * P], K.ident[:, :])
                for j in range(J):
                    last = nc.tensor.transpose(pden[:, j * P:(j + 1) * P], den[u][:, j * P:(j + 1) * P], K.ident[:, :])
                last.then_inc(turned_back, 1)

            def step(q, k, left=G):
                g = q * 4 + k
                pe.wait_ge(multiplied, g + 1)
                if not first(q, k, 1):
                    pe.wait_ge(largest, g)
                nc.tensor.matmul(pshift[:, :], K.headsum[:, :], prod[k][:, 0:W], start=True, stop=True).then_inc(shifted, 1)
                if not first(q, k, 1):
                    subtract(at(q, k, -1)[1], g - 1, first(q, k, 3))
                if left >= 2:
                    turn_in(*at(q, k, 2))
                if not first(q, k, 3):
                    turn_back(at(q, k, -3)[1], g - 3, first(q, k, 4))
            turn_in(0, 0)
            turn_in(0, 1)
            groups(pe, step, tail=step)
            subtract((G - 1) % 4, G - 1, False)
            for h in range(G - 3, G):
                turn_back(h % 4, h, False)

        @block.vector
        def _(dve):
            def multiply(q, k):
                g = q * 4 + k
                u = k % 2
                dve.wait_ge(q_turned, g + 1)
                if not first(q, k, 2):
                    dve.wait_ge(multiplied, g - 1)
                if not first(q, k, 1):
                    dve.wait_ge(spread, g)
                nc.vector.tensor_tensor_scan(qx[u][:, :], K.same[:, bass.ds(g * W, W)], pq[:, :],
                                             0.0 if first(q, k, 1) else qx[1 - u][:, W - 1:W],
                                             ALU.mult, ALU.add).then_inc(spread, 1)
                if not first(q, k, 4):
                    dve.wait_ge(difference, g - 3)
                if first(q, k, 1):
                    nc.vector.memset(prod[k][:, 0:1], 0.0).then_inc(before, 1)
                else:
                    dve.wait_ge(multiplied, g)
                    nc.vector.tensor_copy(prod[k][:, 0:1], prod[(k + 3) % 4][:, W:W + 1]).then_inc(before, 1)
                dve.wait_ge(k_turned, g + 1)
                dve.wait_ge(spread, g + 1)
                dve.wait_ge(before, g + 1)
                nc.vector.tensor_tensor(prod[k][:, 1:W + 1], qx[u][:, :], pk[:, :], ALU.mult).then_inc(multiplied, 1)

            def accumulate(k, h, early1, early2):
                u = k % 2
                dve.wait_ge(weighted, 2 * (h + 1))
                dve.wait_ge(v_copied, h + 1)
                if not early1:
                    dve.wait_ge(summed, 2 * h)
                nc.vector.tensor_tensor(message[:, :], value[k][:, :], weight[u][:, :], ALU.mult).then_inc(messaged, 1)
                if not early2:
                    dve.wait_ge(turned_back, h - 1)
                nc.vector.tensor_tensor_scan(den[u][:, :], decay[u][:, :], weight[u][:, :],
                                             0.0 if early1 else den[1 - u][:, W - 1:W], ALU.mult, ALU.add).then_inc(summed, 1)
                dve.wait_ge(messaged, h + 1)
                nc.vector.tensor_tensor_scan(run[u][:, :], decay[u][:, :], message[:, :],
                                             0.0 if early1 else run[1 - u][:, W - 1:W], ALU.mult, ALU.add).then_inc(summed, 1)

            def step(q, k, left=G):
                g = q * 4 + k
                u = k % 2
                if left:
                    multiply(*at(q, k, 1))
                if not first(q, k, 2):
                    accumulate(at(q, k, -2)[1], g - 2, first(q, k, 3), first(q, k, 4))
                dve.wait_ge(shifted, g + 1)
                if not first(q, k, 2):
                    dve.wait_ge(difference, g - 1)
                if not first(q, k, 1):
                    dve.wait_ge(largest, g)
                dve.wait_ge(bias_in[k], q * 16 + 16)
                nc.vector.tensor_tensor_scan(b[u][:, :], pshift[:, :], bias[k][:, :],
                                             0.0 if first(q, k, 1) else b[1 - u][:, W - 1:W],
                                             ALU.max, ALU.add).then_inc(largest, 1)
            multiply(0, 0)
            groups(dve, step, tail=step)
            accumulate((G - 2) % 4, G - 2, False, False)
            accumulate((G - 1) % 4, G - 1, False, False)

        @block.scalar
        def _(act):
            def copy_value(q, k):
                g = q * 4 + k
                act.wait_ge(v_turned, g + 1)
                if not first(q, k, 4):
                    act.wait_ge(messaged, g - 3)
                nc.scalar.activation(value[k][:, :], pv[:, :], ACT.Copy).then_inc(v_copied, 1)

            def weigh(k, h, early, second):
                u = k % 2
                act.wait_ge(difference, h + 1)
                if not early:
                    act.wait_ge(weighted, 2 * h)
                nc.scalar.activation(up[:, :], pdiff[u][:, :], ACT.Relu).then_inc(relued, 1)
                nc.scalar.activation(down[:, :], pdiff[u][:, :], ACT.Relu, scale=-1.0).then_inc(relued, 1)
                if not second:
                    act.wait_ge(summed, 2 * (h - 1))
                act.wait_ge(relued, 2 * h + 1)
                nc.scalar.activation(decay[u][:, :], up[:, :], ACT.Exp, scale=-1.0).then_inc(weighted, 1)
                act.wait_ge(relued, 2 * h + 2)
                nc.scalar.activation(weight[u][:, :], down[:, :], ACT.Exp, scale=-1.0).then_inc(weighted, 1)

            def put_out(q, k, h):
                act.wait_ge(turned_back, h + 1)
                if not (isinstance(q, int) and q == 0):
                    act.wait_ge(stored[k], q * 16)
                nc.scalar.activation(out[k][:, :, 0:P], pback[:, :].rearrange("p (j d) -> p j d", j=J), ACT.Copy).then_inc(copied, 1)
                nc.scalar.activation(out[k][:, :, P:V], pden[:, 0:J * P:HS].rearrange("p (j d) -> p j d", j=J), ACT.Copy).then_inc(copied, 1)
                act.wait_ge(copied, 2 * (h + 1))
                act.dma_start(sums[bass.ds(h, 1), :, :, :].rearrange("g p j d -> (g p) j d"), out[k][:, :, :]).then_inc(stored[k], 16)

            def step(q, k, left=G):
                g = q * 4 + k
                if not first(q, k, 1):
                    weigh(at(q, k, -1)[1], g - 1, first(q, k, 2), first(q, k, 3))
                if left >= 2:
                    copy_value(*at(q, k, 2))
                if not first(q, k, 3):
                    put_out(*at(q, k, -3), g - 3)
            copy_value(0, 0)
            copy_value(0, 1)
            groups(act, step, tail=step)
            weigh((G - 1) % 4, G - 1, False, False)
            for h in range(G - 3, G):
                put_out(h // 4, h % 4, h)
            for k in range(4):
                act.wait_ge(stored[k], 16 * len(range(k, G, 4)))


def mix_with_input(nc, K, D, tag, layer, new, old, out):
    with Stage(nc, tag) as s:
        loaded, gated, hot, spread_, lit, done, mixed = (
            s.sem(x) for x in ("loaded", "gated", "hot", "spread", "lit", "done", "mixed"))
        skip = s.sb("skip", [NTYPES, 1])
        gate = s.sb("gate", [NTYPES, 1])
        gates = s.sb("gates", [NTYPES, P])
        onehot = s.sb("onehot", [NTYPES, NP])
        lifted = s.sb("lifted", [P, 2, CH])
        diff = s.sb("diff", [P, 2, CH])
        alpha = [s.ps(f"alpha{i}") for i in range(2)]
        block = s.block()

        @block.sync
        def _(sp):
            sp.dma_start(skip[:, :], D.L0_gnn_skip[layer, :].rearrange("(p o) -> p o", o=1)).then_inc(loaded, 16)

        @block.tensor
        def _(pe):
            pe.wait_ge(hot, 2)
            for c in range(NC):
                if c >= 2:
                    pe.wait_ge(mixed, 2 * (c - 1))
                nc.tensor.matmul(alpha[c % 2][:, 0:CH], gates[:, :], onehot[:, c * CH:(c + 1) * CH], start=True, stop=True).then_inc(spread_, 1)

        @block.scalar
        def _(act):
            act.wait_ge(loaded, 16)
            nc.scalar.activation(gate[:, :], skip[:, :], ACT.Sigmoid).then_inc(gated, 1)
            for c in range(NC):
                if c >= 2:
                    act.wait_ge(mixed, 2 * (c - 1))
                nc.scalar.activation(lifted[:, c % 2, :], new[:, c * CH:(c + 1) * CH], ACT.Silu).then_inc(lit, 1)

        @block.vector
        def _(dve):
            dve.wait_ge(gated, 1)
            nc.vector.tensor_copy(gates[:, :], gate[:, :].broadcast_to([NTYPES, P])).then_inc(hot, 1)
            nc.vector.tensor_scalar(onehot[:, :], K.ntype[0:NTYPES, :], K.pid[0:NTYPES, 0:1], None, ALU.is_equal).then_inc(hot, 1)
            for c in range(NC):
                part = slice(c * CH, (c + 1) * CH)
                dve.wait_ge(lit, c + 1)
                if c >= 2:
                    dve.wait_ge(done, c - 1)
                nc.vector.tensor_tensor(diff[:, c % 2, :], lifted[:, c % 2, :], old[:, part], ALU.subtract).then_inc(mixed, 1)
                dve.wait_ge(spread_, c + 1)
                dve.wait_ge(mixed, 2 * c + 1)
                nc.vector.tensor_tensor(diff[:, c % 2, :], diff[:, c % 2, :], alpha[c % 2][:, 0:CH], ALU.mult).then_inc(mixed, 1)
                dve.wait_ge(mixed, 2 * c + 2)
                nc.vector.tensor_tensor(out[:, part], diff[:, c % 2, :], old[:, part], ALU.add).then_inc(done, 1)


def degree_scale(nc, K, D):
    with Stage(nc, "deg") as s:
        moved, made, rooted = s.sem("moved"), s.sem("made"), s.sem("rooted")
        root = s.sb("root", [P, NT])
        inv = s.sb("inv", [P, NT])
        block = s.block()

        @block.scalar
        def _(act):
            nc.scalar.activation(root[:, :], K.degree[:, :], ACT.Sqrt, bias=K.ones[:, 0:1]).then_inc(rooted, 1)

        @block.vector
        def _(dve):
            dve.wait_ge(rooted, 1)
            nc.vector.reciprocal(inv[:, :], root[:, :]).then_inc(made, 1)

        @block.sync
        def _(sp):
            sp.wait_ge(made, 1)
            with nc.allow_non_contiguous_dma(reason="one number of each node"):
                sp.dma_start(D.scale.rearrange("(t p) -> p t", p=P), inv[:, :]).then_inc(moved, 16)
            sp.wait_ge(moved, 16)
            sp.dma_start(K.isd[:, :], D.scale.partition_broadcast(P)).then_inc(moved, 16)
            sp.wait_ge(moved, 32)


def batch_norm(nc, K, D, tag, sums, own, bias, gain, shift, out, relu):
    with Stage(nc, tag) as s:
        loaded, made, squared, rooted = (s.sem(x) for x in ("loaded", "made", "squared", "rooted"))
        cols = s.sb("cols", [P, 3])
        y = s.sb("y", [P, NP])
        sq = s.sb("sq", [P, N])
        st = s.sb("st", [P, 6])
        block = s.block()

        @block.sync
        def _(sp):
            for i, v in enumerate((bias, gain, shift)):
                sp.dma_start(cols[:, i:i + 1], v.rearrange("(p o) -> p o", o=1)).then_inc(loaded, 16)

        @block.vector
        def _(dve):
            link = linked(dve, made)
            link(nc.vector.tensor_tensor(y[:, :], sums[:, :], own[:, :], ALU.add))
            link(nc.vector.tensor_tensor(y[:, :], y[:, :], K.isd[:, :], ALU.mult))
            dve.wait_ge(loaded, 48)
            link(nc.vector.tensor_scalar(y[:, :], y[:, :], cols[:, 0:1], None, ALU.add))
            link(nc.vector.tensor_reduce(st[:, 0:1], y[:, 0:N], AX.X, ALU.add))
            link(nc.vector.tensor_scalar(st[:, 0:1], st[:, 0:1], 1.0 / N, None, ALU.mult))
            link(nc.vector.tensor_scalar(y[:, :], y[:, :], st[:, 0:1], None, ALU.subtract))
            link(nc.vector.tensor_tensor(sq[:, :], y[:, 0:N], y[:, 0:N], ALU.mult))
            link(nc.vector.tensor_reduce(st[:, 1:2], sq[:, :], AX.X, ALU.add))
            dve.wait_ge(rooted, 1)
            link(nc.vector.reciprocal(st[:, 3:4], st[:, 2:3]))
            link(nc.vector.tensor_tensor(st[:, 4:5], st[:, 3:4], cols[:, 1:2], ALU.mult))
            link(nc.vector.tensor_scalar(y[:, :], y[:, :], st[:, 4:5], cols[:, 2:3], ALU.mult, ALU.add))
            nc.vector.tensor_scalar(out[:, :], y[:, :], 0.0 if relu else -3.0e38, None, ALU.max).then_inc(squared, 1)

        @block.scalar
        def _(act):
            act.wait_ge(made, 8)
            nc.scalar.activation(st[:, 2:3], st[:, 1:2], ACT.Sqrt, scale=1.0 / N, bias=K.eps[:, 0:1]).then_inc(rooted, 1)


def message_weights(nc, K, D, up, down):
    c = 1.0 / (10.0 * (2 * 32) ** 0.5)
    with Stage(nc, "mwt") as s:
        zeroed, loaded, made = s.sem("zeroed"), s.sem("loaded"), s.sem("made")
        tmp = [s.sb(f"tmp{i}", [P, 32]) for i in range(2)]
        block = s.block()

        @block.gpsimd
        def _(pool):
            for m in (up, *down, *tmp):
                nc.gpsimd.memset(m[:, :], 0.0).then_inc(zeroed, 1)

        @block.sync
        def _(sp):
            sp.wait_ge(zeroed, 5)
            sp.dma_start(up[0:32, 0:32], D.L2_gnn_W_up_s).then_inc(loaded, 16)
            sp.dma_start(tmp[0][0:32, :], D.L2_gnn_W_out_s[0:32, :]).then_inc(loaded, 16)
            sp.dma_start(tmp[1][0:32, :], D.L2_gnn_W_out_v[0:32, :]).then_inc(loaded, 16)
            for i in range(3):
                blk = slice(32 + 32 * i, 64 + 32 * i)
                sp.dma_start(up[32 + i:P:3, blk], D.L2_gnn_W_up_v).then_inc(loaded, 16)
                sp.dma_start(tmp[0][blk, :], D.L2_gnn_W_out_v[32:64, :]).then_inc(loaded, 16)
                sp.dma_start(tmp[1][blk, :], D.L2_gnn_W_out_s[32:64, :]).then_inc(loaded, 16)

        @block.vector
        def _(dve):
            dve.wait_ge(loaded, 16 * 12)
            link = linked(dve, made)
            link(nc.vector.tensor_scalar(up[:, :], up[:, :], 32 ** -0.5, None, ALU.mult))
            link(nc.vector.tensor_scalar(down[0][0:32, 0:32], tmp[0][0:32, :], c, None, ALU.mult))
            for i in range(3):
                blk = slice(32 + 32 * i, 64 + 32 * i)
                link(nc.vector.tensor_scalar(down[0][blk, 32 + i:P:3], tmp[0][blk, :], c, None, ALU.mult))
                link(nc.vector.tensor_scalar(down[1][0:32, 32 + i:P:3], tmp[1][0:32, :], c, None, ALU.mult))
                link(nc.vector.tensor_scalar(down[1][blk, 0:32], tmp[1][blk, :], c * 3 ** -0.5, None, ALU.mult))


def messages(nc, K, D, tag, down):
    with Stage(nc, tag) as s:
        idx_in, rows_in, edge_in, hidden_in, out_y_in, stored = ([s.sem(f"{x}{k}") for k in range(4)] for x in
                                                                 ("idx_in", "rows_in", "edge_in", "hidden_in", "out_y_in", "stored"))
        began, loaded, ones_set, scaled, turned, upcopied, radial, multiplied, mapped, graded, added, scanned, turned_back, copied = (
            s.sem(x) for x in ("began", "loaded", "ones_set", "scaled", "turned", "upcopied", "radial", "multiplied", "mapped",
                               "graded", "added", "scanned", "turned_back", "copied"))
        a3 = [s.sb(f"a3{k}", [64, P]) for k in range(2)]
        idx = [s.sb(f"idx{k}", [P, J], I32) for k in range(4)]
        rows = [s.sb(f"rows{k}", [P, J, P]) for k in range(4)]
        edge = [s.sb(f"edge{k}", [P, J, 5]) for k in range(4)]
        hidden = [s.sb(f"hidden{k}", [64, W]) for k in range(4)]
        out_y = [s.sb(f"out_y{k}", [P, W]) for k in range(4)]
        sc = [[s.sb(f"sc{u}{k}", [P, J, P]) for k in range(2)] for u in range(2)]
        un = [[s.sb(f"un{u}{k}", [P, W]) for k in range(2)] for u in range(2)]
        prod = [s.sb(f"prod{k}", [P, W]) for k in range(2)]
        vec = s.sb("vec", [P, W])
        total = s.sb("total", [P, W])
        run = [s.sb(f"run{u}", [P, W]) for u in range(2)]
        out = [s.sb(f"out{k}", [P, J, P]) for k in range(4)]
        pu = [s.ps(f"pu{k}") for k in range(2)]
        pr = [s.ps(f"pr{k}") for k in range(2)]
        pm = [s.ps(f"pm{k}") for k in range(2)]
        pback = s.ps("pback")
        sums = D.sums.rearrange("(g j p) d -> g p j d", j=J, p=P)
        block = s.block()

        @block.sync
        def _(sp):
            for k, which in enumerate(((0, 2, 2, 2), (1, 3, 3, 3))):
                for n, w in enumerate(which):
                    sp.dma_start(a3[k][:, n * 32:(n + 1) * 32], D.L2_gnn_A3[:, w * 32:(w + 1) * 32]).then_inc(loaded, 16)

            def later(q, k, here, pair):
                g = q * 4 + k
                if not first(q, k, 4):
                    sp.wait_ge(graded, g - 3)
                elif first(q, k, 1):
                    sp.wait_ge(ones_set, 4)
                sp.dma_start(hidden[k][:, :], D.hidden[(k % 2) * 64:(k % 2) * 64 + 64, bass.ds(pair, W)]).then_inc(hidden_in[k], 16)
                for i in range(3):
                    sp.dma_start(out_y[k][32 + i:P:3, :], D.ea4[1 + i, bass.ds(here, W)].partition_broadcast(32)).then_inc(out_y_in[k], 16)

            def step(q, k):
                g = q * 4 + k
                here = sp.snap((g - 2) * W) if not isinstance(g, int) else (g - 2) * W
                pair = sp.snap((q * 2 + k // 2 - 1) * W) if not isinstance(g, int) else (g // 2 - 1) * W
                if not first(q, k, 4):
                    sp.wait_ge(rows_in[k], q * 64)
                sp.dma_start(idx[k][:, :], D.src4[bass.ds(g, 1), :, :].rearrange("g p j -> (g p) j")).then_inc(idx_in[k], 16)
                if not first(q, k, 4):
                    sp.wait_ge(scaled, 2 * (g - 3))
                sp.dma_start(edge[k][:, :, :], D.ea5[bass.ds(g, 1), :, :].rearrange("g p (j c) -> (g p) j c", c=5)).then_inc(edge_in[k], 16)
                if not first(q, k, 2):
                    later(*at(q, k, -2), here, pair)
            groups(sp, step)
            for g in (G - 2, G - 1):
                later(g // 4, g % 4, g * W, g // 2 * W)

        @block.gpsimd
        def _(pool):
            for k in range(4):
                nc.gpsimd.memset(out_y[k][0:32, :], 1.0).then_inc(ones_set, 1)

            def step(q, k):
                g = q * 4 + k
                pool.wait_ge(idx_in[k], q * 16 + 16)
                if not first(q, k, 4):
                    pool.wait_ge(scaled, 2 * (g - 3))
                pool.sem_inc(began, 1)
                for j in range(J):
                    nc.gpsimd.indirect_dma_start(rows[k][:, j, :], None, D.rows,
                                                 bass.IndirectOffsetOnAxis(ap=idx[k][:, j:j + 1], axis=0)).then_inc(rows_in[k], 16)
            groups(pool, step)

        @block.tensor
        def _(pe):
            def turn(q, k):
                g = q * 4 + k
                u = k % 2
                for n in range(2):
                    pe.wait_ge(scaled, 2 * g + n + 1)
                    if not first(q, k, 1):
                        pe.wait_ge(upcopied, 2 * g + n - 1)
                    for j in range(J):
                        last = nc.tensor.transpose(pu[n][:, j * P:(j + 1) * P], sc[u][n][:, j, :], K.ident[:, :])
                    last.then_inc(turned, 1)

            def weigh(q, k):
                g = q * 4 + k
                pe.wait_ge(hidden_in[k], q * 16 + 16)
                for n in range(2):
                    if not first(q, k, 1):
                        pe.wait_ge(multiplied, 2 * g + n - 1)
                    nc.tensor.matmul(pr[n][:, :], a3[n][:, :], hidden[k][:, :], start=True, stop=True).then_inc(radial, 1)

            def turn_back(u, g, early):
                pe.wait_ge(scanned, g + 1)
                if not early:
                    pe.wait_ge(copied, g)
                for j in range(J):
                    last = nc.tensor.transpose(pback[:, j * P:(j + 1) * P], run[u][:, j * P:(j + 1) * P], K.ident[:, :])
                last.then_inc(turned_back, 1)

            def step(q, k, left=G):
                g = q * 4 + k
                for n, free in enumerate((added, graded)):
                    pe.wait_ge(multiplied, 2 * g + n + 1)
                    if not first(q, k, 1):
                        pe.wait_ge(free, g)
                    nc.tensor.matmul(pm[n][:, :], down[n][:, :], prod[n][:, :], start=True, stop=True).then_inc(mapped, 1)
                if left:
                    weigh(*at(q, k, 1))
                if left >= 2:
                    turn(*at(q, k, 2))
                if not first(q, k, 1):
                    turn_back(1 - k % 2, g - 1, first(q, k, 2))
            pe.wait_ge(loaded, 16 * 8)
            turn(0, 0)
            turn(0, 1)
            weigh(0, 0)
            groups(pe, step, tail=step)
            turn_back((G - 1) % 2, G - 1, False)

        @block.scalar
        def _(act):
            def copy_up(q, k):
                g = q * 4 + k
                for n in range(2):
                    act.wait_ge(turned, 2 * g + n + 1)
                    if not first(q, k, 2):
                        act.wait_ge(multiplied, 2 * (g - 1) + n - 1)
                    nc.scalar.activation(un[k % 2][n][:, :], pu[n][:, :], ACT.Copy).then_inc(upcopied, 1)

            def copy_out(k, h, uses):
                act.wait_ge(turned_back, h + 1)
                if not (isinstance(uses, int) and uses == 0):
                    act.wait_ge(stored[k], uses * 16)
                nc.scalar.activation(out[k][:, :, :].rearrange("p j d -> p (j d)"), pback[:, :], ACT.Copy).then_inc(copied, 1)
                act.wait_ge(copied, h + 1)
                act.dma_start(sums[bass.ds(h, 1), :, :, :].rearrange("g p j d -> (g p) j d"), out[k][:, :, :]).then_inc(stored[k], 16)

            def step(q, k, left=G):
                if left >= 2:
                    copy_up(*at(q, k, 2))
                if not first(q, k, 1):
                    copy_out(at(q, k, -1)[1], q * 4 + k - 1, at(q, k, -1)[0])
            copy_up(0, 0)
            copy_up(0, 1)
            groups(act, step, tail=step)
            copy_out((G - 1) % 4, G - 1, (G - 1) // 4)
            for k in range(4):
                act.wait_ge(stored[k], 16 * len(range(k, G, 4)))

        @block.vector
        def _(dve):
            def scale(q, k):
                g = q * 4 + k
                u = k % 2
                dve.wait_ge(rows_in[k], q * 64 + 64)
                dve.wait_ge(edge_in[k], q * 16 + 16)
                if not first(q, k, 2):
                    dve.wait_ge(turned, 2 * (g - 1))
                nc.vector.tensor_tensor(sc[u][0][:, :, :], rows[k][:, :, :],
                                        edge[k][:, :, 0:1].broadcast_to([P, J, P]), ALU.mult).then_inc(scaled, 1)
                nc.vector.tensor_tensor(sc[u][1][:, :, :].rearrange("p j (b c) -> p j b c", c=32),
                                        rows[k][:, :, :].rearrange("p j (b c) -> p j b c", c=32),
                                        edge[k][:, :, 1:5].unsqueeze(3).broadcast_to([P, J, 4, 32]), ALU.mult).then_inc(scaled, 1)

            def weight(q, k, n):
                g = q * 4 + k
                dve.wait_ge(upcopied, 2 * g + n + 1)
                dve.wait_ge(radial, 2 * g + n + 1)
                if not first(q, k, 1):
                    dve.wait_ge(mapped, 2 * g + n - 1)
                nc.vector.tensor_tensor(prod[n][:, :], pr[n][:, :], un[k % 2][n][:, :], ALU.mult).then_inc(multiplied, 1)

            def step(q, k, left=G):
                g = q * 4 + k
                u = k % 2
                dve.wait_ge(out_y_in[k], q * 48 + 48)
                dve.wait_ge(mapped, 2 * g + 2)
                if not first(q, k, 1):
                    dve.wait_ge(added, g)
                nc.vector.tensor_tensor(vec[:, :], pm[1][:, :], out_y[k][:, :], ALU.mult).then_inc(graded, 1)
                if left:
                    weight(*at(q, k, 1), 0)
                dve.wait_ge(graded, g + 1)
                if not first(q, k, 1):
                    dve.wait_ge(scanned, g)
                nc.vector.tensor_tensor(total[:, :], pm[0][:, :], vec[:, :], ALU.add).then_inc(added, 1)
                if left:
                    weight(*at(q, k, 1), 1)
                dve.wait_ge(added, g + 1)
                if not first(q, k, 2):
                    dve.wait_ge(turned_back, g - 1)
                nc.vector.tensor_tensor_scan(run[u][:, :], K.same[:, bass.ds(g * W, W)], total[:, :],
                                             0.0 if first(q, k, 1) else run[1 - u][:, W - 1:W], ALU.mult, ALU.add).then_inc(scanned, 1)
                if left >= 3:
                    scale(*at(q, k, 3))
            scale(0, 0)
            scale(0, 1)
            scale(0, 2)
            weight(0, 0, 0)
            weight(0, 0, 1)
            groups(dve, step, tail=step)


class Names:
    pass


def build(nc, D, out):
    def dram(name, shape, dt=F32):
        return nc.dram_tensor(name, shape, dt).ap()

    D.coarse = dram("coarse", (TILES,), I32)
    D.same = dram("same", (EP,), U8)
    D.start_bias = dram("start_bias", (EP,), BF16)
    D.kvrow = dram("kvrow", (EP,), I32)
    D.degree = dram("degree", (NP,))
    D.scale = dram("scale", (NP,))
    D.query_rows = dram("query_rows", (EP, P))
    D.table = dram("table", (NP * RELS, 2 * P))
    D.att_sums = dram("att_sums", (EP, P + HEADS))
    D.sums = dram("sums", (EP, P))
    D.rows = dram("rows", (NP, P))
    D.hidden = dram("hidden", (P, EP // 2))

    K = Names()
    with ExitStack() as stack:
        def sb(name, shape, dt=F32, st=stack):
            return st.enter_context(nc.sbuf_tensor(name, shape, dt))
        K.ident, K.negid, K.mean, K.headsum = (sb(x, [P, P]) for x in ("ident", "negid", "meanm", "headsum"))
        K.eps, K.ones, K.pid = sb("eps", [P, 1]), sb("ones", [P, 1]), sb("pid", [P, 1])
        K.end, K.start = sb("end", [P, NT], I32), sb("start", [P, NT], I32)
        K.degree, K.has = sb("degree_sb", [P, NT]), sb("has", [P, NT])
        constants(nc, K)
        K.same = sb("same_sb", [P, EP], U8)
        a, b, c = (sb(x, [P, NP]) for x in ("a", "b", "c"))

        with ExitStack() as inner:
            h = sb("h", [P, NP], st=inner)
            K.ntype = sb("ntype", [P, NP], st=inner)
            graph_index(nc, K, D, h)
            for l in range(LAYERS):
                with ExitStack() as table:
                    wk, wv = (sb(f"{x}{l}", [P, RELS, P], st=table) for x in ("wk", "wv"))
                    typed_linear(nc, K, f"qkv{l}", h, [D.L0_gnn_Wq[l], D.L0_gnn_Wk[l], D.L0_gnn_Wv[l]], [a, b, c],
                                 clear=D.query_rows if l == 0 else None,
                                 edges=(D.ea128, D.sums) if l == 1 else None, relations=(D, l, wk, wv))
                    query = sb(f"query{l}", [P, NT, P], st=table)
                    to_rows(nc, K, f"qr{l}", a, rows=query)
                    relation_table(nc, K, D, f"tab{l}", wk, wv, b, c, query)
                attention(nc, K, D, f"att{l}")
                ends(nc, K, D, f"agg{l}", a, per_head=True)
                typed_linear(nc, K, f"wa{l}", a, [D.L0_gnn_Wa[l]], [b])
                mix_with_input(nc, K, D, f"mix{l}", l, b, h, c)
                layernorm(nc, K, f"ln{l}", c, h, D.L0_gnn_ln_g[l], D.L0_gnn_ln_b[l])
            linear(nc, K, "ff", a, [(D.L0_gnn_ff_w, h)], D.L0_gnn_ff_b)
        K.x = sb("x", [P, NP])
        load_input(nc, K, D)
        layernorm(nc, K, "norm0", K.x, K.x, add=a)

        ends(nc, K, D, "eae", a)
        linear(nc, K, "emb", b, [(D.L1_gnn_We, a)], row_term=(D.L1_gnn_be, D.degree))
        linear(nc, K, "w1", a, [(D.L1_gnn_W1[0:P, :], K.x), (D.L1_gnn_W1[P:2 * P, :], b)])
        to_rows(nc, K, "yr", a, dram=D.rows)
        sum_edges(nc, K, D, "nb", table=D.rows, radial=True)
        ends(nc, K, D, "nbe", b)
        relu_sum(nc, K, "act1", c, a, b, D.L1_gnn_b1)
        linear(nc, K, "w2", a, [(D.L1_gnn_W2, c)], D.L1_gnn_b2)
        layernorm(nc, K, "norm1", K.x, K.x, add=a)

        with ExitStack() as inner:
            up = sb("up", [P, P], st=inner)
            down = [sb(f"down{k}", [P, P], st=inner) for k in range(2)]
            message_weights(nc, K, D, up, down)
            linear(nc, K, "upl", a, [(up, K.x)])
            to_rows(nc, K, "ur", a, dram=D.rows)
            messages(nc, K, D, "msg", down)
        ends(nc, K, D, "mse", a)
        layernorm(nc, K, "norm2", K.x, K.x, add=a)

        K.isd = sb("isd", [P, NP])
        degree_scale(nc, K, D)
        source = K.x
        for l in range(2):
            w, bias, gain, shift = D.l3[l]
            linear(nc, K, f"gcn{l}", b, [(w, source)], times=K.isd)
            to_rows(nc, K, f"gr{l}", b, dram=D.rows)
            sum_edges(nc, K, D, f"gsum{l}", table=D.rows)
            ends(nc, K, D, f"ge{l}", a)
            batch_norm(nc, K, D, f"bn{l}", a, b, bias, gain, shift, c, relu=l == 0)
            source = c
        layernorm(nc, K, "norm3", K.x, K.x, add=c)
        store_nodes(nc, K, out)


def load_input(nc, K, D):
    with Stage(nc, "ldx") as s:
        loaded = s.sem("loaded")
        block = s.block()

        @block.sync
        def _(sp):
            sp.dma_start(K.x[:, :], D.x).then_inc(loaded, 16)
            sp.wait_ge(loaded, 16)


def relu_sum(nc, K, tag, out, a, b, bias):
    with Stage(nc, tag) as s:
        loaded, added, done = s.sem("loaded"), s.sem("added"), s.sem("done")
        col = s.sb("col", [P, 1])
        total = s.sb("total", [P, NP])
        block = s.block()

        @block.sync
        def _(sp):
            sp.dma_start(col[:, :], bias.rearrange("(p o) -> p o", o=1)).then_inc(loaded, 16)

        @block.vector
        def _(dve):
            for c in range(NC):
                part = slice(c * CH, (c + 1) * CH)
                nc.vector.tensor_tensor(total[:, part], a[:, part], b[:, part], ALU.add).then_inc(added, 1)

        @block.scalar
        def _(act):
            act.wait_ge(loaded, 16)
            for c in range(NC):
                part = slice(c * CH, (c + 1) * CH)
                act.wait_ge(added, c + 1)
                nc.scalar.activation(out[:, part], total[:, part], ACT.Relu, bias=col[:, 0:1]).then_inc(done, 1)


def store_nodes(nc, K, out):
    with Stage(nc, "sto") as s:
        rows = s.sb("rows", [P, NT, P])
        to_rows(nc, K, "outr", K.x, rows=rows)
        stored = s.sem("stored")
        block = s.block()
        full = N // P

        @block.sync
        def _(sp):
            sp.dma_start(out[0:full * P, :].rearrange("(t p) d -> p t d", p=P), rows[:, 0:full, :]).then_inc(stored, 16)
            sp.dma_start(out[full * P:N, :], rows[0:N - full * P, full, :]).then_inc(stored, 16)
            sp.wait_ge(stored, 32)


_WEIGHTS = ['L0_gnn_Wk', 'L0_gnn_Wq', 'L0_gnn_Wv', 'L0_gnn_Wa', 'L0_gnn_Watt', 'L0_gnn_Wmsg', 'L0_gnn_pri', 'L0_gnn_skip',
            'L0_gnn_ln_g', 'L0_gnn_ln_b', 'L0_gnn_ff_w', 'L0_gnn_ff_b', 'L1_gnn_We', 'L1_gnn_be', 'L1_gnn_W1', 'L1_gnn_b1',
            'L1_gnn_W2', 'L1_gnn_b2', 'L2_gnn_W_up_s', 'L2_gnn_W_up_v', 'L2_gnn_A1', 'L2_gnn_b1', 'L2_gnn_A2', 'L2_gnn_b2',
            'L2_gnn_A3', 'L2_gnn_W_out_s', 'L2_gnn_W_out_v', 'L3_gnn_W1', 'L3_gnn_b1', 'L3_gnn_g1', 'L3_gnn_bt1',
            'L3_gnn_W2', 'L3_gnn_b2', 'L3_gnn_g2', 'L3_gnn_bt2']


def kernel(**inputs):
    import numpy as np
    import concourse.bacc as bacc
    from concourse.bass_utils import run_bass_kernel_spmd

    def padded(a, n, fill=0):
        wide = np.full(a.shape[:-1] + (n,), fill, a.dtype)
        wide[..., :a.shape[-1]] = a
        return wide

    given = {k: np.asarray(v) for k, v in inputs.items()}
    src, dst = padded(given["src"], EP), padded(given["dst"], EP, N)
    by_edge = np.ones((EP, 5), np.float32)
    by_edge[:E, [0, 2, 3, 4]] = given["edge_attr_4"]
    arrays = {
        "x": padded(given["x"].T, NP), "ntype": padded(given["node_type_16"], NP),
        "dst": dst, "dst_before": np.concatenate([np.full(1, -1, dst.dtype), dst[:-1]]),
        "src_flat": src, "src4": np.ascontiguousarray(src.reshape(G, J, P).transpose(0, 2, 1)),
        "etype_flat": padded(given["edge_type_32"], EP),
        "ea128": padded(given["edge_attr_128"].T, EP), "ea4": padded(given["edge_attr_4"].T, EP),
        "ea8": np.ascontiguousarray(padded(given["edge_attr_8"].T, EP).reshape(8, G // 2, 2, W)
                                    .transpose(2, 0, 1, 3)).reshape(16, EP // 2),
        "ea5": np.ascontiguousarray(by_edge.reshape(G, J, P, 5).transpose(0, 2, 1, 3)).reshape(G, P, J * 5),
    }
    arrays.update({k: given[k] for k in _WEIGHTS})
    nc = bacc.Bacc("TRN2", target_bir_lowering=False, num_devices=1)
    D = Names()
    for name, a in arrays.items():
        ap = nc.dram_tensor(f"in_{name}", a.shape, mybir.dt.from_np(a.dtype), kind="ExternalInput").ap()
        D.__dict__[name] = ap
    D.l3 = [(D.L3_gnn_W1, D.L3_gnn_b1, D.L3_gnn_g1, D.L3_gnn_bt1), (D.L3_gnn_W2, D.L3_gnn_b2, D.L3_gnn_g2, D.L3_gnn_bt2)]
    out = nc.dram_tensor("out", (N, P), F32, kind="ExternalOutput").ap()
    build(nc, D, out)
    r = run_bass_kernel_spmd(nc, [{f"in_{k}": v for k, v in arrays.items()}], core_ids=[0])
    return r.results[0]["out"]
```
